# Optimizing a Trainium2 kernel written in Bass

```python
import numpy as np
import jax
import jax.numpy as jnp

def _softmax(x, axis=-1):
    return jax.nn.softmax(x, axis=axis)

def _gelu(x):
    return jax.nn.gelu(x, approximate=True)

def _silu(x):
    return jax.nn.silu(x)

def _sigmoid(x):
    return jax.nn.sigmoid(x)

def _layernorm(x, axis=-1, eps=1e-05):
    m = jnp.mean(x, axis=axis, keepdims=True)
    v = jnp.var(x, axis=axis, keepdims=True)
    return (x - m) / jnp.sqrt(v + eps)

def _scatter_add(tgt, idx, src, axis=0):
    return tgt.at[idx].add(src)

def _segment_sum(src, seg, n):
    return jax.ops.segment_sum(src, seg, n)
kernel_name = 'mk_vit_tower_postln_d2_tok_img768_r4_5e2490'

def setup_inputs(seed: int=0):
    np.random.seed(seed)
    _w = jnp.asarray

    def _rec_inputs():
        import jax
        import jax.numpy as jnp
        _rk = jax.random.key(seed)
        x = -0.000222058 + 0.999998 * jax.random.normal(jax.random.fold_in(_rk, 1), (16, 3, 96, 96), jnp.float32)
        return x
    x = _rec_inputs()

    def _L0_tok_setup():
        import jax, jax.numpy as jnp
        import numpy as np
        from jax import lax
        HIDDEN = 192
        C_IN = 3
        PATCH = 16
        SIDE = 32
        NUM_PATCHES = SIDE * SIDE

        def _position_ids(nb_h, nb_w):
            boundaries = np.arange(1.0 / SIDE, 1.0, 1.0 / SIDE, dtype=np.float32)
            frac_h = np.arange(0.0, 1.0 - 1e-06, 1.0 / nb_h, dtype=np.float32)
            frac_w = np.arange(0.0, 1.0 - 1e-06, 1.0 / nb_w, dtype=np.float32)
            bh = np.searchsorted(boundaries, frac_h, side='right')
            bw = np.searchsorted(boundaries, frac_w, side='right')
            return jnp.asarray((bh[:, None] * SIDE + bw).reshape(-1), dtype=jnp.int32)
        key = jax.random.key(seed)
        k1, k2, k3 = jax.random.split(key, 3)
        pixel_values = jax.random.normal(k1, (32, C_IN, 128, 128), dtype=jnp.float32)
        conv_w = jax.random.normal(k2, (HIDDEN, C_IN, PATCH, PATCH), dtype=jnp.float32) * 0.02
        conv_b = jnp.zeros((HIDDEN,), dtype=jnp.float32)
        pos_table = jax.random.normal(k3, (NUM_PATCHES, HIDDEN), dtype=jnp.float32) * 0.02
        return {'pixel_values': pixel_values, 'conv_w': conv_w, 'conv_b': conv_b, 'pos_table': pos_table}
    _L0_tok_all = _L0_tok_setup()
    _L0_tok_in = {k: v for k, v in _L0_tok_all.items() if k in ('conv_w', 'conv_b', 'pos_table')}
    del _L0_tok_all

    def _L0_attn_setup():
        import jax, jax.numpy as jnp
        import numpy as np
        DIM = 192
        NUM_HEADS = 12
        HEAD_DIM = DIM // NUM_HEADS
        SCALE = HEAD_DIM ** (-0.5)
        key = jax.random.key(seed)
        ks = jax.random.split(key, 5)
        B, N = (4, 256)
        s = DIM ** (-0.5)
        return {'x': jax.random.normal(ks[0], (B, N, DIM), dtype=jnp.float32), 'w_qkv': jax.random.normal(ks[1], (DIM, 3 * DIM), dtype=jnp.float32) * s, 'b_qkv': jnp.zeros((3 * DIM,), dtype=jnp.float32), 'w_proj': jax.random.normal(ks[2], (DIM, DIM), dtype=jnp.float32) * s, 'b_proj': jnp.zeros((DIM,), dtype=jnp.float32)}
    _L0_attn_all = _L0_attn_setup()
    _L0_attn_in = {k: v for k, v in _L0_attn_all.items() if k in ('w_qkv', 'b_qkv', 'w_proj', 'b_proj')}
    del _L0_attn_all

    def _L0_ffn_setup():
        import jax, jax.numpy as jnp
        import numpy as np
        E = 192
        H = 12
        D = E // H
        HID = 768
        NEXP = 4
        TOPK = 2
        EPS = 1e-05

        def _ln(x, g, b):
            m = jnp.mean(x, axis=-1, keepdims=True)
            v = jnp.mean(jnp.square(x - m), axis=-1, keepdims=True)
            return (x - m) * jax.lax.rsqrt(v + EPS) * g + b
        key = jax.random.key(seed)
        ks = jax.random.split(key, 10)
        s = 0.02
        return {'x': jax.random.normal(ks[0], (8, 256, E), jnp.float32), 'ln1_g': jnp.ones((E,), jnp.float32), 'ln1_b': jnp.zeros((E,), jnp.float32), 'in_w': jax.random.normal(ks[1], (3 * E, E), jnp.float32) * s, 'in_b': jnp.zeros((3 * E,), jnp.float32), 'out_w': jax.random.normal(ks[2], (E, E), jnp.float32) * s, 'out_b': jnp.zeros((E,), jnp.float32), 'mlp_w1': jax.random.normal(ks[3], (E, HID), jnp.float32) * s, 'mlp_b1': jnp.zeros((HID,), jnp.float32), 'mlp_w2': jax.random.normal(ks[4], (HID, E), jnp.float32) * s, 'mlp_b2': jnp.zeros((E,), jnp.float32), 'ln2_g': jnp.ones((E,), jnp.float32), 'ln2_b': jnp.zeros((E,), jnp.float32), 'gate_w': jax.random.normal(ks[5], (NEXP, E), jnp.float32) * s, 'gate_b': jnp.zeros((NEXP,), jnp.float32), 'exp_w1': jax.random.normal(ks[6], (NEXP, E, HID), jnp.float32) * s, 'exp_b1': jnp.zeros((NEXP, HID), jnp.float32), 'exp_w2': jax.random.normal(ks[7], (NEXP, HID, E), jnp.float32) * s, 'exp_b2': jnp.zeros((NEXP, E), jnp.float32)}
    _L0_ffn_all = _L0_ffn_setup()
    _L0_ffn_in = {k: v for k, v in _L0_ffn_all.items() if k in ('ln1_g', 'ln1_b', 'in_w', 'in_b', 'out_w', 'out_b', 'mlp_w1', 'mlp_b1', 'mlp_w2', 'mlp_b2', 'ln2_g', 'ln2_b', 'gate_w', 'gate_b', 'exp_w1', 'exp_b1', 'exp_w2', 'exp_b2')}
    del _L0_ffn_all

    def _L1_attn_setup():
        import jax, jax.numpy as jnp
        import numpy as np
        key = jax.random.key(seed)
        ks = jax.random.split(key, 4)
        B, S, D = (8, 512, 192)
        lim = (6.0 / (D + D)) ** 0.5
        Z = jax.random.normal(ks[0], (B, S, D), dtype=jnp.float32)
        Wq = jax.random.uniform(ks[1], (D, D), dtype=jnp.float32, minval=-lim, maxval=lim)
        Wk = jax.random.uniform(ks[2], (D, D), dtype=jnp.float32, minval=-lim, maxval=lim)
        Wv = jax.random.uniform(ks[3], (D, D), dtype=jnp.float32, minval=-lim, maxval=lim)
        bq = jnp.zeros((D,), dtype=jnp.float32)
        bk = jnp.zeros((D,), dtype=jnp.float32)
        bv = jnp.zeros((D,), dtype=jnp.float32)
        return {'Z': Z, 'Wq': Wq, 'bq': bq, 'Wk': Wk, 'bk': bk, 'Wv': Wv, 'bv': bv}
    _L1_attn_all = _L1_attn_setup()
    _L1_attn_in = {k: v for k, v in _L1_attn_all.items() if k in ('Wq', 'bq', 'Wk', 'bk', 'Wv', 'bv')}
    del _L1_attn_all

    def _L1_ffn_setup():
        import jax, jax.numpy as jnp
        import numpy as np
        H = 12
        ALPHA = (1, 2, 3)
        DEPTH = 5
        BLOCK_DEPTH = 3
        TOTAL_DEPTH_M1 = 14 - 1
        SMALL_ACTIVE = BLOCK_DEPTH <= DEPTH <= TOTAL_DEPTH_M1 - BLOCK_DEPTH

        def _ln(x, g, b, eps=1e-05):
            m = jnp.mean(x, axis=-1, keepdims=True)
            v = jnp.mean((x - m) ** 2, axis=-1, keepdims=True)
            return (x - m) * jax.lax.rsqrt(v + eps) * g + b

        def _attn_branch(xp, w_qkv, w_proj, b_proj, keep_heads, keep_ch):
            B2, N, C = xp.shape
            hd = C // H
            scale = hd ** (-0.5)
            qkv = (xp @ w_qkv).reshape(B2, N, 3, H, hd).transpose(2, 0, 3, 1, 4)
            hmask = (jnp.arange(H) < keep_heads).astype(xp.dtype)[None, :, None, None]
            q, k, v = (qkv[0] * hmask, qkv[1] * hmask, qkv[2] * hmask)
            a = jax.nn.softmax(jnp.einsum('bhnd,bhmd->bhnm', q, k) * scale, axis=-1)
            o = jnp.einsum('bhnm,bhmd->bhnd', a, v).transpose(0, 2, 1, 3).reshape(B2, N, C)
            o = o @ w_proj + b_proj
            cmask = (jnp.arange(C) < keep_ch).astype(xp.dtype)
            return o * cmask

        def _mlp_branch(xp, w1, b1, w2, b2, keep_ch):
            C = xp.shape[-1]
            cmask = (jnp.arange(C) < keep_ch).astype(xp.dtype)
            h = jax.nn.gelu(xp * cmask @ w1 + b1, approximate=False)
            return (h @ w2 + b2) * cmask
        key = jax.random.key(seed)
        ks = jax.random.split(key, 8)
        B, N, C = (64, 257, 192)
        HID = 4 * C

        def w(k, shape):
            return jax.random.normal(k, shape, jnp.float32) * 0.02
        return {'x': jax.random.normal(ks[0], (B, N, C), jnp.float32), 'gumbel_weights': jax.random.uniform(ks[1], (3,), jnp.float32), 'n1l_g': jnp.ones((C,), jnp.float32), 'n1l_b': jnp.zeros((C,), jnp.float32), 'n1s_g': jnp.ones((C,), jnp.float32), 'n1s_b': jnp.zeros((C,), jnp.float32), 'w_qkv': w(ks[2], (C, 3 * C)), 'w_proj': w(ks[3], (C, C)), 'b_proj': jnp.zeros((C,), jnp.float32), 'n2l_g': jnp.ones((C,), jnp.float32), 'n2l_b': jnp.zeros((C,), jnp.float32), 'n2s_g': jnp.ones((C,), jnp.float32), 'n2s_b': jnp.zeros((C,), jnp.float32), 'w_fc1': w(ks[4], (C, HID)), 'b_fc1': jnp.zeros((HID,), jnp.float32), 'w_fc2': w(ks[5], (HID, C)), 'b_fc2': jnp.zeros((C,), jnp.float32)}
    _L1_ffn_all = _L1_ffn_setup()
    _L1_ffn_in = {k: v for k, v in _L1_ffn_all.items() if k in ('gumbel_weights', 'n1l_g', 'n1l_b', 'n1s_g', 'n1s_b', 'w_qkv', 'w_proj', 'b_proj', 'n2l_g', 'n2l_b', 'n2s_g', 'n2s_b', 'w_fc1', 'b_fc1', 'w_fc2', 'b_fc2')}
    del _L1_ffn_all
    return {'x': x, 'L0_tok_conv_w': _L0_tok_in['conv_w'], 'L0_tok_conv_b': _L0_tok_in['conv_b'], 'L0_tok_pos_table': _L0_tok_in['pos_table'], 'L0_attn_w_qkv': _L0_attn_in['w_qkv'], 'L0_attn_b_qkv': _L0_attn_in['b_qkv'], 'L0_attn_w_proj': _L0_attn_in['w_proj'], 'L0_attn_b_proj': _L0_attn_in['b_proj'], 'L0_ffn_ln1_g': _L0_ffn_in['ln1_g'], 'L0_ffn_ln1_b': _L0_ffn_in['ln1_b'], 'L0_ffn_in_w': _L0_ffn_in['in_w'], 'L0_ffn_in_b': _L0_ffn_in['in_b'], 'L0_ffn_out_w': _L0_ffn_in['out_w'], 'L0_ffn_out_b': _L0_ffn_in['out_b'], 'L0_ffn_mlp_w1': _L0_ffn_in['mlp_w1'], 'L0_ffn_mlp_b1': _L0_ffn_in['mlp_b1'], 'L0_ffn_mlp_w2': _L0_ffn_in['mlp_w2'], 'L0_ffn_mlp_b2': _L0_ffn_in['mlp_b2'], 'L0_ffn_ln2_g': _L0_ffn_in['ln2_g'], 'L0_ffn_ln2_b': _L0_ffn_in['ln2_b'], 'L0_ffn_gate_w': _L0_ffn_in['gate_w'], 'L0_ffn_gate_b': _L0_ffn_in['gate_b'], 'L0_ffn_exp_w1': _L0_ffn_in['exp_w1'], 'L0_ffn_exp_b1': _L0_ffn_in['exp_b1'], 'L0_ffn_exp_w2': _L0_ffn_in['exp_w2'], 'L0_ffn_exp_b2': _L0_ffn_in['exp_b2'], 'L1_attn_Wq': _L1_attn_in['Wq'], 'L1_attn_bq': _L1_attn_in['bq'], 'L1_attn_Wk': _L1_attn_in['Wk'], 'L1_attn_bk': _L1_attn_in['bk'], 'L1_attn_Wv': _L1_attn_in['Wv'], 'L1_attn_bv': _L1_attn_in['bv'], 'L1_ffn_gumbel_weights': _L1_ffn_in['gumbel_weights'], 'L1_ffn_n1l_g': _L1_ffn_in['n1l_g'], 'L1_ffn_n1l_b': _L1_ffn_in['n1l_b'], 'L1_ffn_n1s_g': _L1_ffn_in['n1s_g'], 'L1_ffn_n1s_b': _L1_ffn_in['n1s_b'], 'L1_ffn_w_qkv': _L1_ffn_in['w_qkv'], 'L1_ffn_w_proj': _L1_ffn_in['w_proj'], 'L1_ffn_b_proj': _L1_ffn_in['b_proj'], 'L1_ffn_n2l_g': _L1_ffn_in['n2l_g'], 'L1_ffn_n2l_b': _L1_ffn_in['n2l_b'], 'L1_ffn_n2s_g': _L1_ffn_in['n2s_g'], 'L1_ffn_n2s_b': _L1_ffn_in['n2s_b'], 'L1_ffn_w_fc1': _L1_ffn_in['w_fc1'], 'L1_ffn_b_fc1': _L1_ffn_in['b_fc1'], 'L1_ffn_w_fc2': _L1_ffn_in['w_fc2'], 'L1_ffn_b_fc2': _L1_ffn_in['b_fc2']}

def reference(x, L0_tok_conv_w, L0_tok_conv_b, L0_tok_pos_table, L0_attn_w_qkv, L0_attn_b_qkv, L0_attn_w_proj, L0_attn_b_proj, L0_ffn_ln1_g, L0_ffn_ln1_b, L0_ffn_in_w, L0_ffn_in_b, L0_ffn_out_w, L0_ffn_out_b, L0_ffn_mlp_w1, L0_ffn_mlp_b1, L0_ffn_mlp_w2, L0_ffn_mlp_b2, L0_ffn_ln2_g, L0_ffn_ln2_b, L0_ffn_gate_w, L0_ffn_gate_b, L0_ffn_exp_w1, L0_ffn_exp_b1, L0_ffn_exp_w2, L0_ffn_exp_b2, L1_attn_Wq, L1_attn_bq, L1_attn_Wk, L1_attn_bk, L1_attn_Wv, L1_attn_bv, L1_ffn_gumbel_weights, L1_ffn_n1l_g, L1_ffn_n1l_b, L1_ffn_n1s_g, L1_ffn_n1s_b, L1_ffn_w_qkv, L1_ffn_w_proj, L1_ffn_b_proj, L1_ffn_n2l_g, L1_ffn_n2l_b, L1_ffn_n2s_g, L1_ffn_n2s_b, L1_ffn_w_fc1, L1_ffn_b_fc1, L1_ffn_w_fc2, L1_ffn_b_fc2):
    import jax
    import jax.numpy as jnp

    def _L0_tok_ref(pixel_values, conv_w, conv_b, pos_table):
        import jax, jax.numpy as jnp
        import numpy as np
        from jax import lax
        HIDDEN = 192
        C_IN = 3
        PATCH = 16
        SIDE = 32
        NUM_PATCHES = SIDE * SIDE

        def _position_ids(nb_h, nb_w):
            boundaries = np.arange(1.0 / SIDE, 1.0, 1.0 / SIDE, dtype=np.float32)
            frac_h = np.arange(0.0, 1.0 - 1e-06, 1.0 / nb_h, dtype=np.float32)
            frac_w = np.arange(0.0, 1.0 - 1e-06, 1.0 / nb_w, dtype=np.float32)
            bh = np.searchsorted(boundaries, frac_h, side='right')
            bw = np.searchsorted(boundaries, frac_w, side='right')
            return jnp.asarray((bh[:, None] * SIDE + bw).reshape(-1), dtype=jnp.int32)
        B, _, H, W = pixel_values.shape
        nb_h, nb_w = (H // PATCH, W // PATCH)
        patches = lax.conv_general_dilated(pixel_values, conv_w, window_strides=(PATCH, PATCH), padding='VALID', dimension_numbers=('NCHW', 'OIHW', 'NCHW'))
        patches = patches + conv_b[None, :, None, None]
        embeddings = patches.reshape(B, HIDDEN, nb_h * nb_w).transpose(0, 2, 1)
        pos_ids = _position_ids(nb_h, nb_w)
        pos_emb = pos_table[pos_ids]
        return embeddings + pos_emb[None, :, :]

    def _L0_attn_ref(x, w_qkv, b_qkv, w_proj, b_proj):
        import jax, jax.numpy as jnp
        import numpy as np
        DIM = 192
        NUM_HEADS = 12
        HEAD_DIM = DIM // NUM_HEADS
        SCALE = HEAD_DIM ** (-0.5)
        B, N, C = x.shape
        H, D = (NUM_HEADS, HEAD_DIM)
        qkv = x @ w_qkv + b_qkv
        qkv = qkv.reshape(B, N, 3, H, D).transpose(2, 0, 3, 1, 4)
        q, k, v = (qkv[0] * SCALE, qkv[1], qkv[2])
        A = jnp.einsum('bhnd,bhmd->bhnm', q, k)
        numerator = 1.0 + A + 0.5 * A * A
        attn = numerator / numerator.sum(axis=-1, keepdims=True)
        out = jnp.einsum('bhnm,bhmd->bhnd', attn, v)
        out = out.transpose(0, 2, 1, 3).reshape(B, N, C)
        return out @ w_proj + b_proj

    def _L0_ffn_ref(x, ln1_g, ln1_b, in_w, in_b, out_w, out_b, mlp_w1, mlp_b1, mlp_w2, mlp_b2, ln2_g, ln2_b, gate_w, gate_b, exp_w1, exp_b1, exp_w2, exp_b2):
        import jax, jax.numpy as jnp
        import numpy as np
        E = 192
        H = 12
        D = E // H
        HID = 768
        NEXP = 4
        TOPK = 2
        EPS = 1e-05

        def _ln(x, g, b):
            m = jnp.mean(x, axis=-1, keepdims=True)
            v = jnp.mean(jnp.square(x - m), axis=-1, keepdims=True)
            return (x - m) * jax.lax.rsqrt(v + EPS) * g + b
        B, N, _ = x.shape
        h = _ln(x, ln1_g, ln1_b)
        qkv = h @ in_w.T + in_b
        q, k, v = jnp.split(qkv, 3, axis=-1)
        q = q.reshape(B, N, H, D)
        k = k.reshape(B, N, H, D)
        v = v.reshape(B, N, H, D)
        scores = jnp.einsum('bqhd,bkhd->bhqk', q, k) / jnp.sqrt(jnp.float32(D))
        attn = jax.nn.softmax(scores, axis=-1)
        ctx = jnp.einsum('bhqk,bkhd->bqhd', attn, v).reshape(B, N, E)
        x = x + ctx @ out_w.T + out_b
        x = x + jax.nn.gelu(x @ mlp_w1 + mlp_b1, approximate=False) @ mlp_w2 + mlp_b2
        xm = _ln(x, ln2_g, ln2_b)
        logits = xm @ gate_w.T + gate_b
        topv, topi = jax.lax.top_k(logits, TOPK)
        gates = jax.nn.softmax(topv, axis=-1)
        onehot = jax.nn.one_hot(topi, NEXP, dtype=x.dtype)
        comb = jnp.einsum('bnk,bnke->bne', gates, onehot)
        moe_out = jnp.zeros_like(x)
        for e in range(NEXP):
            he = jax.nn.gelu(xm @ exp_w1[e] + exp_b1[e], approximate=False)
            oe = he @ exp_w2[e] + exp_b2[e]
            moe_out = moe_out + comb[..., e:e + 1] * oe
        return x + moe_out

    def _L1_attn_ref(Z, Wq, bq, Wk, bk, Wv, bv):
        import jax, jax.numpy as jnp
        import numpy as np
        D = Z.shape[-1]
        scale = 1.0 / D ** 0.5
        Q = jnp.einsum('bsd,ed->bse', Z, Wq) + bq
        K = jnp.einsum('bsd,ed->bse', Z, Wk) + bk
        V = jnp.einsum('bsd,ed->bse', Z, Wv) + bv
        scores = jnp.einsum('bqd,bkd->bqk', Q, K) * scale
        attn = jax.nn.softmax(scores, axis=-1)
        Z_hat = jnp.einsum('bqk,bkd->bqd', attn, V)
        return Z_hat

    def _L1_ffn_ref(x, gumbel_weights, n1l_g, n1l_b, n1s_g, n1s_b, w_qkv, w_proj, b_proj, n2l_g, n2l_b, n2s_g, n2s_b, w_fc1, b_fc1, w_fc2, b_fc2):
        import jax, jax.numpy as jnp
        import numpy as np
        H = 12
        ALPHA = (1, 2, 3)
        DEPTH = 5
        BLOCK_DEPTH = 3
        TOTAL_DEPTH_M1 = 14 - 1
        SMALL_ACTIVE = BLOCK_DEPTH <= DEPTH <= TOTAL_DEPTH_M1 - BLOCK_DEPTH

        def _ln(x, g, b, eps=1e-05):
            m = jnp.mean(x, axis=-1, keepdims=True)
            v = jnp.mean((x - m) ** 2, axis=-1, keepdims=True)
            return (x - m) * jax.lax.rsqrt(v + eps) * g + b

        def _attn_branch(xp, w_qkv, w_proj, b_proj, keep_heads, keep_ch):
            B2, N, C = xp.shape
            hd = C // H
            scale = hd ** (-0.5)
            qkv = (xp @ w_qkv).reshape(B2, N, 3, H, hd).transpose(2, 0, 3, 1, 4)
            hmask = (jnp.arange(H) < keep_heads).astype(xp.dtype)[None, :, None, None]
            q, k, v = (qkv[0] * hmask, qkv[1] * hmask, qkv[2] * hmask)
            a = jax.nn.softmax(jnp.einsum('bhnd,bhmd->bhnm', q, k) * scale, axis=-1)
            o = jnp.einsum('bhnm,bhmd->bhnd', a, v).transpose(0, 2, 1, 3).reshape(B2, N, C)
            o = o @ w_proj + b_proj
            cmask = (jnp.arange(C) < keep_ch).astype(xp.dtype)
            return o * cmask

        def _mlp_branch(xp, w1, b1, w2, b2, keep_ch):
            C = xp.shape[-1]
            cmask = (jnp.arange(C) < keep_ch).astype(xp.dtype)
            h = jax.nn.gelu(xp * cmask @ w1 + b1, approximate=False)
            return (h @ w2 + b2) * cmask
        B, N, C = x.shape
        B2 = B // 2
        nl = _ln(x[:B2], n1l_g, n1l_b)
        ns = _ln(x[B2:], n1s_g, n1s_b)
        a_large = _attn_branch(nl, w_qkv, w_proj, b_proj, H, C)
        if SMALL_ACTIVE:
            a_small = sum((gumbel_weights[i] * _attn_branch(ns, w_qkv, w_proj, b_proj, H // ALPHA[i], C // ALPHA[i]) for i in range(3)))
            attn_out = jnp.concatenate([a_large, a_small], axis=0)
        else:
            attn_out = jnp.concatenate([a_large, a_large], axis=0)
        x = x + attn_out
        nl2 = _ln(x[:B2], n2l_g, n2l_b)
        ns2 = _ln(x[B2:], n2s_g, n2s_b)
        m_large = _mlp_branch(nl2, w_fc1, b_fc1, w_fc2, b_fc2, C)
        if SMALL_ACTIVE:
            m_small = sum((gumbel_weights[i] * _mlp_branch(ns2, w_fc1, b_fc1, w_fc2, b_fc2, C // ALPHA[i]) for i in range(3)))
            mlp_out = jnp.concatenate([m_large, m_small], axis=0)
        else:
            mlp_out = jnp.concatenate([m_large, m_large], axis=0)
        return x + mlp_out
    h = _L0_tok_ref(x, L0_tok_conv_w, L0_tok_conv_b, L0_tok_pos_table)
    h = _layernorm(h + _L0_attn_ref(h, L0_attn_w_qkv, L0_attn_b_qkv, L0_attn_w_proj, L0_attn_b_proj), axis=-1)
    h = _layernorm(h + _L0_ffn_ref(h, L0_ffn_ln1_g, L0_ffn_ln1_b, L0_ffn_in_w, L0_ffn_in_b, L0_ffn_out_w, L0_ffn_out_b, L0_ffn_mlp_w1, L0_ffn_mlp_b1, L0_ffn_mlp_w2, L0_ffn_mlp_b2, L0_ffn_ln2_g, L0_ffn_ln2_b, L0_ffn_gate_w, L0_ffn_gate_b, L0_ffn_exp_w1, L0_ffn_exp_b1, L0_ffn_exp_w2, L0_ffn_exp_b2), axis=-1)
    h = _layernorm(h + _L1_attn_ref(h, L1_attn_Wq, L1_attn_bq, L1_attn_Wk, L1_attn_bk, L1_attn_Wv, L1_attn_bv), axis=-1)
    h = _layernorm(h + _L1_ffn_ref(h, L1_ffn_gumbel_weights, L1_ffn_n1l_g, L1_ffn_n1l_b, L1_ffn_n1s_g, L1_ffn_n1s_b, L1_ffn_w_qkv, L1_ffn_w_proj, L1_ffn_b_proj, L1_ffn_n2l_g, L1_ffn_n2l_b, L1_ffn_n2s_g, L1_ffn_n2s_b, L1_ffn_w_fc1, L1_ffn_b_fc1, L1_ffn_w_fc2, L1_ffn_b_fc2), axis=-1)
    return h

_drawn_inputs = setup_inputs


def setup_inputs(seed=0):
    import zlib

    import numpy as np

    out = dict(_drawn_inputs(seed))
    spreads = {'L0_tok_conv_b': (0.0, 0.1),
     'L0_attn_b_qkv': (0.0, 0.1),
     'L0_attn_b_proj': (0.0, 0.1),
     'L0_ffn_ln1_g': (1.0, 0.6),
     'L0_ffn_ln1_b': (0.0, 0.8),
     'L0_ffn_in_b': (0.0, 0.448),
     'L0_ffn_out_b': (0.0, 0.1),
     'L0_ffn_mlp_b1': (0.0, 0.398),
     'L0_ffn_mlp_b2': (0.0, 0.1),
     'L0_ffn_ln2_g': (1.0, 0.6),
     'L0_ffn_ln2_b': (0.0, 0.649),
     'L0_ffn_gate_b': (0.0, 0.35),
     'L0_ffn_exp_b1': (0.0, 0.599),
     'L0_ffn_exp_b2': (0.0, 0.1),
     'L1_attn_bq': (0.0, 0.38),
     'L1_attn_bk': (0.0, 2.0),
     'L1_attn_bv': (0.0, 0.1),
     'L1_ffn_n1l_g': (1.0, 0.6),
     'L1_ffn_n1l_b': (0.0, 0.8),
     'L1_ffn_n1s_g': (1.0, 0.6),
     'L1_ffn_n1s_b': (0.0, 0.8),
     'L1_ffn_b_proj': (0.0, 0.1),
     'L1_ffn_n2l_g': (1.0, 0.6),
     'L1_ffn_n2l_b': (0.0, 2.0),
     'L1_ffn_n2s_g': (1.0, 0.6),
     'L1_ffn_n2s_b': (0.0, 2.0),
     'L1_ffn_b_fc1': (0.0, 0.748),
     'L1_ffn_b_fc2': (0.0, 0.1)}
    factors = {'L1_ffn_gumbel_weights': 6.148, 'L1_ffn_w_qkv': 3.461, 'L1_ffn_w_proj': 3.54}
    for name, (base, spread) in spreads.items():
        noise = np.random.default_rng([zlib.crc32(name.encode()), seed]).standard_normal(out[name].shape)
        drawn = base * np.exp(spread * noise) if base else spread * noise
        out[name] = jnp.asarray(drawn.astype(out[name].dtype))
    for name, factor in factors.items():
        out[name] = (out[name] * factor).astype(out[name].dtype)
    return out
```

```python
import numpy as np
import concourse.bass as bass
from concourse import mybir
from contextlib import ExitStack

F32 = mybir.dt.float32
ALU = mybir.AluOpType
ACT = mybir.ActivationFunctionType
AX = mybir.AxisListType

IMAGES, IN_CH, SIDE_PX, PATCH = 16, 3, 96, 16
GRID = SIDE_PX // PATCH
SEQ = GRID * GRID
TOKENS = IMAGES * SEQ
DIM, HEADS, HIDDEN, EXPERTS = 192, 12, 768, 4
HEAD = DIM // HEADS
PATCH_K = IN_CH * PATCH * PATCH // 128
HALF = DIM // 2
TILE = 96
TILES = TOKENS // TILE
BLOCK = TOKENS // 2
BTILES = TILES // 2
HK = HIDDEN // 128
PAIRS = IMAGES // 2
BPAIRS = PAIRS // 2
PAIR = 2 * SEQ
SECOND = 64
ROWS = SECOND + SEQ
GROUP = 3
GROUPS = HEADS // GROUP
GK = GROUP * SEQ
GV = GROUP * HEAD
GW = GV + GROUP
HHEADS = HEADS // 2
EPS = 1e-5
BANK = 512
SLOT = 256
KEEP = (DIM, DIM // 2, DIM // 3)

COLS = ["A0_bq", "A0_bk", "A0_bv", "ln1_g", "ln1_b", "A1_bq", "A1_bk", "A1_bv", "ln2_g", "ln2_b",
        "A2_bq", "A2_bk", "n1l_g", "n1l_b", "n1s_g", "n1s_b", "n2l_g", "n2l_b", "n2s_g", "n2s_b"]
HCOLS = ["M", "E0", "E1", "E2", "E3", "F"]
BROWS = ["conv_b", "A0_bp", "A1_bp", "mlp_b2", "A2_bv", "A3_bp", "fc2_b"]
GATE_AT = len(BROWS) * DIM
GUM_AT = GATE_AT + EXPERTS
NROWS = GUM_AT + 3
ID_AT = 0
HM_AT = ID_AT + 128
VM_AT = HM_AT + HHEADS
AM_AT = VM_AT + GROUPS * GW
GT_AT = AM_AT + PAIR
GE_AT = GT_AT + EXPERTS * EXPERTS
NCONST = GE_AT + EXPERTS * EXPERTS

TURNS = [("c0", 1), ("c1", 1)]


def _mha_turns(a):
    t = [(f"k{a}_0", 2), (f"q{a}_0", 2), (f"k{a}_1", 2), (f"q{a}_1", 2)]
    t += [(f"v{a}_{j}", 1) for j in range(4)]
    return t + [(f"o{a}_0", 2), (f"p{a}_0", 1), (f"o{a}_1", 2), (f"p{a}_1", 1)]


def _x_turns(k, n):
    return [(f"x{k}_0", n), (f"x{k}_1", n)]


TURNS += _x_turns(0, 1) + _mha_turns(0)
TURNS += _x_turns(1, 2) + _mha_turns(1)
TURNS += _x_turns(2, 1) + [(f"M{j}", 1) for j in range(HK)]
TURNS += _x_turns(3, 2) + [("gate", 1)]
TURNS += [(f"E0{j}", 1) for j in range(HK)] + [(f"E1{j}", 1) for j in range(HK)]
TURNS += [("ct", 1), ("cb0", 1), ("cb1", 1)]
TURNS += [(f"E2{j}", 1) for j in range(HK)] + [(f"E3{j}", 1) for j in range(HK)]
TURNS += _x_turns(4, 1) + [("k2_0", 2), ("q2_0", 2), ("k2_1", 2), ("q2_1", 2), ("s2", 1), ("t2", 1),
                           ("z2_0", 1), ("z2_1", 1), ("p2_0", 1), ("p2_1", 1)]
TURNS += _x_turns(5, 2) + _mha_turns(3)
TURNS += _x_turns(6, 2)
for _j in range(HK):
    TURNS += [(f"F{_j}", 1), (f"S{_j}", 1)]

TURN = {n: i for i, (n, _) in enumerate(TURNS)}
EMPTIED = {}
_sum = [0, 0]
for _i, (_n, _c) in enumerate(TURNS):
    _sum[_i % 2] += _c
    EMPTIED[_n] = _sum[_i % 2]

NORMS = [("a", 2), ("ln2", 1), ("b", 1), ("c", 2), ("n2", 1), ("d", 1)]
NORMED = {}
_at = 0
for _n, _c in NORMS:
    for _b in range(2):
        _at += _c * BTILES
        NORMED[f"{_n}{_b}"] = _at
RESIDUALS = [f"{s}{b}" for s in ("A0", "A1", "M", "E", "A2", "A3", "F") for b in range(2)]
ROUND = {"M": 0, "E0": 1, "E1": 2, "E2": 3, "E3": 4, "F": 5}
MHA = {0: 0, 1: 1, 3: 2}


def tower(nc, x, conv_w, pos, qkv0, proj0, inw, outw, mw1, mw2, ew1, ew2, eb2, gw, qkv2, qkv3, proj3,
          fw1, fw2, cols, hcols, brows, const, out):
    ctx = ExitStack()
    with ctx:
        def sb(name, shape):
            return ctx.enter_context(nc.sbuf_tensor(name, shape, F32))

        def sem(name):
            return ctx.enter_context(nc.semaphore(name))

        early = sb("early", [128, 2 * GROUP * TOKENS])
        conv_sb = early[:, 0:PATCH_K * DIM].rearrange("p (k c) -> p k c", k=PATCH_K)
        pos_sb = early[0:TILE, PATCH_K * DIM:(PATCH_K + TILES) * DIM].rearrange("p (t c) -> p t c", t=TILES)
        XT3 = early[0:HALF, :].rearrange("p (a i r) -> p a i r", a=2, r=GROUP * SEQ)
        qkv_sb = {0: sb("qkv0_sb", [HALF, 2, 3 * DIM]), 1: sb("inw_sb", [HALF, 2, 3 * DIM]),
                  2: sb("qkv2_sb", [HALF, 2, 3 * DIM]), 3: sb("qkv3_sb", [HALF, 2, 3 * DIM])}
        proj_sb = {0: sb("proj0_sb", [HALF, 2, DIM]), 1: sb("outw_sb", [HALF, 2, DIM]),
                   3: sb("proj3_sb", [HALF, 2, DIM])}
        proj3s_sb = sb("proj3s_sb", [HALF, 2, DIM])
        mw1_sb = sb("mw1_sb", [HALF, 2, HIDDEN])
        mw2_sb = sb("mw2_sb", [128, HK, DIM])
        ew1_sb = sb("ew1_sb", [HALF, EXPERTS, 2, HIDDEN])
        ew2_sb = sb("ew2_sb", [128, EXPERTS, HK, DIM])
        eb2_sb = sb("eb2_sb", [EXPERTS, DIM])
        gw_sb = sb("gw_sb", [HALF, 2, EXPERTS])
        fw1_sb = sb("fw1_sb", [HALF, 2, HIDDEN])
        fw2_sb = sb("fw2_sb", [128, HK, DIM])
        fw2s_sb = [sb(f"fw2s{i}_sb", [128, HK, KEEP[i]]) for i in range(3)]
        cols_sb = sb("cols_sb", [HALF, len(COLS), 2])
        hcols_sb = sb("hcols_sb", [128, len(HCOLS), HK])
        brows_sb = sb("brows_sb", [128, NROWS])
        const_sb = sb("const_sb", [128, NCONST])
        ident = const_sb[:, ID_AT:ID_AT + 128]
        vmask = const_sb[0:GK, VM_AT:VM_AT + GROUPS * GW].rearrange("p (g w) -> p g w", g=GROUPS)
        amask = const_sb[0:PAIR, AM_AT:AM_AT + PAIR]
        gsum = sb("gsum", [128, 3])
        gcol = sb("gcol", [HALF, 1])
        browss = sb("browss", [128, 2, DIM])

        big = sb("big", [128, 2 * HK * TOKENS])
        xp_sb = big[:, 0:PATCH_K * TOKENS].rearrange("p (k t) -> p k t", k=PATCH_K)
        hid = [big[:, i * HK * TOKENS:(i + 1) * HK * TOKENS].rearrange("p (k t) -> p k t", k=HK)
               for i in range(2)]
        KB = big[0:HALF, 0:2 * IMAGES * HHEADS * SEQ].rearrange("p (a i h m) -> p a i h m", a=2, i=IMAGES, h=HHEADS)
        H = sb("H", [TILE, TILES, DIM])
        RB = sb("RB", [TILE, TILES, DIM])
        Y = sb("Y", [TILE, TILES, DIM])
        NRM = sb("NRM", [TILE, TILES, DIM])
        XT = sb("XT", [HALF, 2, TOKENS])
        QT = sb("QT", [HALF, 2, TOKENS])
        KT = sb("KT", [HALF, 2, TOKENS])
        OT = sb("OT", [HALF, 2, TOKENS])
        V = sb("V", [GK, IMAGES, GROUPS, GW])
        P = sb("P", [ROWS, 2, HEADS, SEQ])
        PT = sb("PT", [GK, 2, GROUPS, ROWS])
        O = sb("O", [ROWS, 2, DIM])
        mx = sb("mx", [ROWS, 2, HEADS])
        rden = sb("rden", [ROWS, 2, GROUPS, GROUP])
        X72 = V[0:PAIR, :, :, :].rearrange("p i g w -> p (i g w)")[:, 0:PAIRS * DIM].rearrange("p (t c) -> p t c", t=PAIRS)
        P1 = NRM[0:PAIR, :, :].rearrange("p t c -> p (t c)")[:, 0:PAIRS * PAIR].rearrange("p (t m) -> p t m", t=PAIRS)
        P1T = PT[0:PAIR, :, :, :].rearrange("p b g r -> p (b g r)")[:, 0:PAIRS * PAIR].rearrange("p (t m) -> p t m", t=PAIRS)
        st1 = sb("st1", [PAIR, 3, PAIRS])
        bst = sb("bst", [TILE, TILES, 6])
        mv = sb("mv", [TILE, TILES, 2])
        rs = sb("rs", [TILE, TILES, 4])
        mhalf = sb("mhalf", [TILE, BTILES])
        L = sb("L", [TILE, TILES, EXPERTS])
        LX = sb("LX", [TILE, TILES, EXPERTS])
        LE = sb("LE", [TILE, TILES, EXPERTS])
        lm = sb("lm", [TILE, 2, TILES])
        gtm = sb("gtm", [TILE, TILES, EXPERTS * EXPERTS])
        gem = sb("gem", [TILE, TILES, EXPERTS * EXPERTS])
        comb = sb("comb", [TILE, TILES, EXPERTS])
        combT = sb("combT", [EXPERTS, TOKENS])

        G = [ctx.enter_context(nc.psum_tensor(f"G{i}", [128, 2, BANK], F32)) for i in range(2)]
        R = ctx.enter_context(nc.psum_tensor("R", [128, 4, BANK], F32))
        R_slots = R[:, :, :].rearrange("p b n -> p (b n)")

        h_dram = nc.dram_tensor("h_scratch", [TOKENS, DIM], F32).ap()

        def gslots(name, parts, n):
            g = G[TURN[name] % 2][0:parts, :, :].rearrange("p b n -> p (b n)")
            return g.rearrange("p (s c) -> p s c", c=SLOT)[:, 0:n, 0:DIM]

        def gbanks(name, parts, n):
            return G[TURN[name] % 2][0:parts, :, 0:n]

        def col(name, half):
            i = COLS.index(name)
            return cols_sb[:, i, half:half + 1]

        def row(name, parts, n):
            i = BROWS.index(name)
            return brows_sb[0:parts, i * DIM:(i + 1) * DIM].unsqueeze(1).broadcast_to([parts, n, DIM])

        LOADS = ["x", "conv_w", "pos", "brows", "const", "cols", "qkv0", "proj0", "inw", "outw", "mw1",
                 "hcols", "mw2", "gw", "ew1", "ew2", "eb2", "qkv2", "qkv3", "proj3", "fw1", "fw2"]
        loaded = {n: sem("loaded_" + n) for n in LOADS}
        full = sem("turn_full")
        emptied = [sem("turn_emptied_0"), sem("turn_emptied_1")]
        pad_set = sem("pad_set")
        ones_set = sem("ones_set")
        xt3_ready = sem("inputs_repeated")
        kb_dve = sem("keys_spread_dve")
        kb_pool = sem("keys_spread_pool")
        scored = sem("scored")
        shifted = sem("shifted")
        probs = sem("probs")
        turned = sem("probs_transposed")
        pt_ready = sem("pt_ready")
        mixed = sem("mixed")
        o_ready = sem("o_ready")
        o_turned = sem("o_transposed")
        stats = sem("stats_ready")
        rstd = sem("rstd_ready")
        normed = sem("normed")
        resid = sem("residual_ready")
        rfull = sem("r_full")
        rfree = sem("r_read")
        single = sem("single_steps")
        single_exp = sem("single_exp")
        h_saved = sem("h_saved")
        x72_loaded = sem("x72_loaded")
        logit_max = sem("logits_shifted")
        logit_exp = sem("logits_exp")
        comb_ready = sem("comb_ready")
        eff = sem("scaled_weights")
        dve_step = sem("dve_step")
        pool_step = sem("pool_step")
        act_step = sem("act_step")
        done = sem("out_saved")

        def wait_full(eng, name):
            eng.wait_ge(full, TURN[name] + 1)

        def wait_emptied(eng, name):
            eng.wait_ge(emptied[TURN[name] % 2], EMPTIED[name])

        block = ctx.enter_context(nc.Block())

        @block.sync
        def _(sp):
            def load(name, dst, src):
                sp.dma_start(dst, src).then_inc(loaded[name], 16)
            load("x", xp_sb, x)
            load("conv_w", conv_sb, conv_w)
            load("pos", pos_sb, pos)
            load("brows", brows_sb[:], brows.partition_broadcast(128))
            load("const", const_sb[:], const)
            load("cols", cols_sb[:], cols)
            load("qkv0", qkv_sb[0][:], qkv0)
            load("proj0", proj_sb[0][:], proj0)
            load("inw", qkv_sb[1][:], inw)
            load("outw", proj_sb[1][:], outw)
            load("mw1", mw1_sb[:], mw1)
            load("hcols", hcols_sb[:], hcols)
            load("mw2", mw2_sb[:], mw2)
            load("gw", gw_sb[:], gw)
            load("ew1", ew1_sb[:], ew1)
            load("ew2", ew2_sb[:], ew2)
            load("eb2", eb2_sb[:], eb2)
            load("qkv2", qkv_sb[2][:], qkv2)
            load("qkv3", qkv_sb[3][:], qkv3)
            load("proj3", proj_sb[3][:], proj3)
            load("fw1", fw1_sb[:], fw1)
            load("fw2", fw2_sb[:], fw2)
            sp.wait_ge(normed, NORMED["b1"])
            sp.dma_start(h_dram.rearrange("(t p) c -> p t c", p=TILE), H[:]).then_inc(h_saved, 16)
            sp.wait_ge(h_saved, 16)
            sp.dma_start(X72, h_dram.rearrange("(t p) c -> p t c", p=PAIR)).then_inc(x72_loaded, 16)
            for b in range(2):
                sp.wait_ge(normed, NORMED[f"d{b}"])
                sp.dma_start(out.rearrange("(t p) c -> p t c", p=TILE)[:, b * BTILES:(b + 1) * BTILES, :],
                             H[:, b * BTILES:(b + 1) * BTILES, :]).then_inc(done, 16)
            sp.wait_ge(done, 32)

        @block.tensor
        def _(pe):
            mm, tr = nc.tensor.matmul, nc.tensor.transpose

            def claim(name):
                i = TURN[name]
                if i >= 2:
                    wait_emptied(pe, TURNS[i - 2][0])

            def tokens_to_channels(k, b, src):
                name = f"x{k}_{b}"
                claim(name)
                g = gbanks(name, HALF, BLOCK)
                for t in range(BTILES):
                    for a in range(2):
                        last = tr(g[:, a, t * TILE:(t + 1) * TILE],
                                  src[:, b * BTILES + t, a * HALF:(a + 1) * HALF], ident[0:TILE, 0:TILE])
                last.then_inc(full, 1)

            def project(name, w, at, x_in, b):
                claim(name)
                g = gbanks(name, HALF, BLOCK)
                for a in range(2):
                    for k in range(2):
                        last = mm(g[:, a, :], w[:, k, at + a * HALF:at + (a + 1) * HALF],
                                  x_in[:, k, b * BLOCK:(b + 1) * BLOCK], start=(k == 0), stop=(k == 1))
                last.then_inc(full, 1)

            def project_out(name, w, b):
                claim(name)
                g = gslots(name, TILE, BTILES)
                for t in range(BTILES):
                    for k in range(2):
                        at = b * BLOCK + t * TILE
                        last = mm(g[:, t, :], OT[:, k, at:at + TILE], w[:, k, 0:DIM], start=(k == 0), stop=(k == 1))
                last.then_inc(full, 1)

            def heads_attention(a):
                n0 = MHA[a] * PAIRS
                w = qkv_sb[a]
                for b in range(2):
                    wait_emptied(pe, f"x{ {0: 0, 1: 1, 3: 5}[a] }_{b}")
                    project(f"k{a}_{b}", w, DIM, XT, b)
                    project(f"q{a}_{b}", w, 0, XT, b)

                def values(j):
                    claim(f"v{a}_{j}")
                    pe.wait_ge(xt3_ready, 2 * (2 * MHA[a] + j // 2 + 1))
                    g = gslots(f"v{a}_{j}", GK, 4)
                    for i in range(4):
                        for k in range(2):
                            last = mm(g[:, i, :], XT3[:, k, 4 * j + i, :], w[:, k, 2 * DIM:3 * DIM], start=(k == 0), stop=(k == 1))
                    last.then_inc(full, 1)

                def scores(t):
                    if t == 0:
                        wait_emptied(pe, f"q{a}_0")
                        pe.wait_ge(kb_dve, 4 * (2 * MHA[a] + 1))
                        pe.wait_ge(kb_pool, 2 * (2 * MHA[a] + 1))
                    if t == BPAIRS:
                        wait_emptied(pe, f"q{a}_1")
                        pe.wait_ge(kb_dve, 4 * (2 * MHA[a] + 2))
                        pe.wait_ge(kb_pool, 2 * (2 * MHA[a] + 2))
                    if t >= 2:
                        pe.wait_ge(shifted, n0 + t - 1)
                    for s in range(2):
                        i = 2 * t + s
                        for k in range(2):
                            last = mm(R[SECOND * s:SECOND * s + SEQ, t % 2, k * HHEADS * SEQ:(k + 1) * HHEADS * SEQ],
                                      QT[:, k, i * SEQ:(i + 1) * SEQ],
                                      KB[:, k, i, :, :].rearrange("p h m -> p (h m)"), start=True, stop=True)
                    last.then_inc(scored, 1)

                def transpose_probs(t):
                    pe.wait_ge(probs, n0 + t + 1)
                    if t >= 1:
                        pe.wait_ge(pt_ready, n0 + t)
                    for g in range(GROUPS):
                        last = tr(R[0:GK, 2, g * ROWS:(g + 1) * ROWS],
                                  P[:, t % 2, g * GROUP:(g + 1) * GROUP, :].rearrange("p h m -> p (h m)"),
                                  ident[0:ROWS, 0:ROWS])
                    last.then_inc(turned, 1)

                def mix(t):
                    pe.wait_ge(pt_ready, n0 + t + 1)
                    if t % 2 == 0:
                        wait_emptied(pe, f"v{a}_{t // 2}")
                    if t >= 1:
                        pe.wait_ge(o_ready, n0 + t)
                    for s in range(2):
                        for g in range(GROUPS):
                            at = g * GW
                            last = mm(R[SECOND * s:SECOND * s + SEQ, 3, at:at + GW],
                                      PT[:, t % 2, g, SECOND * s:SECOND * s + SEQ],
                                      V[:, 2 * t + s, g, :], start=True, stop=True)
                    last.then_inc(mixed, 1)

                def transpose_out(t):
                    name = f"o{a}_{t // BPAIRS}"
                    if t % BPAIRS == 0:
                        claim(name)
                    pe.wait_ge(o_ready, n0 + t + 1)
                    g = gbanks(name, HALF, BPAIRS * ROWS)
                    at = (t % BPAIRS) * ROWS
                    for k in range(2):
                        last = tr(g[:, k, at:at + ROWS], O[:, t % 2, k * HALF:(k + 1) * HALF], ident[0:ROWS, 0:ROWS])
                    if t % BPAIRS == BPAIRS - 1:
                        pe.wait_ge(o_ready, n0 + t + 1)
                        last.then_inc(full, 1)
                    else:
                        last.then_inc(o_turned, 1)

                values(0)
                values(1)
                for t in range(PAIRS + 3):
                    if t < PAIRS:
                        scores(t)
                    if t < 2:
                        values(2 + t)
                    if 1 <= t <= PAIRS:
                        transpose_probs(t - 1)
                    if 2 <= t <= PAIRS + 1:
                        mix(t - 2)
                    if 3 <= t:
                        transpose_out(t - 3)
                    if t == 7:
                        wait_emptied(pe, f"o{a}_0")
                        project_out(f"p{a}_0", proj_sb[a], 0)
                wait_emptied(pe, f"o{a}_1")
                if a == 3:
                    pe.wait_ge(eff, 4)
                project_out(f"p{a}_1", proj3s_sb if a == 3 else proj_sb[a], 1)

            def hidden(name, w, b_from=0):
                claim(name)
                g = gbanks(name, 128, BLOCK)
                j = int(name[-1])
                for b in range(2):
                    for k in range(2):
                        last = mm(g[:, b, :], w[:, k, j * 128:(j + 1) * 128], XT[:, k, b * BLOCK:(b + 1) * BLOCK],
                                  start=(k == 0), stop=(k == 1))
                last.then_inc(full, 1)

            def hidden_small(j):
                name = f"S{j}"
                claim(name)
                g = gbanks(name, 128, BLOCK)
                for i in (1, 2):
                    last = mm(g[:, i - 1, :], fw1_sb[0:KEEP[i], 0, j * 128:(j + 1) * 128],
                              XT[0:KEEP[i], 0, BLOCK:TOKENS], start=True, stop=True)
                last.then_inc(full, 1)

            def second(rnd, w, src):
                r = ROUND[rnd]
                wait_emptied(pe, f"{rnd}{HK - 1}")
                if HK > 1:
                    wait_emptied(pe, f"{rnd}{HK - 2}")
                for t in range(TILES):
                    if r > 0:
                        pe.wait_ge(rfree, TILES * (r - 1) + (t | 1) + 1)
                    o = R_slots[0:TILE, SLOT * t:SLOT * t + DIM]
                    for k in range(HK):
                        last = mm(o, src[:, k, t * TILE:(t + 1) * TILE], w[:, k, :], start=(k == 0), stop=(k == HK - 1))
                    last.then_inc(rfull, 1)

            pe.wait_ge(loaded["x"], 16)
            pe.wait_ge(loaded["conv_w"], 16)
            for b in range(2):
                g = gslots(f"c{b}", TILE, BTILES)
                for t in range(BTILES):
                    at = b * BLOCK + t * TILE
                    for k in range(PATCH_K):
                        last = mm(g[:, t, :], xp_sb[:, k, at:at + TILE], conv_sb[:, k, :],
                                  start=(k == 0), stop=(k == PATCH_K - 1))
                last.then_inc(full, 1)
            pe.wait_ge(loaded["const"], 16)
            for b in range(2):
                wait_emptied(pe, f"c{b}")
                tokens_to_channels(0, b, H)
            pe.wait_ge(loaded["qkv0"], 16)
            pe.wait_ge(loaded["proj0"], 16)
            pe.wait_ge(pad_set, 2)
            pe.wait_ge(ones_set, 1)
            heads_attention(0)
            for b in range(2):
                pe.wait_ge(normed, NORMED[f"a{b}"])
                tokens_to_channels(1, b, NRM)
            pe.wait_ge(loaded["inw"], 16)
            pe.wait_ge(loaded["outw"], 16)
            heads_attention(1)
            for b in range(2):
                wait_emptied(pe, f"p1_{b}")
                tokens_to_channels(2, b, Y)
            pe.wait_ge(loaded["mw1"], 16)
            pe.wait_ge(loaded["mw2"], 16)
            wait_emptied(pe, "x2_0")
            wait_emptied(pe, "x2_1")
            for j in range(HK):
                hidden(f"M{j}", mw1_sb)
            second("M", mw2_sb, hid[0])
            for b in range(2):
                pe.wait_ge(normed, NORMED[f"ln2{b}"])
                tokens_to_channels(3, b, NRM)
            pe.wait_ge(loaded["gw"], 16)
            wait_emptied(pe, "x3_0")
            wait_emptied(pe, "x3_1")
            claim("gate")
            for t in range(TILES):
                for k in range(2):
                    last = mm(gbanks("gate", TILE, TILES * EXPERTS)[:, 0, t * EXPERTS:(t + 1) * EXPERTS],
                              XT[:, k, t * TILE:(t + 1) * TILE], gw_sb[:, k, :], start=(k == 0), stop=(k == 1))
            last.then_inc(full, 1)
            pe.wait_ge(loaded["ew1"], 16)
            pe.wait_ge(loaded["ew2"], 16)
            pe.wait_ge(loaded["eb2"], 16)
            for e in range(EXPERTS):
                for j in range(HK):
                    hidden(f"E{e}{j}", ew1_sb[:, e, :, :])
                if e == 1:
                    pe.wait_ge(comb_ready, 1)
                    claim("ct")
                    for t in range(TILES):
                        last = tr(gbanks("ct", EXPERTS, BLOCK)[:, t // BTILES, (t % BTILES) * TILE:(t % BTILES + 1) * TILE],
                                  comb[:, t, :], ident[0:TILE, 0:TILE])
                    last.then_inc(full, 1)
                    wait_emptied(pe, "ct")
                    for b in range(2):
                        claim(f"cb{b}")
                        for t in range(BTILES):
                            at = b * BLOCK + t * TILE
                            last = mm(gslots(f"cb{b}", TILE, BTILES)[:, t, :], combT[:, at:at + TILE], eb2_sb[:],
                                      start=True, stop=True)
                        last.then_inc(full, 1)
                if e >= 1:
                    second(f"E{e - 1}", ew2_sb[:, e - 1, :, :], hid[e % 2])
            second(f"E{EXPERTS - 1}", ew2_sb[:, EXPERTS - 1, :, :], hid[EXPERTS % 2])
            pe.wait_ge(loaded["qkv2"], 16)
            for b in range(2):
                pe.wait_ge(normed, NORMED[f"b{b}"])
                tokens_to_channels(4, b, H)
            for b in range(2):
                wait_emptied(pe, f"x4_{b}")
                project(f"k2_{b}", qkv_sb[2], DIM, XT, b)
                project(f"q2_{b}", qkv_sb[2], 0, XT, b)
            for n in ("k2_0", "k2_1", "q2_0", "q2_1"):
                wait_emptied(pe, n)
            claim("s2")
            g = gbanks("s2", PAIR, BPAIRS * PAIR)
            for t in range(PAIRS):
                for k in range(2):
                    at = (t % BPAIRS) * PAIR
                    last = mm(g[:, t // BPAIRS, at:at + PAIR], QT[:, k, t * PAIR:(t + 1) * PAIR],
                              KT[:, k, t * PAIR:(t + 1) * PAIR], start=(k == 0), stop=(k == 1))
            last.then_inc(full, 1)
            pe.wait_ge(single, 2)
            claim("t2")
            g = gbanks("t2", PAIR, BPAIRS * PAIR)
            for t in range(PAIRS):
                at = (t % BPAIRS) * PAIR
                last = tr(g[:, t // BPAIRS, at:at + PAIR], P1[:, t, :], ident[0:PAIR, 0:PAIR])
            last.then_inc(full, 1)
            wait_emptied(pe, "t2")
            pe.wait_ge(x72_loaded, 16)
            for b in range(2):
                name = f"z2_{b}"
                claim(name)
                g = gbanks(name, HALF, BLOCK)
                for t in range(BPAIRS):
                    for k in range(2):
                        last = mm(g[:, k, t * PAIR:(t + 1) * PAIR], X72[:, b * BPAIRS + t, k * HALF:(k + 1) * HALF],
                                  P1T[:, b * BPAIRS + t, :], start=True, stop=True)
                last.then_inc(full, 1)
            for b in range(2):
                wait_emptied(pe, f"z2_{b}")
                project_out(f"p2_{b}", qkv_sb[2][:, :, 2 * DIM:3 * DIM], b)
            for b in range(2):
                pe.wait_ge(normed, NORMED[f"c{b}"])
                tokens_to_channels(5, b, NRM)
            pe.wait_ge(loaded["qkv3"], 16)
            pe.wait_ge(loaded["proj3"], 16)
            pe.wait_ge(ones_set, 2)
            heads_attention(3)
            for b in range(2):
                pe.wait_ge(normed, NORMED[f"n2{b}"])
                tokens_to_channels(6, b, NRM)
            pe.wait_ge(loaded["fw1"], 16)
            wait_emptied(pe, "x6_0")
            wait_emptied(pe, "x6_1")
            for j in range(HK):
                hidden(f"F{j}", fw1_sb)
                hidden_small(j)
            pe.wait_ge(loaded["fw2"], 16)
            pe.wait_ge(eff, 4 + 6 + 3)
            wait_emptied(pe, f"F{HK - 1}")
            wait_emptied(pe, f"S{HK - 1}")
            for t in range(TILES):
                pe.wait_ge(rfree, TILES * (ROUND["F"] - 1) + (t | 1) + 1)
                o = R_slots[0:TILE, SLOT * t:SLOT * t + DIM]
                if t < BTILES:
                    for k in range(HK):
                        last = mm(o, hid[0][:, k, t * TILE:(t + 1) * TILE], fw2_sb[:, k, :],
                                  start=(k == 0), stop=(k == HK - 1))
                else:
                    for i in range(3):
                        for k in range(HK):
                            if i == 0:
                                h = hid[0][:, k, t * TILE:(t + 1) * TILE]
                            else:
                                at = (i - 1) * BLOCK + (t - BTILES) * TILE
                                h = hid[1][:, k, at:at + TILE]
                            last = mm(o[:, 0:KEEP[i]], h, fw2s_sb[i][:, k, :], start=(i == 0 and k == 0),
                                      stop=(i == 2 and k == HK - 1), skip_group_check=True)
                last.then_inc(rfull, 1)

        @block.scalar
        def _(act):
            A = nc.scalar.activation

            def out_of(name, ins):
                ins.then_inc(emptied[TURN[name] % 2], 1)

            def channels(k, b, gain=None, shift=None):
                name = f"x{k}_{b}"
                wait_full(act, name)
                g = gbanks(name, HALF, BLOCK)
                dst = XT[:, :, b * BLOCK:(b + 1) * BLOCK]
                if gain is None:
                    out_of(name, A(dst, g, ACT.Copy))
                    return
                for a in range(2):
                    out_of(name, A(dst[:, a, :], g[:, a, :], ACT.Identity, bias=col(shift, a), scale=col(gain, a)))

            def with_bias(name, dst, bias, b):
                wait_full(act, name)
                g = gbanks(name, HALF, BLOCK)
                for a in range(2):
                    out_of(name, A(dst[:, a, b * BLOCK:(b + 1) * BLOCK], g[:, a, :], ACT.Identity, bias=col(bias, a)))

            def heads_attention(a):
                n0 = MHA[a] * PAIRS
                scale = HEAD ** -0.5
                pre = {0: "A0", 1: "A1", 3: None}[a]
                for b in range(2):
                    for n, dst in (("k", KT), ("q", QT)):
                        if pre is None:
                            wait_full(act, f"{n}{a}_{b}")
                            for i in range(2):
                                out_of(f"{n}{a}_{b}", A(dst[:, i, b * BLOCK:(b + 1) * BLOCK],
                                                        gbanks(f"{n}{a}_{b}", HALF, BLOCK)[:, i, :], ACT.Copy))
                        else:
                            with_bias(f"{n}{a}_{b}", dst, f"{pre}_b{n}", b)
                for t in range(PAIRS + 3):
                    if t < PAIRS:
                        p = P[:, t % 2, :, :].rearrange("p h m -> p (h m)")
                        if a == 0:
                            act.wait_ge(scored, n0 + t + 1)
                            if t >= 2:
                                act.wait_ge(turned, n0 + t - 1)
                            A(p, R[0:ROWS, t % 2, 0:HEADS * SEQ], ACT.Square, bias=1.0, scale=scale).then_inc(shifted, 1)
                        else:
                            act.wait_ge(shifted, n0 + t + 1)
                            A(p, p, ACT.Exp, scale=scale).then_inc(probs, 1)
                    if 1 <= t <= PAIRS:
                        u = t - 1
                        act.wait_ge(turned, n0 + u + 1)
                        if u >= 2:
                            act.wait_ge(mixed, n0 + u - 1)
                        A(PT[:, u % 2, :, :].rearrange("p g r -> p (g r)"), R[0:GK, 2, 0:GROUPS * ROWS],
                          ACT.Copy).then_inc(pt_ready, 1)
                    if t - 3 in (BPAIRS - 1, PAIRS - 1):
                        b = (t - 3) // BPAIRS
                        name = f"o{a}_{b}"
                        wait_full(act, name)
                        for k in range(2):
                            src = gbanks(name, HALF, BPAIRS * ROWS)[:, k, :].rearrange("p (t r) -> p t r", r=ROWS)
                            dst = OT[:, k, b * BLOCK:(b + 1) * BLOCK].rearrange("p (t s m) -> p t s m", s=2, m=SEQ)
                            for s in range(2):
                                i = src[:, :, s * SECOND:s * SECOND + SEQ]
                                o = dst[:, :, s, :]
                                last = (A(o, i, ACT.Copy) if pre is None else
                                        A(o, i, ACT.Identity, bias=col(f"{pre}_bv", k)))
                                if s == 1:
                                    out_of(name, last)
                                else:
                                    last.then_inc(act_step, 1)

            def gelu(name, dst):
                wait_full(act, name)
                which = name[:-1]
                out_of(name, A(dst, gbanks(name, 128, BLOCK), ACT.Gelu,
                               bias=hcols_sb[:, HCOLS.index("F" if which == "S" else which), int(name[-1]):int(name[-1]) + 1]))

            def halves(i, j):
                return hid[i][:, j, :].rearrange("p (b t) -> p b t", b=2)

            act.wait_ge(loaded["cols"], 16)
            for b in range(2):
                channels(0, b)
            heads_attention(0)
            for b in range(2):
                channels(1, b, "ln1_g", "ln1_b")
            heads_attention(1)
            for b in range(2):
                channels(2, b)
            act.wait_ge(loaded["hcols"], 16)
            for j in range(HK):
                gelu(f"M{j}", halves(0, j))
            for b in range(2):
                channels(3, b, "ln2_g", "ln2_b")
            for e in range(EXPERTS):
                for j in range(HK):
                    gelu(f"E{e}{j}", halves((e + 1) % 2, j))
                if e == 0:
                    act.wait_ge(logit_max, 1)
                    A(LE[:], LX[:], ACT.Exp).then_inc(logit_exp, 1)
                if e == 1:
                    wait_full(act, "ct")
                    out_of("ct", A(combT[:].rearrange("p (b t) -> p b t", b=2), gbanks("ct", EXPERTS, BLOCK), ACT.Copy))
            for b in range(2):
                channels(4, b)
            for b in range(2):
                with_bias(f"k2_{b}", KT, "A2_bk", b)
                with_bias(f"q2_{b}", QT, "A2_bq", b)
            act.wait_ge(single, 1)
            A(P1, P1, ACT.Exp, scale=DIM ** -0.5).then_inc(single_exp, 1)
            wait_full(act, "t2")
            out_of("t2", A(P1T.rearrange("p (b t) m -> p b (t m)", b=2), gbanks("t2", PAIR, BPAIRS * PAIR), ACT.Copy))
            for b in range(2):
                wait_full(act, f"z2_{b}")
                out_of(f"z2_{b}", A(OT[:, :, b * BLOCK:(b + 1) * BLOCK], gbanks(f"z2_{b}", HALF, BLOCK), ACT.Copy))
            channels(5, 0, "n1l_g", "n1l_b")
            channels(5, 1, "n1s_g", "n1s_b")
            heads_attention(3)
            channels(6, 0, "n2l_g", "n2l_b")
            channels(6, 1, "n2s_g", "n2s_b")
            for j in range(HK):
                gelu(f"F{j}", halves(0, j))
                gelu(f"S{j}", halves(1, j))

        @block.vector
        def _(dve):
            v = nc.vector
            steps = [0]

            def link(ins):
                ins.then_inc(dve_step, 1)
                steps[0] += 1
                dve.wait_ge(dve_step, steps[0])

            def out_of(name, ins):
                ins.then_inc(emptied[TURN[name] % 2], 1)

            def wait_resid(stage, b):
                dve.wait_ge(resid, RESIDUALS.index(f"{stage}{b}") + 1)

            def statistics(src, b, first_wait=None):
                for t in range(b * BTILES, (b + 1) * BTILES):
                    link(v.bn_stats(bst[:, t, :], src[:, t, :]))
                for t in range(b * BTILES, (b + 1) * BTILES):
                    v.bn_aggr(mv[:, t, :], bst[:, t, :]).then_inc(stats, 1)

            def normalise(norm, src, b, outs):
                n = [m for m, _ in NORMS].index(norm)
                dve.wait_ge(rstd, 2 * n + b + 1)
                for t in range(b * BTILES, (b + 1) * BTILES):
                    for dst, i in outs:
                        v.tensor_scalar(dst[:, t, :], src[:, t, :], mv[:, t, 0:1], rs[:, t, i:i + 1],
                                        ALU.subtract, ALU.mult).then_inc(normed, 1)

            def add_projection(stage, a, b):
                name = f"p{a}_{b}"
                wait_full(dve, name)
                wait_resid(stage, b)
                out_of(name, v.tensor_tensor(Y[:, b * BTILES:(b + 1) * BTILES, :], gslots(name, TILE, BTILES),
                                             RB[:, b * BTILES:(b + 1) * BTILES, :], ALU.add))
                wait_emptied(dve, name)

            def heads_attention(a, after_first):
                n0 = MHA[a] * PAIRS
                for b in range(2):
                    wait_emptied(dve, f"k{a}_{b}")
                    for h in range(4):
                        for_heads = KT[:, :, b * BLOCK:(b + 1) * BLOCK].rearrange("p a (i m) -> p a i m", m=SEQ)
                        v.tensor_scalar(KB[:, :, b * IMAGES // 2:(b + 1) * IMAGES // 2, h, :], for_heads,
                                        const_sb[0:HALF, HM_AT + h:HM_AT + h + 1], None, ALU.mult).then_inc(kb_dve, 1)

                def values(j):
                    name = f"v{a}_{j}"
                    wait_full(dve, name)
                    src = gslots(name, GK, 4).rearrange("p i (g c) -> p i g c", g=GROUPS)
                    mask = vmask[:, :, 0:GV].unsqueeze(1).broadcast_to([GK, 4, GROUPS, GV])
                    out_of(name, v.tensor_tensor(V[:, 4 * j:4 * j + 4, :, 0:GV], src, mask, ALU.mult))

                values(0)
                values(1)
                for t in range(PAIRS + 2):
                    if t < PAIRS and a == 0:
                        dve.wait_ge(shifted, n0 + t + 1)
                        p = P[:, t % 2, :, :].rearrange("p h m -> p (h m)")
                        v.tensor_scalar(p, p, 1.0, None, ALU.add).then_inc(probs, 1)
                    elif t < PAIRS:
                        dve.wait_ge(scored, n0 + t + 1)
                        s = R[0:ROWS, t % 2, 0:HEADS * SEQ].rearrange("p (h m) -> p h m", m=SEQ)
                        link(v.tensor_reduce(mx[:, t % 2, :], s, AX.X, ALU.max))
                        if t >= 2:
                            dve.wait_ge(turned, n0 + t - 1)
                        v.tensor_tensor(P[:, t % 2, :, :], s, mx[:, t % 2, :].unsqueeze(2).broadcast_to([ROWS, HEADS, SEQ]),
                                        ALU.subtract).then_inc(shifted, 1)
                    if t < 2:
                        values(2 + t)
                    if t >= 2:
                        u = t - 2
                        dve.wait_ge(mixed, n0 + u + 1)
                        o = R[0:ROWS, 3, 0:GROUPS * GW].rearrange("p (g w) -> p g w", w=GW)
                        link(v.reciprocal(rden[:, u % 2, :, :], o[:, :, GV:GW]))
                        if u >= 2:
                            w = u - 2
                            if w % BPAIRS == BPAIRS - 1:
                                wait_full(dve, f"o{a}_{w // BPAIRS}")
                            else:
                                dve.wait_ge(o_turned, MHA[a] * (PAIRS - 2) + (w + 1) - (w + 1) // BPAIRS)
                        v.tensor_tensor(O[:, u % 2, :].rearrange("p (g s d) -> p g s d", g=GROUPS, s=GROUP),
                                        o[:, :, 0:GV].rearrange("p g (s d) -> p g s d", s=GROUP),
                                        rden[:, u % 2, :, :].unsqueeze(3).broadcast_to([ROWS, GROUPS, GROUP, HEAD]),
                                        ALU.mult).then_inc(o_ready, 1)
                after_first(0)
                after_first(1)

            def gate():
                EE = EXPERTS * EXPERTS
                wait_full(dve, "gate")
                out_of("gate", v.tensor_tensor(
                    L[:], gbanks("gate", TILE, TILES * EXPERTS)[:, 0, :].rearrange("p (t e) -> p t e", e=EXPERTS),
                    brows_sb[0:TILE, GATE_AT:GATE_AT + EXPERTS].unsqueeze(1).broadcast_to([TILE, TILES, EXPERTS]), ALU.add))
                wait_emptied(dve, "gate")
                link(v.tensor_reduce(lm[:, 0, :], L[:], AX.X, ALU.max))
                v.tensor_tensor(LX[:], L[:], lm[:, 0, :].unsqueeze(2).broadcast_to([TILE, TILES, EXPERTS]),
                                ALU.subtract).then_inc(logit_max, 1)
                mine = L[:].unsqueeze(3).broadcast_to([TILE, TILES, EXPERTS, EXPERTS])
                other = L[:].unsqueeze(2).broadcast_to([TILE, TILES, EXPERTS, EXPERTS])
                for m, op, at in ((gtm, ALU.is_gt, GT_AT), (gem, ALU.is_ge, GE_AT)):
                    link(v.tensor_tensor(m[:].rearrange("p t (e f) -> p t e f", e=EXPERTS), other, mine, op))
                    link(v.tensor_tensor(m[:], m[:], const_sb[0:TILE, at:at + EE].unsqueeze(1)
                                         .broadcast_to([TILE, TILES, EE]), ALU.mult))
                link(v.tensor_tensor(gtm[:], gtm[:], gem[:], ALU.add))
                link(v.tensor_reduce(L[:], gtm[:].rearrange("p t (e f) -> p t e f", e=EXPERTS), AX.X, ALU.add))
                link(v.tensor_scalar(L[:], L[:], 1.5, None, ALU.is_lt))
                dve.wait_ge(logit_exp, 1)
                link(v.tensor_tensor(LE[:], LE[:], L[:], ALU.mult))
                link(v.tensor_reduce(lm[:, 1, :], LE[:], AX.X, ALU.add))
                link(v.reciprocal(lm[:, 1, :], lm[:, 1, :]))
                v.tensor_tensor(comb[:], LE[:], lm[:, 1, :].unsqueeze(2).broadcast_to([TILE, TILES, EXPERTS]),
                                ALU.mult).then_inc(comb_ready, 1)

            def second_plain(rnd, stage):
                for t in range(TILES):
                    if t % BTILES == 0:
                        wait_resid(stage, t // BTILES)
                    dve.wait_ge(rfull, TILES * ROUND[rnd] + (t | 1) + 1)
                    v.tensor_tensor(Y[:, t, :], R_slots[0:TILE, SLOT * t:SLOT * t + DIM], RB[:, t, :],
                                    ALU.add).then_inc(rfree, 1)
                    if t % BTILES == BTILES - 1:
                        dve.wait_ge(rfree, TILES * ROUND[rnd] + t + 1)
                        statistics(Y, t // BTILES)

            v.memset(R[32:64, 0:2, :], 1.0).then_inc(pad_set, 1)
            v.memset(R[32:64, 3, :], 1.0).then_inc(pad_set, 1)
            dve.wait_ge(loaded["pos"], 16)
            dve.wait_ge(loaded["brows"], 16)
            link(v.tensor_tensor(pos_sb, pos_sb, row("conv_b", TILE, TILES), ALU.add))
            for b in range(2):
                wait_full(dve, f"c{b}")
                out_of(f"c{b}", v.tensor_tensor(H[:, b * BTILES:(b + 1) * BTILES, :], gslots(f"c{b}", TILE, BTILES),
                                                pos_sb[:, b * BTILES:(b + 1) * BTILES, :], ALU.add))
            dve.wait_ge(loaded["const"], 16)

            def after_a0(b):
                add_projection("A0", 0, b)
                statistics(Y, b)
                normalise("a", Y, b, ((H, 0), (NRM, 2)))

            heads_attention(0, after_a0)
            heads_attention(1, lambda b: add_projection("A1", 1, b))
            second_plain("M", "M")
            for b in range(2):
                normalise("ln2", Y, b, ((NRM, 0),))
            gate()
            for b in range(2):
                wait_resid("E", b)
            for b in range(2):
                wait_full(dve, f"cb{b}")
                rb = RB[:, b * BTILES:(b + 1) * BTILES, :]
                out_of(f"cb{b}", v.tensor_tensor(rb, gslots(f"cb{b}", TILE, BTILES), rb, ALU.add))
            for b in range(2):
                wait_emptied(dve, f"cb{b}")
            dve.wait_ge(comb_ready, 1)
            for e in range(EXPERTS):
                for t in range(TILES):
                    dve.wait_ge(rfull, TILES * ROUND[f"E{e}"] + (t | 1) + 1)
                    if e >= 1:
                        dve.wait_ge(rfree, TILES * ROUND[f"E{e - 1}"] + t + 1)
                    v.scalar_tensor_tensor(out=RB[:, t, :], in0=R_slots[0:TILE, SLOT * t:SLOT * t + DIM],
                                           scalar=comb[:, t, e:e + 1], in1=RB[:, t, :], op0=ALU.mult,
                                           op1=ALU.add).then_inc(rfree, 1)
                    if e == EXPERTS - 1 and t % BTILES == BTILES - 1:
                        dve.wait_ge(rfree, TILES * ROUND[f"E{e}"] + t + 1)
                        statistics(RB, t // BTILES)
            for b in range(2):
                normalise("b", RB, b, ((H, 0),))
            wait_full(dve, "s2")
            mask = amask.unsqueeze(1).broadcast_to([PAIR, PAIRS, PAIR])
            for i in range(2):
                at = i * BPAIRS
                last = v.tensor_tensor(P1[:, at:at + BPAIRS, :],
                                       gbanks("s2", PAIR, BPAIRS * PAIR)[:, i, :].rearrange("p (t m) -> p t m", m=PAIR),
                                       mask[:, at:at + BPAIRS, :], ALU.add)
                if i == 0:
                    link(last)
                else:
                    out_of("s2", last)
            wait_emptied(dve, "s2")
            link(v.tensor_reduce(st1[:, 0, :], P1, AX.X, ALU.max))
            v.tensor_tensor(P1, P1, st1[:, 0, :].unsqueeze(2).broadcast_to([PAIR, PAIRS, PAIR]),
                            ALU.subtract).then_inc(single, 1)
            dve.wait_ge(single_exp, 1)
            link(v.tensor_reduce(st1[:, 1, :], P1, AX.X, ALU.add))
            link(v.reciprocal(st1[:, 2, :], st1[:, 1, :]))
            v.tensor_tensor(P1, P1, st1[:, 2, :].unsqueeze(2).broadcast_to([PAIR, PAIRS, PAIR]),
                            ALU.mult).then_inc(single, 1)
            for b in range(2):
                add_projection("A2", 2, b)
                statistics(Y, b)
                normalise("c", Y, b, ((H, 0), (NRM, 2)))

            def after_a3(b):
                add_projection("A3", 3, b)
                statistics(Y, b)
                normalise("n2", Y, b, ((NRM, 0),))

            heads_attention(3, after_a3)
            second_plain("F", "F")
            for b in range(2):
                normalise("d", Y, b, ((H, 0),))

        @block.gpsimd
        def _(pool):
            g = nc.gpsimd
            steps = [0]

            def link(ins):
                ins.then_inc(pool_step, 1)
                steps[0] += 1
                pool.wait_ge(pool_step, steps[0])

            def bl(b):
                return slice(b * BTILES, (b + 1) * BTILES)

            def residual(b, first, second_):
                g.tensor_tensor(RB[:, bl(b), :], first[:, bl(b), :], second_, ALU.add).then_inc(resid, 1)

            def keys(a):
                for b in range(2):
                    wait_emptied(pool, f"x{ {0: 0, 1: 1, 3: 5}[a] }_{b}")
                    im = slice(b * IMAGES // 2, (b + 1) * IMAGES // 2)
                    for k in range(2):
                        g.tensor_copy(XT3[:, k, im, :].rearrange("p i (r m) -> p i r m", r=GROUP),
                                      XT[:, k, b * BLOCK:(b + 1) * BLOCK].rearrange("p (i m) -> p i m", m=SEQ)
                                      .unsqueeze(2).broadcast_to([HALF, IMAGES // 2, GROUP, SEQ])).then_inc(xt3_ready, 1)
                    wait_emptied(pool, f"k{a}_{b}")
                    for h in range(4, HHEADS):
                        src = KT[:, :, b * BLOCK:(b + 1) * BLOCK].rearrange("p a (i m) -> p a i m", m=SEQ)
                        g.tensor_scalar(KB[:, :, b * IMAGES // 2:(b + 1) * IMAGES // 2, h, :], src,
                                        const_sb[0:HALF, HM_AT + h:HM_AT + h + 1], None, ALU.mult).then_inc(kb_pool, 1)

            def inverse_deviation(norm, b):
                n = [m for m, _ in NORMS].index(norm)
                both = NORMS[n][1] == 2
                pool.wait_ge(stats, TILES * n + BTILES * (b + 1))
                var, r0, r1, r2, tmp = mv[:, bl(b), 1], rs[:, bl(b), 0], rs[:, bl(b), 1], rs[:, bl(b), 2], rs[:, bl(b), 3]
                link(g.tensor_scalar(tmp, var, EPS, None, ALU.add))
                first = g.tensor_tensor(r0, tmp, mhalf[:], ALU.pow)
                if not both:
                    first.then_inc(rstd, 1)
                    return
                link(first)
                link(g.tensor_tensor(tmp, var, r0, ALU.mult))
                link(g.tensor_tensor(tmp, tmp, r0, ALU.mult))
                link(g.tensor_scalar(tmp, tmp, EPS, None, ALU.add))
                link(g.tensor_tensor(r1, tmp, mhalf[:], ALU.pow))
                g.tensor_tensor(r2, r0, r1, ALU.mult).then_inc(rstd, 1)

            link(g.memset(mhalf[:], -0.5))
            pool.wait_ge(loaded["const"], 16)
            ones = vmask[:, :, GV:GW].unsqueeze(1).broadcast_to([GK, IMAGES, GROUPS, GROUP])

            def set_ones():
                g.tensor_copy(V[:, :, :, GV:GW], ones).then_inc(ones_set, 1)

            set_ones()
            pool.wait_ge(loaded["brows"], 16)
            for b in range(2):
                wait_emptied(pool, f"c{b}")
                residual(b, H, row("A0_bp", TILE, BTILES))
            keys(0)
            for b in range(2):
                inverse_deviation("a", b)
            for b in range(2):
                pool.wait_ge(normed, NORMED[f"a{b}"])
                residual(b, H, row("A1_bp", TILE, BTILES))
            keys(1)
            gum = brows_sb[:, GUM_AT:GUM_AT + 3]
            link(g.tensor_copy(gsum[:, 0:1], gum[:, 0:1]))
            link(g.tensor_tensor(gsum[:, 1:2], gsum[:, 0:1], gum[:, 1:2], ALU.add))
            link(g.tensor_tensor(gsum[:, 2:3], gsum[:, 1:2], gum[:, 2:3], ALU.add))
            c1, c2 = KEEP[2], KEEP[1]
            link(g.tensor_copy(gcol[0:c1, :], gsum[0:c1, 2:3]))
            link(g.tensor_copy(gcol[c1:HALF, :], gsum[c1:HALF, 1:2]))
            pool.wait_ge(loaded["proj3"], 16)
            w = proj_sb[3]
            for a, lo, hi, s in ((0, 0, c1, gcol[:, 0:1]), (0, c1, c2, gsum[0:HALF, 1:2]),
                                 (0, c2, DIM, gsum[0:HALF, 0:1]), (1, 0, DIM, gsum[0:HALF, 0:1])):
                g.tensor_scalar(proj3s_sb[:, a, lo:hi], w[:, a, lo:hi], s, None, ALU.mult).then_inc(eff, 1)
            for i, name in enumerate(("A3_bp", "fc2_b")):
                r = BROWS.index(name) * DIM
                for lo, hi, k in ((0, c1, 2), (c1, c2, 1), (c2, DIM, 0)):
                    g.tensor_scalar(browss[:, i, lo:hi], brows_sb[:, r + lo:r + hi], gsum[:, k:k + 1], None,
                                    ALU.mult).then_inc(eff, 1)
            pool.wait_ge(loaded["fw2"], 16)
            for i in range(3):
                g.tensor_scalar(fw2s_sb[i][:], fw2_sb[:, :, 0:KEEP[i]], gum[:, i:i + 1], None,
                                ALU.mult).then_inc(eff, 1)

            def small_row(i, b):
                return browss[0:TILE, i, :].unsqueeze(1).broadcast_to([TILE, BTILES, DIM])

            for b in range(2):
                wait_emptied(pool, f"p1_{b}")
                residual(b, Y, row("mlp_b2", TILE, BTILES))
            for b in range(2):
                inverse_deviation("ln2", b)
            for b in range(2):
                pool.wait_ge(rfree, TILES * ROUND["M"] + BTILES * (b + 1))
                residual(b, Y, H[:, bl(b), :])
            for b in range(2):
                inverse_deviation("b", b)
            for b in range(2):
                pool.wait_ge(normed, NORMED[f"b{b}"])
                residual(b, H, row("A2_bv", TILE, BTILES))
            for b in range(2):
                inverse_deviation("c", b)
            pool.wait_ge(full, TURN["z2_1"] + 1)
            set_ones()
            for b in range(2):
                pool.wait_ge(normed, NORMED[f"c{b}"])
                if b == 1:
                    pool.wait_ge(eff, 4 + 6)
                residual(b, H, row("A3_bp", TILE, BTILES) if b == 0 else small_row(0, b))
            keys(3)
            for b in range(2):
                inverse_deviation("n2", b)
            for b in range(2):
                wait_emptied(pool, f"p3_{b}")
                link(g.tensor_tensor(RB[:, bl(b), :], Y[:, bl(b), :], H[:, bl(b), :], ALU.add))
                residual(b, RB, row("fc2_b", TILE, BTILES) if b == 0 else small_row(1, b))
            for b in range(2):
                inverse_deviation("d", b)


def _constants():
    c = np.zeros((128, NCONST), np.float32)
    c[:, ID_AT:ID_AT + 128] = np.eye(128)
    for p in range(HALF):
        c[p, HM_AT + p // HEAD] = 1
    for p in range(GK):
        for g in range(GROUPS):
            at = VM_AT + g * GW
            s = p // SEQ
            c[p, at + s * HEAD:at + (s + 1) * HEAD] = 1
            c[p, at + GV + s] = 1
    for p in range(PAIR):
        for m in range(PAIR):
            c[p, AM_AT + m] = 0 if p // SEQ == m // SEQ else -1e30
    for e in range(EXPERTS):
        for f in range(EXPERTS):
            c[:, GT_AT + e * EXPERTS + f] = f > e
            c[:, GE_AT + e * EXPERTS + f] = f < e
    return c


def _position_ids(n, side=32):
    boundaries = np.arange(1.0 / side, 1.0, 1.0 / side, dtype=np.float32)
    frac = np.arange(0.0, 1.0 - 1e-06, 1.0 / n, dtype=np.float32)
    at = np.searchsorted(boundaries, frac, side="right")
    return (at[:, None] * side + at).reshape(-1)


def kernel(**inputs):
    import concourse.bacc as _bacc
    from concourse.bass_utils import run_bass_kernel_spmd as _run

    a = {k: np.asarray(v) for k, v in inputs.items()}

    def channels(w):
        return w.reshape(2, HALF, -1).transpose(1, 0, 2)

    def hidden(w):
        return w.reshape(HK, 128, -1).transpose(1, 0, 2)

    x = a["x"].reshape(IMAGES, IN_CH, GRID, PATCH, GRID, PATCH).transpose(1, 3, 5, 0, 2, 4)
    x = x.reshape(PATCH_K, 128, TOKENS).transpose(1, 0, 2)
    conv = a["L0_tok_conv_w"].reshape(DIM, PATCH_K, 128).transpose(2, 1, 0)
    pos = a["L0_tok_pos_table"][_position_ids(GRID)]
    pos = np.concatenate([pos] * IMAGES).reshape(TILES, TILE, DIM).transpose(1, 0, 2)
    qb, ib = a["L0_attn_b_qkv"], a["L0_ffn_in_b"]
    cols = [qb[0:DIM], qb[DIM:2 * DIM], qb[2 * DIM:], a["L0_ffn_ln1_g"], a["L0_ffn_ln1_b"], ib[0:DIM], ib[DIM:2 * DIM],
            ib[2 * DIM:], a["L0_ffn_ln2_g"], a["L0_ffn_ln2_b"], a["L1_attn_bq"], a["L1_attn_bk"]]
    cols += [a["L1_ffn_" + n] for n in ("n1l_g", "n1l_b", "n1s_g", "n1s_b", "n2l_g", "n2l_b", "n2s_g", "n2s_b")]
    cols = np.stack(cols).reshape(len(COLS), 2, HALF).transpose(2, 0, 1)
    hcols = np.concatenate([a["L0_ffn_mlp_b1"][None], a["L0_ffn_exp_b1"], a["L1_ffn_b_fc1"][None]])
    hcols = hcols.reshape(len(HCOLS), HK, 128).transpose(2, 0, 1)
    brows = np.concatenate([a["L0_tok_conv_b"], a["L0_attn_b_proj"], a["L0_ffn_out_b"], a["L0_ffn_mlp_b2"],
                            a["L1_attn_bv"], a["L1_ffn_b_proj"], a["L1_ffn_b_fc2"], a["L0_ffn_gate_b"],
                            a["L1_ffn_gumbel_weights"]])
    ins = {
        "x": x, "conv_w": conv, "pos": pos, "qkv0": channels(a["L0_attn_w_qkv"]), "proj0": channels(a["L0_attn_w_proj"]),
        "inw": channels(a["L0_ffn_in_w"].T), "outw": channels(a["L0_ffn_out_w"].T),
        "mw1": channels(a["L0_ffn_mlp_w1"]), "mw2": hidden(a["L0_ffn_mlp_w2"]),
        "ew1": a["L0_ffn_exp_w1"].reshape(EXPERTS, 2, HALF, HIDDEN).transpose(2, 0, 1, 3),
        "ew2": a["L0_ffn_exp_w2"].reshape(EXPERTS, HK, 128, DIM).transpose(2, 0, 1, 3), "eb2": a["L0_ffn_exp_b2"],
        "gw": channels(a["L0_ffn_gate_w"].T),
        "qkv2": channels(np.concatenate([a["L1_attn_Wq"].T, a["L1_attn_Wk"].T, a["L1_attn_Wv"].T], axis=1)),
        "qkv3": channels(a["L1_ffn_w_qkv"]), "proj3": channels(a["L1_ffn_w_proj"]),
        "fw1": channels(a["L1_ffn_w_fc1"]), "fw2": hidden(a["L1_ffn_w_fc2"]),
        "cols": cols, "hcols": hcols, "brows": brows, "const": _constants(),
    }
    nc = _bacc.Bacc("TRN2", target_bir_lowering=False, num_devices=1)
    arrays, args = {}, []
    for name, v in ins.items():
        v = np.ascontiguousarray(v)
        arrays["in_" + name] = v
        args.append(nc.dram_tensor("in_" + name, v.shape, mybir.dt.from_np(v.dtype), kind="ExternalInput").ap())
    res = nc.dram_tensor("out_dram", (TOKENS, DIM), F32, kind="ExternalOutput").ap()
    tower(nc, out=res, **dict(zip(ins, args)))
    r = _run(nc, [arrays], core_ids=[0])
    return r.results[0]["out_dram"].reshape(IMAGES, SEQ, DIM)
```

```python
import numpy as np
import concourse.bass as bass
from concourse import mybir
from contextlib import ExitStack

F32 = mybir.dt.float32
F32R = mybir.dt.float32r
ALU = mybir.AluOpType
ACT = mybir.ActivationFunctionType
AX = mybir.AxisListType

IMAGES, IN_CH, SIDE_PX, PATCH = 16, 3, 96, 16
GRID = SIDE_PX // PATCH
SEQ = GRID * GRID
TOKENS = IMAGES * SEQ
DIM, HEADS, HIDDEN, EXPERTS = 192, 12, 768, 4
HEAD = DIM // HEADS
PATCH_K = IN_CH * PATCH * PATCH // 128
HALF = DIM // 2
TILE = 96
TILES = TOKENS // TILE
BLOCK = TOKENS // 2
BTILES = TILES // 2
HK = HIDDEN // 128
PAIRS = IMAGES // 2
BPAIRS = PAIRS // 2
PAIR = 2 * SEQ
SECOND = 64
ROWS = SECOND + SEQ
GROUP = 3
GROUPS = HEADS // GROUP
GK = GROUP * SEQ
GV = GROUP * HEAD
GW = GV + GROUP
HHEADS = HEADS // 2
POOL_FROM = 5
EPS = 1e-5
WARM = 5
BANK = 512
SLOT = 256
KEEP = (DIM, DIM // 2, DIM // 3)

COLS = ["A0_bq", "A0_bk", "A0_bv", "ln1_g", "ln1_b", "A1_bq", "A1_bk", "A1_bv", "ln2_g", "ln2_b",
        "A2_bq", "A2_bk", "n1l_g", "n1l_b", "n1s_g", "n1s_b", "n2l_g", "n2l_b", "n2s_g", "n2s_b"]
HCOLS = ["M", "E0", "E1", "E2", "E3", "F"]
BROWS = ["conv_b", "A0_bp", "A1_bp", "mlp_b2", "A2_bv", "A3_bp", "fc2_b"]
GATE_AT = len(BROWS) * DIM
GUM_AT = GATE_AT + EXPERTS
NROWS = GUM_AT + 3
ID_AT = 0
HM_AT = ID_AT + 128
VM_AT = HM_AT + HHEADS
AM_AT = VM_AT + GROUPS * GW
GT_AT = AM_AT + PAIR
GE_AT = GT_AT + EXPERTS * EXPERTS
NCONST = GE_AT + EXPERTS * EXPERTS

MHA = {0: 0, 1: 1, 3: 2}
ROUNDS = ["M", "E0", "E1", "E2", "E3", "F"]
X_OF = {0: 0, 1: 1, 2: 4, 3: 5}
NORM_OF = {0: "a", 2: "c", 3: "n2"}


NORM_BEHIND = {("M", 0): "ln2", ("M", 1): "ln2", ("E3", 0): "b", ("E3", 1): "b", ("F", 0): "d", ("V2", 1): "d"}


def _front(a, b):
    return [("x", X_OF[a], b), ("k", a, b), ("q", a, b), ("vt", a, b)]


def _attend(a, b, before, norm, split, then):
    s, e, t, w = [[(n, a, b, i) for i in range(BPAIRS)] for n in "SETW"]
    v = [("v", a, b, j) for j in range(2)]
    out = [] if not before else [("z2", before[1])] if before[0] == 2 else [("O", *before)]
    o = [s[0]] + out + [e[0], s[1], e[1]] + ([("p", *before)] if before else [])
    o += [v[0], t[0], s[2], e[2]] + norm + [t[1], s[3]]
    if then[-1][0] == "h":
        return o + [v[1], e[3], w[0], then[0], t[2], w[1]] + _residual_norm(norm) + split + [
            t[3], w[2], ("table", "gelu"), w[3], then[2], then[3]]
    return o + [w[0], then[0], e[3], t[2], w[1]] + _residual_norm(norm) + [then[1]] + split + [
        v[1], t[3], then[2], w[2], then[3], w[3]]


def _residual_norm(norm):
    return [("nh",) + n[1:] for n in norm if n[1] in ("a", "c")]


def _hidden(rnd, b):
    return [("h", rnd, b, i) for i in range(HK // 2)]


def _order():
    o = [("c", 0), ("c", 1), ("x", 0, 0), ("x", 0, 1), ("k", 0, 0), ("q", 0, 0), ("vt", 0, 0)]
    o += _attend(0, 0, (), [], [("ws", 0, 0)], [("nop",)] + _front(0, 1)[1:])
    o += _attend(0, 1, (0, 0), [("n", "a", 0)], [("ws", 0, 1)], _front(1, 0))
    o += _attend(1, 0, (0, 1), [("n", "a", 1)], [("ws", 1, 0)], _front(1, 1))
    h = _hidden("M", 0)
    o += _attend(1, 1, (1, 0), [], [("ws", 1, 1)], [("x", 2, 0), ("nop",)] + h[0:2])
    o += [("O", 1, 1), h[2], ("p", 1, 1), ("x", 2, 1), ("s", "M", 0)]
    h = _hidden("M", 1)
    o += [("n", "ln2", 0), h[0], h[1], ("x", 3, 0), h[2], ("ws", 2, 0)]
    h = _hidden("E0", 0)
    o += [h[0], ("s", "M", 1), ("n", "ln2", 1), h[1], h[2], ("gate", 0), ("x", 3, 1), ("ws", 2, 1), ("gate", 1), ("comb",),
          ("table", "gelu"), ("s", "E0", 0)] + _hidden("E0", 1) + [("ws", 3, 0)]
    for e in range(1, EXPERTS):
        if e > 1:
            o += [("s", f"E{e - 1}", 0)]
        o += _hidden(f"E{e}", 0) + [("s", f"E{e - 1}", 1)]
        if e + 2 < len(ROUNDS):
            o += [("ws", e + 2, 1)]
        h = _hidden(f"E{e}", 1)
        if e == 3:
            o += [("s", "E3", 0), ("n", "b", 0)] + h
        elif e == 1:
            o += [("ct",), h[0], ("cb", 0), h[1], ("cb", 1), h[2], ("branches",)]
        else:
            o += h
        if e + 3 < len(ROUNDS):
            o += [("ws", e + 3, 0)]
    o += [("x", 4, 0), ("k", 2, 0), ("q", 2, 0), ("table", "exp"), ("s2", 0), ("e2", 0), ("s", "E3", 1), ("t2", 0), ("z2", 0),
          ("n", "b", 1), ("x", 4, 1), ("p", 2, 0), ("k", 2, 1), ("q", 2, 1), ("n", "c", 0), ("s2", 1), ("x", 5, 0), ("e2", 1), ("nh", "c", 0)]
    o += _front(3, 0)[1:] + [("t2", 1)]
    o += _attend(3, 0, (2, 1), [("n", "c", 1)], [], _front(3, 1))
    h = _hidden("F", 0)
    o += _attend(3, 1, (3, 0), [("n", "n2", 0)], [], [("x", 6, 0), ("nop",)] + h[0:2])
    o += [("O", 3, 1), h[2], ("p", 3, 1), ("n", "n2", 1), ("s", "F", 0), ("x", 6, 1), ("n", "d", 0)]
    o += _hidden("F", 1) + _hidden("V1", 1) + [("s", "F", 1)] + _hidden("V2", 1) + [("s", "V1", 1), ("s", "V2", 1)]
    o += [("n", "d", 1)]
    with_statistics = []
    for p in o:
        with_statistics.append(p)
        if p[0] == "p" and p[1] in NORM_OF:
            with_statistics.append(("st", NORM_OF[p[1]], p[2]))
        elif p[1:] in NORM_BEHIND and p[0] == "s":
            with_statistics.append(("st", NORM_BEHIND[p[1:]], p[2]))
    return with_statistics


ORDER = _order()
SPLIT_X = [(2, 0), (2, 1), (3, 0), (3, 1), (6, 0), (6, 1)]


def _vector_order():
    o = list(ORDER)

    def move(piece, behind):
        o.remove(piece)
        o.insert(o.index(behind) + 1, piece)

    move(("h", "M", 0, 2), ("p", 1, 1))
    move(("h", "F", 0, 2), ("p", 3, 1))
    move(("st", "d", 0), ("x", 6, 1))
    return o


VECTOR_ORDER = _vector_order()


def _emptying(piece):
    kind = piece[0]
    if kind == "x":
        return 0 if piece[1:] in SPLIT_X else 2 if piece[1] in GAINS else 1
    if kind in ("k", "q", "vt", "h"):
        return 2
    if kind == "O":
        return 2
    if kind == "v":
        return GROUP
    return 1 if kind in ("c", "p", "gate", "ct", "cb", "s2", "t2", "z2") else None


GAINS = {1: (("ln1_g", "ln1_b"),) * 2, 3: (("ln2_g", "ln2_b"),) * 2,
         5: (("n1l_g", "n1l_b"), ("n1s_g", "n1s_b")), 6: (("n2l_g", "n2l_b"), ("n2s_g", "n2s_b"))}
TURNS = [p for p in ORDER if _emptying(p) is not None]
TURN = {p: i for i, p in enumerate(TURNS)}
EMPTIED = {}
_sum = [0, 0]
for _i, _p in enumerate(TURNS):
    _sum[_i % 2] += _emptying(_p)
    EMPTIED[_p] = _sum[_i % 2]


def _numbered(kind):
    return {p: i for i, p in enumerate([p for p in ORDER if p[0] == kind])}


HIDDEN_NO, SECOND_NO, SPLIT_NO, VALUES_NO = _numbered("h"), _numbered("s"), _numbered("ws"), _numbered("v")
NORMS = {"a": 2, "ln2": 1, "b": 1, "c": 2, "n2": 1, "d": 1}
NORM_NO, NORMED_FIRST, NORMED = {}, {}, {}
_at = 0
for _p in [p for p in ORDER if p[0] in ("n", "nh")]:
    _at += BTILES
    NORMED[_p[1:]] = _at
    if _p[0] == "n":
        NORM_NO[_p[1:]] = len(NORM_NO)
        NORMED_FIRST[_p[1:]] = _at
WIDTH = {"V1": KEEP[1], "V2": KEEP[2]}
RESIDUAL_AT = {("c", 0): ("A0", 0), ("c", 1): ("A0", 1)}
for _b in range(2):
    RESIDUAL_AT[("nh", "a", _b)] = ("A1", _b)
    RESIDUAL_AT[("p", 1, _b)] = ("M", _b)
    RESIDUAL_AT[("n", "ln2", _b)] = ("E", _b)
    RESIDUAL_AT[("n", "b", _b)] = ("A2", _b)
    RESIDUAL_AT[("nh", "c", _b)] = ("A3", _b)
    RESIDUAL_AT[("n", "n2", _b)] = ("F", _b)
RESIDUAL_NO = {RESIDUAL_AT[p]: i for i, p in enumerate([p for p in ORDER if p in RESIDUAL_AT])}


def tower(nc, x, conv_w, pos, qkv0, proj0, inw, outw, mw1, mw2, ew1, ew2, eb2, gw, qkv2, qkv3, proj3,
          fw1, fw2, cols, hcols, brows, const, out):
    ctx = ExitStack()
    with ctx:
        def sb(name, shape, dt=F32):
            return ctx.enter_context(nc.sbuf_tensor(name, shape, dt))

        def sem(name):
            return ctx.enter_context(nc.semaphore(name))

        qkv_at = [sb("qkv_even", [HALF, 2, 3 * DIM]), sb("qkv_odd", [HALF, 2, 3 * DIM])]
        qkv_sb = {a: qkv_at[a % 2] for a in range(4)}
        proj_sb = {a: sb(f"proj{a}_sb", [HALF, 2, DIM]) for a in (0, 1, 3)}
        proj3s_sb = sb("proj3s_sb", [HALF, 2, DIM])
        raw = [sb("raw_w1", [HALF, 2, HIDDEN]), sb("raw_w2", [128, HK, DIM])]
        w_parts = [[[sb(f"w{i + 1}_{part}{s}", shape, F32R) for part in ("hi", "lo")]
                    for i, shape in enumerate(([HALF, 2, HIDDEN], [128, HK, DIM]))] for s in range(2)]
        eb2_sb = sb("eb2_sb", [EXPERTS, DIM])
        gw_sb = sb("gw_sb", [HALF, 2, EXPERTS])
        cols_sb = sb("cols_sb", [HALF, len(COLS), 2])
        hcols_sb = sb("hcols_sb", [128, len(HCOLS), HK])
        brows_sb = sb("brows_sb", [128, NROWS])
        const_sb = sb("const_sb", [128, NCONST])
        ident = const_sb[:, ID_AT:ID_AT + 128]
        vmask = const_sb[0:GK, VM_AT:VM_AT + GROUPS * GW].rearrange("p (g w) -> p g w", g=GROUPS)
        amask = const_sb[0:PAIR, AM_AT:AM_AT + PAIR]
        gum = brows_sb[:, GUM_AT:GUM_AT + 3]
        gsum = sb("gsum", [128, 3])
        gcol = sb("gcol", [HALF, 1])
        idle = sb("idle", [128, 1])
        browss = sb("browss", [128, 2, DIM])

        keys = sb("keys", [128, 2 * IMAGES * HHEADS * SEQ])
        xp_sb = keys[:, 0:PATCH_K * TOKENS].rearrange("p (b t k m) -> p b t k m", b=2, t=BTILES, k=PATCH_K)
        KB = keys[0:HALF, :].rearrange("p (a i h m) -> p a i h m", a=2, i=IMAGES, h=HHEADS)
        H = sb("H", [TILE, TILES, DIM])
        RB = sb("RB", [TILE, TILES, DIM])
        Y = sb("Y", [TILE, TILES, DIM])
        NRM = sb("NRM", [TILE, TILES, DIM])
        XT = sb("XT", [HALF, 2, TOKENS])
        XS = [sb(f"XT_{part}", [HALF, 2, TOKENS], F32R) for part in ("hi", "lo")]
        VT3 = sb("VT3", [HALF, 2, IMAGES // 2, GROUP * SEQ])
        QT = sb("QT", [HALF, 2, TOKENS])
        KT = sb("KT", [HALF, 2, TOKENS])
        OT = KT
        hid_tmp = sb("hid_tmp", [128, 2, 2 * BLOCK])
        hid = [[sb(f"hid{b}_{part}", [128, HK, BLOCK], F32R) for part in ("hi", "lo")] for b in range(2)]
        values = sb("values", [128, IMAGES * GROUPS * GW])
        V = values[0:GK, :].rearrange("p (i g w) -> p i g w", i=IMAGES, g=GROUPS)
        conv_sb = values[:, 0:PATCH_K * DIM].rearrange("p (k c) -> p k c", k=PATCH_K)
        pos_sb = values[0:TILE, PATCH_K * DIM:(PATCH_K + TILES) * DIM].rearrange("p (t c) -> p t c", t=TILES)
        XP = values[0:PAIR, 0:PAIRS * DIM].rearrange("p (t c) -> p t c", t=PAIRS)
        P = sb("P", [ROWS, 2, HEADS, SEQ])
        PT = sb("PT", [GK, 2, GROUPS, ROWS])
        O = sb("O", [ROWS, BPAIRS, DIM])
        mx = sb("mx", [ROWS, 2, HEADS])
        rden = sb("rden", [ROWS, 2, GROUPS, GROUP])
        P1 = [NRM[0:PAIR, b * BTILES:(b + 1) * BTILES, :].rearrange("p t c -> p (t c)")[:, 0:BPAIRS * PAIR]
              .rearrange("p (t m) -> p t m", t=BPAIRS) for b in range(2)]
        P1T = PT[0:PAIR, :, :, :].rearrange("p b g r -> p (b g r)")[:, 0:PAIRS * PAIR].rearrange("p (t m) -> p t m", t=PAIRS)
        st1 = sb("st1", [PAIR, 3, PAIRS])
        bst = sb("bst", [TILE, TILES, 6])
        mv = sb("mv", [TILE, TILES, 2])
        shifted_var = sb("shifted_var", [TILE, 2, TILES])
        rs = sb("rs", [TILE, 2, TILES])
        mhalf = sb("mhalf", [TILE, 2, BTILES])
        L = sb("L", [TILE, TILES, EXPERTS])
        LX = sb("LX", [TILE, TILES, EXPERTS])
        LE = sb("LE", [TILE, TILES, EXPERTS])
        lm = sb("lm", [TILE, 2, TILES])
        gtm = sb("gtm", [TILE, TILES, EXPERTS * EXPERTS])
        gem = sb("gem", [TILE, TILES, EXPERTS * EXPERTS])
        comb = sb("comb", [TILE, TILES, EXPERTS])
        combT = QT[0:EXPERTS, 0, :]

        G = [ctx.enter_context(nc.psum_tensor(f"G{i}", [128, 2, BANK], F32)) for i in range(2)]
        R = ctx.enter_context(nc.psum_tensor("R", [128, 4, BANK], F32))
        R_slots = R[:, :, :].rearrange("p b n -> p (b n)")
        h_dram = nc.dram_tensor("h_scratch", [TOKENS, DIM], F32).ap()

        def gslots(turn, parts, n):
            g = G[TURN[turn] % 2][0:parts, :, :].rearrange("p b n -> p (b n)")
            return g.rearrange("p (s c) -> p s c", c=SLOT)[:, 0:n, 0:DIM]

        def gbanks(turn, parts, n):
            return G[TURN[turn] % 2][0:parts, :, 0:n]

        def bt(b):
            return slice(b * BTILES, (b + 1) * BTILES)

        def bc(b):
            return slice(b * BLOCK, (b + 1) * BLOCK)

        def col(name, half):
            return cols_sb[:, COLS.index(name), half:half + 1]

        def row(name, parts, n):
            i = BROWS.index(name)
            return brows_sb[0:parts, i * DIM:(i + 1) * DIM].unsqueeze(1).broadcast_to([parts, n, DIM])

        LOADS = [f"x{t}" for t in range(BTILES + 1)] + ["conv_w", "pos", "brows", "const", "cols", "qkv0", "qkv1", "qkv2", "qkv3", "proj0",
                 "proj1", "proj3", "hcols", "gw", "eb2"]
        loaded = {n: sem("loaded_" + n) for n in LOADS}
        raw_loaded = [sem("raw_w1_loaded"), sem("raw_w2_loaded")]
        full = sem("turn_full")
        emptied = [sem("turn_emptied_0"), sem("turn_emptied_1")]
        pad_set = sem("pad_set")
        ones_set = sem("ones_set")
        warm_set = sem("warm_set")
        kb_dve = sem("keys_spread_dve")
        kb_pool = sem("keys_spread_pool")
        scored = sem("scored")
        shifted = sem("shifted")
        probs = sem("probs")
        turned = sem("probs_transposed")
        pt_ready = sem("pt_ready")
        mixed = sem("mixed")
        o_ready = sem("o_ready")
        stats = sem("stats_ready")
        rstd = sem("rstd_ready")
        normed = sem("normed")
        resid = sem("residual_ready")
        xs_hi, xs_lo = sem("x_hi"), sem("x_lo")
        xs_sum = sem("x_unsplit")
        hid_hi, hid_lo = sem("hid_hi"), sem("hid_lo")
        tmp_ready = sem("hid_tmp_ready")
        ws_hi, ws_lo = sem("w_hi"), sem("w_lo")
        rfull = sem("r_full")
        rfree = sem("r_read")
        single = sem("single_steps")
        single_exp = sem("single_exp")
        h_saved = sem("h_saved")
        xp_loaded = [sem("xp_loaded_0"), sem("xp_loaded_1")]
        logit_max = sem("logits_shifted")
        logit_exp = sem("logits_exp")
        comb_ready = sem("comb_ready")
        eff = sem("scaled_weights")
        dve_step = sem("dve_step")
        pool_step = sem("pool_step")
        done = sem("out_saved")

        def wait_full(eng, turn):
            eng.wait_ge(full, TURN[turn] + 1)

        def wait_emptied(eng, turn):
            if turn[0] == "x" and turn[1:] in SPLIT_X:
                n = 2 * (SPLIT_X.index(turn[1:]) + 1)
                eng.wait_ge(xs_hi, n)
                eng.wait_ge(xs_sum, n)
                return
            eng.wait_ge(emptied[TURN[turn] % 2], EMPTIED[turn])

        def pair_no(a, b, t):
            return (2 * MHA[a] + b) * BPAIRS + t

        def wait_hid_free(eng, rnd, b):
            n = HIDDEN_NO["h", rnd, b, 0]
            before = [h for h in list(HIDDEN_NO)[:n] if HID_AT[h[1], h[2]] == HID_AT[rnd, b]]
            if before:
                eng.wait_ge(rfull, BTILES * (SECOND_NO["s", before[-1][1], before[-1][2]] + 1))

        def wait_slot_free(eng, r, i):
            if r >= 2 and i == 0:
                wait_full(eng, ("h", ROUNDS[r - 2], 1, HK // 2 - 1))
            elif r >= 2:
                eng.wait_ge(rfull, BTILES * (SECOND_NO["s", ROUNDS[r - 2], 1] + 1))

        block = ctx.enter_context(nc.Block())

        @block.sync
        def _(sp):
            def load(name, dst, src):
                sp.dma_start(dst, src).then_inc(loaded[name], 16)

            def load_raw(i, src):
                if i >= 2:
                    sp.wait_ge(ws_hi, i - 1)
                    sp.wait_ge(ws_lo, i - 1)
                sp.dma_start(raw[i % 2][:], src).then_inc(raw_loaded[i % 2], 16)

            for t in range(BTILES):
                load(f"x{t}", xp_sb[:, 0, t, :, :], x[:, 0, t, :, :])
            load(f"x{BTILES}", xp_sb[:, 1, :, :, :], x[:, 1, :, :, :])
            load("qkv0", qkv_sb[0][:], qkv0)
            load("proj0", proj_sb[0][:], proj0)
            load("qkv1", qkv_sb[1][:], inw)
            load("proj1", proj_sb[1][:], outw)
            load_raw(0, mw1)
            load_raw(1, mw2)
            load("hcols", hcols_sb[:], hcols)
            load("gw", gw_sb[:], gw)
            load("eb2", eb2_sb[:], eb2)
            load("proj3", proj_sb[3][:], proj3)
            load_raw(2, ew1[:, 0, :, :])
            load_raw(3, ew2[:, 0, :, :])
            wait_full(sp, ("vt", 0, 1))
            load("qkv2", qkv_sb[2][:], qkv2)
            load_raw(4, ew1[:, 1, :, :])
            load_raw(5, ew2[:, 1, :, :])
            wait_full(sp, ("vt", 1, 1))
            load("qkv3", qkv_sb[3][:], qkv3)
            for e in range(2, EXPERTS):
                load_raw(2 * e + 2, ew1[:, e, :, :])
                load_raw(2 * e + 3, ew2[:, e, :, :])
            load_raw(2 * EXPERTS + 2, fw1)
            load_raw(2 * EXPERTS + 3, fw2)
            for b in range(2):
                sp.wait_ge(normed, NORMED["b", b])
                sp.dma_start(h_dram.rearrange("(t p) c -> p t c", p=TILE)[:, bt(b), :], H[:, bt(b), :]).then_inc(h_saved, 16)
                sp.wait_ge(h_saved, 16 * (b + 1))
                pairs = slice(b * BPAIRS, (b + 1) * BPAIRS)
                sp.dma_start(XP[:, pairs, :], h_dram.rearrange("(t p) c -> p t c", p=PAIR)[:, pairs, :]).then_inc(xp_loaded[b], 16)
            for b in range(2):
                sp.wait_ge(normed, NORMED["d", b])
                sp.dma_start(out.rearrange("(t p) c -> p t c", p=TILE)[:, bt(b), :], H[:, bt(b), :]).then_inc(done, 16)
            sp.wait_ge(done, 32)

        @block.tensor
        def _(pe):
            mm, tr = nc.tensor.matmul, nc.tensor.transpose

            def claim(turn):
                if TURN[turn] >= 2:
                    wait_emptied(pe, TURNS[TURN[turn] - 2])

            def mm_split(o, w, m, start, stop):
                mm(o, w[0], m[0], start=start, stop=False)
                mm(o, w[0], m[1], start=False, stop=False)
                return mm(o, w[1], m[0], start=False, stop=stop)

            def patches(b):
                if b == 0:
                    pe.wait_ge(loaded["conv_w"], 16)
                g = gslots(("c", b), TILE, BTILES)
                for t in range(BTILES):
                    if b == 0 or t == 0:
                        pe.wait_ge(loaded[f"x{b * BTILES + t}"], 16)
                    for k in range(PATCH_K):
                        last = mm(g[:, t, :], xp_sb[:, b, t, k, :], conv_sb[:, k, :],
                                  start=(k == 0), stop=(k == PATCH_K - 1))
                last.then_inc(full, 1)

            def tokens_to_channels(k, b):
                turn = ("x", k, b)
                src = {0: H, 1: NRM, 2: Y, 3: NRM, 4: H, 5: NRM, 6: NRM}[k]
                if k == 0:
                    pe.wait_ge(loaded["const"], 16)
                    wait_emptied(pe, ("c", b))
                elif k == 2:
                    wait_emptied(pe, ("p", 1, b))
                claim(turn)
                g = gbanks(turn, HALF, BLOCK)
                for t in range(BTILES):
                    if k not in (0, 2):
                        first = NORMED_FIRST[{1: "a", 3: "ln2", 4: "b", 5: "c", 6: "n2"}[k], b]
                        pe.wait_ge(normed, first - BTILES + t + 1)
                    for a in range(2):
                        last = tr(g[:, a, t * TILE:(t + 1) * TILE],
                                  src[:, b * BTILES + t, a * HALF:(a + 1) * HALF], ident[0:TILE, 0:TILE])
                last.then_inc(full, 1)

            def project(n, a, b):
                if n == "k":
                    pe.wait_ge(loaded[f"qkv{a}"], 16)
                    wait_emptied(pe, ("x", X_OF[a], b))
                claim((n, a, b))
                g = gbanks((n, a, b), HALF, BLOCK)
                at = {"q": 0, "k": DIM, "vt": 2 * DIM}[n]
                for i in range(2):
                    for k in range(2):
                        last = mm(g[:, i, :], qkv_sb[a][:, k, at + i * HALF:at + (i + 1) * HALF], XT[:, k, bc(b)],
                                  start=(k == 0), stop=(k == 1))
                last.then_inc(full, 1)

            def project_out(a, b):
                turn = ("p", a, b)
                w = qkv_sb[a][:, :, 2 * DIM:3 * DIM] if a == 2 else proj_sb[a]
                if a == 3 and b == 1:
                    w = proj3s_sb
                    pe.wait_ge(eff, 4)
                if a != 2:
                    pe.wait_ge(loaded[f"proj{a}"], 16)
                wait_emptied(pe, ("z2", b) if a == 2 else ("O", a, b))
                claim(turn)
                g = gslots(turn, TILE, BTILES)
                for t in range(BTILES):
                    at = b * BLOCK + t * TILE
                    for k in range(2):
                        last = mm(g[:, t, :], OT[:, k, at:at + TILE], w[:, k, 0:DIM], start=(k == 0), stop=(k == 1))
                last.then_inc(full, 1)

            def values_of(a, b, j):
                turn = ("v", a, b, j)
                claim(turn)
                wait_emptied(pe, ("vt", a, b))
                g = gslots(turn, GK, 4)
                for i in range(4):
                    for k in range(2):
                        last = tr(g[:, i, k * HALF:(k + 1) * HALF], VT3[:, k, 4 * j + i, :], ident[0:HALF, 0:HALF])
                last.then_inc(full, 1)

            def scores(a, b, t):
                n = pair_no(a, b, t)
                if t == 0:
                    wait_emptied(pe, ("q", a, b))
                    pe.wait_ge(kb_dve, POOL_FROM * (2 * MHA[a] + b + 1))
                    pe.wait_ge(kb_pool, (HHEADS - POOL_FROM) * (2 * MHA[a] + b + 1))
                if n == 0:
                    pe.wait_ge(pad_set, 2)
                if n >= 2:
                    pe.wait_ge(shifted, n - 1)
                for s in range(2):
                    i = 2 * (b * BPAIRS + t) + s
                    for k in range(2):
                        last = mm(R[SECOND * s:SECOND * s + SEQ, n % 2, k * HHEADS * SEQ:(k + 1) * HHEADS * SEQ],
                                  QT[:, k, i * SEQ:(i + 1) * SEQ],
                                  KB[:, k, i, :, :].rearrange("p h m -> p (h m)"), start=True, stop=True)
                last.then_inc(scored, 1)

            def transpose_probs(a, b, t):
                n = pair_no(a, b, t)
                if a == 0:
                    pe.wait_ge(shifted, n + 1)
                else:
                    pe.wait_ge(probs, n + 1 - PAIRS)
                if n >= 1:
                    pe.wait_ge(pt_ready, n)
                for g in range(GROUPS):
                    last = tr(R[0:GK, 2, g * ROWS:(g + 1) * ROWS],
                              P[:, n % 2, g * GROUP:(g + 1) * GROUP, :].rearrange("p h m -> p (h m)"),
                              ident[0:ROWS, 0:ROWS])
                last.then_inc(turned, 1)

            def mix(a, b, t):
                n = pair_no(a, b, t)
                pe.wait_ge(pt_ready, n + 1)
                if t % 2 == 0:
                    wait_emptied(pe, ("v", a, b, t // 2))
                if t == 0:
                    pe.wait_ge(ones_set, 2 if a == 3 else 1)
                    pe.wait_ge(pad_set, 3 if a == 3 else 2)
                if n >= 1:
                    pe.wait_ge(o_ready, n)
                for s in range(2):
                    for g in range(GROUPS):
                        last = mm(R[SECOND * s:SECOND * s + SEQ, 3, g * GW:(g + 1) * GW],
                                  PT[:, n % 2, g, SECOND * s:SECOND * s + SEQ],
                                  V[:, 2 * (b * BPAIRS + t) + s, g, :], start=True, stop=True)
                last.then_inc(mixed, 1)

            def transpose_out(a, b):
                turn = ("O", a, b)
                claim(turn)
                pe.wait_ge(o_ready, pair_no(a, b, BPAIRS))
                g = gbanks(turn, HALF, BPAIRS * 2 * SECOND)
                for t in range(BPAIRS):
                    for k in range(2):
                        last = tr(g[:, k, 2 * SECOND * t:2 * SECOND * t + ROWS], O[:, t, k * HALF:(k + 1) * HALF], ident[0:ROWS, 0:ROWS])
                last.then_inc(full, 1)

            def hidden(rnd, b, i):
                r = ROUNDS.index("F" if rnd in WIDTH else rnd)
                turn = ("h", rnd, b, i)
                if i == 0:
                    pe.wait_ge(ws_hi, 2 * r + 1)
                    pe.wait_ge(ws_lo, 2 * r + 1)
                    n = SPLIT_X.index(({"M": 2, "F": 6, "V1": 6, "V2": 6}.get(rnd, 3), b)) + 1
                    pe.wait_ge(xs_hi, 2 * n)
                    pe.wait_ge(xs_lo, n)
                claim(turn)
                g = gbanks(turn, 128, BLOCK)
                w = w_parts[r % 2][0]
                keep = WIDTH.get(rnd, HALF)
                for u in range(2):
                    at = (2 * i + u) * 128
                    for k in range(1 if rnd in WIDTH else 2):
                        last = mm_split(g[:, u, :], [p[0:keep, k, at:at + 128] for p in w],
                                        [p[0:keep, k, bc(b)] for p in XS], k == 0, k == 1 or rnd in WIDTH)
                last.then_inc(full, 1)

            def second(rnd, b):
                r = ROUNDS.index("F" if rnd in WIDTH else rnd)
                no = SECOND_NO["s", rnd, b]
                pe.wait_ge(ws_hi, 2 * r + 2)
                pe.wait_ge(ws_lo, 2 * r + 2)
                h = HIDDEN_NO["h", rnd, b, HK // 2 - 1] + 1
                pe.wait_ge(hid_hi, h)
                pe.wait_ge(hid_lo, h)
                before = [s for s in list(SECOND_NO)[:no] if s[2] == b]
                if before:
                    pe.wait_ge(rfree, BTILES * (SECOND_NO[before[-1]] + 1))
                width = WIDTH.get(rnd, DIM)
                src = hid[HID_AT[rnd, b]]
                for t in range(BTILES):
                    at = 2 * BANK * b + SLOT * t
                    for k in range(HK):
                        last = mm_split(R_slots[0:TILE, at:at + width], [p[:, k, t * TILE:(t + 1) * TILE] for p in src],
                                        [p[:, k, 0:width] for p in w_parts[r % 2][1]], k == 0, k == HK - 1)
                    last.then_inc(rfull, 1)

            def gate(b):
                pe.wait_ge(loaded["gw"], 16)
                wait_emptied(pe, ("x", 3, b))
                claim(("gate", b))
                for t in range(BTILES):
                    at = b * BLOCK + t * TILE
                    for k in range(2):
                        last = mm(gbanks(("gate", b), TILE, BTILES * EXPERTS)[:, 0, t * EXPERTS:(t + 1) * EXPERTS],
                                  XT[:, k, at:at + TILE], gw_sb[:, k, :], start=(k == 0), stop=(k == 1))
                last.then_inc(full, 1)

            def transpose_comb():
                pe.wait_ge(comb_ready, 1)
                claim(("ct",))
                g = gbanks(("ct",), EXPERTS, BLOCK)
                for t in range(TILES):
                    at = (t % BTILES) * TILE
                    last = tr(g[:, t // BTILES, at:at + TILE], comb[:, t, :], ident[0:TILE, 0:TILE])
                last.then_inc(full, 1)

            def expert_biases(b):
                if b == 0:
                    pe.wait_ge(loaded["eb2"], 16)
                    wait_emptied(pe, ("ct",))
                claim(("cb", b))
                for t in range(BTILES):
                    at = b * BLOCK + t * TILE
                    last = mm(gslots(("cb", b), TILE, BTILES)[:, t, :], combT[:, at:at + TILE], eb2_sb[:],
                              start=True, stop=True)
                last.then_inc(full, 1)

            def single_scores(b):
                wait_emptied(pe, ("k", 2, b))
                wait_emptied(pe, ("q", 2, b))
                claim(("s2", b))
                g = gbanks(("s2", b), PAIR, BLOCK)
                for t in range(BPAIRS):
                    at = b * BLOCK + t * PAIR
                    for k in range(2):
                        last = mm(g[:, 0, t * PAIR:(t + 1) * PAIR], QT[:, k, at:at + PAIR], KT[:, k, at:at + PAIR],
                                  start=(k == 0), stop=(k == 1))
                last.then_inc(full, 1)

            def single_transpose(b):
                pe.wait_ge(single, 2 * b + 2)
                claim(("t2", b))
                g = gbanks(("t2", b), PAIR, BLOCK)
                for t in range(BPAIRS):
                    last = tr(g[:, 0, t * PAIR:(t + 1) * PAIR], P1[b][:, t, :], ident[0:PAIR, 0:PAIR])
                last.then_inc(full, 1)

            def single_mix(b):
                wait_emptied(pe, ("t2", b))
                pe.wait_ge(xp_loaded[b], 16)
                claim(("z2", b))
                g = gbanks(("z2", b), HALF, BLOCK)
                for t in range(BPAIRS):
                    for k in range(2):
                        last = mm(g[:, k, t * PAIR:(t + 1) * PAIR], XP[:, b * BPAIRS + t, k * HALF:(k + 1) * HALF],
                                  P1T[:, b * BPAIRS + t, :], start=True, stop=True)
                last.then_inc(full, 1)

            pe.wait_ge(warm_set, 1)
            for i in range(WARM):
                mm(R[0:HALF, 2, 0:BLOCK], QT[:, 0, 0:HALF], QT[:, 0, 0:BLOCK], start=True, stop=True)
            for kind, *at in ORDER:
                if kind == "c":
                    patches(*at)
                elif kind == "x":
                    tokens_to_channels(*at)
                elif kind in ("k", "q", "vt"):
                    project(kind, *at)
                elif kind == "v":
                    values_of(*at)
                elif kind == "S":
                    scores(*at)
                elif kind == "T":
                    transpose_probs(*at)
                elif kind == "W":
                    mix(*at)
                elif kind == "O":
                    transpose_out(*at)
                elif kind == "p":
                    project_out(*at)
                elif kind == "h":
                    hidden(*at)
                elif kind == "s":
                    second(*at)
                elif kind == "gate":
                    gate(*at)
                elif kind == "ct":
                    transpose_comb()
                elif kind == "cb":
                    expert_biases(*at)
                elif kind == "s2":
                    single_scores(*at)
                elif kind == "t2":
                    single_transpose(*at)
                elif kind == "z2":
                    single_mix(*at)

        @block.scalar
        def _(act):
            A = nc.scalar.activation

            def out_of(turn, ins):
                ins.then_inc(emptied[TURN[turn] % 2], 1)

            def channels(k, b):
                turn = ("x", k, b)
                wait_full(act, turn)
                g = gbanks(turn, HALF, BLOCK)
                split = (k, b) in SPLIT_X
                dst = (XS[0] if split else XT)[:, :, bc(b)]
                if not split and k not in GAINS:
                    out_of(turn, A(dst, g, ACT.Copy))
                    return
                for a in range(2):
                    if k in GAINS:
                        gain, shift = GAINS[k][b]
                        ins = [(ACT.Identity, dict(bias=col(shift, a), scale=col(gain, a)))]
                    else:
                        ins = [(ACT.Copy, {})]
                    if split and a == 1:
                        act.wait_ge(xs_sum, 2 * SPLIT_X.index((k, b)) + 1)
                    ins = A(dst[:, a, :], g[:, a, :], ins[0][0], **ins[0][1])
                    if split:
                        ins.then_inc(xs_hi, 1)
                    else:
                        out_of(turn, ins)

            def value_channels(a, b):
                turn = ("vt", a, b)
                n = VALUES_NO["v", a, b, 0]
                if n:
                    wait_full(act, list(VALUES_NO)[n - 1])
                wait_full(act, turn)
                for k in range(2):
                    out_of(turn, A(VT3[:, k, :, :].rearrange("p i (r m) -> p i r m", r=GROUP),
                                   gbanks(turn, HALF, BLOCK)[:, k, :].rearrange("p (i m) -> p i m", m=SEQ)
                                   .unsqueeze(2).broadcast_to([HALF, IMAGES // 2, GROUP, SEQ]), ACT.Copy))

            def keys_or_queries(n, a, b):
                turn = (n, a, b)
                wait_full(act, turn)
                g = gbanks(turn, HALF, BLOCK)
                for i in range(2):
                    dst = (KT if n == "k" else QT)[:, i, bc(b)]
                    if a == 3:
                        out_of(turn, A(dst, g[:, i, :], ACT.Copy))
                    else:
                        out_of(turn, A(dst, g[:, i, :], ACT.Identity, bias=col(f"A{a}_b{n}", i)))

            def weights(a, b, t):
                n = pair_no(a, b, t)
                p = P[:, n % 2, :, :].rearrange("p h m -> p (h m)")
                scale = HEAD ** -0.5
                if a == 0:
                    act.wait_ge(scored, n + 1)
                    if n >= 2:
                        act.wait_ge(turned, n - 1)
                    A(p, R[0:ROWS, n % 2, 0:HEADS * SEQ], ACT.Square, bias=1.0, scale=scale).then_inc(shifted, 1)
                else:
                    act.wait_ge(shifted, n + 1)
                    A(p, p, ACT.Exp, scale=scale).then_inc(probs, 1)

            def copy_transposed(a, b, t):
                n = pair_no(a, b, t)
                act.wait_ge(turned, n + 1)
                if n >= 2:
                    act.wait_ge(mixed, n - 1)
                dst, src = PT[:, n % 2, :, :].rearrange("p g r -> p (g r)"), R[0:GK, 2, 0:GROUPS * ROWS]
                (A(dst, src, ACT.Identity, bias=1.0) if a == 0 else A(dst, src, ACT.Copy)).then_inc(pt_ready, 1)

            def values_of(a, b, j):
                turn = ("v", a, b, j)
                wait_full(act, turn)
                src = gslots(turn, GK, 4).rearrange("p i (g c) -> p i g c", g=GROUPS)
                at = b * IMAGES // 2 + 4 * j
                for h in range(GROUP):
                    ch = slice(h * HEAD, (h + 1) * HEAD)
                    out_of(turn, A(V[:, at:at + 4, :, ch], src[:, :, :, ch], ACT.Identity, bias=0.0,
                                   scale=vmask[:, 0, h * HEAD:h * HEAD + 1]))

            def attention_out(a, b):
                turn = ("O", a, b)
                wait_full(act, turn)
                for k in range(2):
                    src = gbanks(turn, HALF, BPAIRS * 2 * SECOND)[:, k, :].rearrange("p (i r) -> p i r", r=SECOND)[:, :, 0:SEQ]
                    dst = OT[:, k, bc(b)].rearrange("p (i m) -> p i m", m=SEQ)
                    out_of(turn, A(dst, src, ACT.Copy) if a == 3 else
                           A(dst, src, ACT.Identity, bias=col(f"A{a}_bv", k)))

            def gelu(rnd, b, i):
                turn = ("h", rnd, b, i)
                n = HIDDEN_NO[turn]
                tmp = hid_tmp[:, n % 2, :].rearrange("p (u t) -> p u t", u=2)
                if n == 0:
                    act.wait_ge(loaded["hcols"], 16)
                if n >= 2:
                    act.wait_ge(hid_lo, n - 1)
                wait_full(act, turn)
                bias = HCOLS.index("F" if rnd in WIDTH else rnd)
                for u in range(2):
                    out_of(turn, A(tmp[:, u, :], gbanks(turn, 128, BLOCK)[:, u, :], ACT.Gelu,
                                   bias=hcols_sb[:, bias, 2 * i + u:2 * i + u + 1]))
                wait_emptied(act, turn)
                if i == 0:
                    wait_hid_free(act, rnd, b)
                dst = hid[HID_AT[rnd, b]][0][:, 2 * i:2 * i + 2, :]
                if (rnd, b) in BRANCH:
                    j = BRANCH[rnd, b]
                    A(dst, tmp, ACT.Identity, bias=0.0, scale=gum[:, j:j + 1]).then_inc(hid_hi, 1)
                else:
                    A(dst, tmp, ACT.Copy).then_inc(hid_hi, 1)

            act.dma_start(conv_sb, conv_w).then_inc(loaded["conv_w"], 16)
            act.dma_start(pos_sb, pos).then_inc(loaded["pos"], 16)
            act.dma_start(const_sb[:], const).then_inc(loaded["const"], 16)
            act.dma_start(brows_sb[:], brows.partition_broadcast(128)).then_inc(loaded["brows"], 16)
            act.dma_start(cols_sb[:], cols).then_inc(loaded["cols"], 16)
            act.wait_ge(loaded["cols"], 16)
            act.wait_ge(loaded["const"], 16)
            A(idle[:], const_sb[:, 0:1], ACT.Exp)
            act.wait_ge(loaded["brows"], 16)
            for kind, *at in ORDER:
                if kind == "x":
                    channels(*at)
                elif kind in ("k", "q"):
                    keys_or_queries(kind, *at)
                elif kind == "vt":
                    value_channels(*at)
                elif kind == "v":
                    values_of(*at)
                elif kind == "E":
                    weights(*at)
                elif kind == "table":
                    A(idle[:], const_sb[:, 0:1], {"exp": ACT.Exp, "gelu": ACT.Gelu}[at[0]])
                elif kind == "T":
                    copy_transposed(*at)
                elif kind == "O":
                    attention_out(*at)
                elif kind == "h":
                    gelu(*at)
                elif kind == "comb":
                    act.wait_ge(logit_max, 1)
                    A(LE[:], LX[:], ACT.Exp).then_inc(logit_exp, 1)
                elif kind == "ct":
                    wait_full(act, ("ct",))
                    out_of(("ct",), A(combT.rearrange("p (b t) -> p b t", b=2), gbanks(("ct",), EXPERTS, BLOCK), ACT.Copy))
                elif kind == "e2":
                    b = at[0]
                    p = P1[b]
                    act.wait_ge(single, 2 * b + 1)
                    A(p, p, ACT.Exp, scale=DIM ** -0.5).then_inc(single_exp, 1)
                elif kind == "t2":
                    turn, b = ("t2", at[0]), at[0]
                    wait_full(act, turn)
                    out_of(turn, A(P1T[:, b * BPAIRS:(b + 1) * BPAIRS, :].rearrange("p t m -> p (t m)"),
                                   gbanks(turn, PAIR, BLOCK)[:, 0, :], ACT.Copy))
                elif kind == "z2":
                    turn = ("z2", at[0])
                    wait_full(act, turn)
                    out_of(turn, A(OT[:, :, bc(at[0])], gbanks(turn, HALF, BLOCK), ACT.Copy))

        @block.vector
        def _(dve):
            v = nc.vector
            steps = [0]

            def link(ins):
                ins.then_inc(dve_step, 1)
                steps[0] += 1
                dve.wait_ge(dve_step, steps[0])

            def out_of(turn, ins):
                ins.then_inc(emptied[TURN[turn] % 2], 1)

            def wait_resid(stage, b):
                dve.wait_ge(resid, RESIDUAL_NO[stage, b] + 1)

            def row_statistics(src, ts):
                for t in ts:
                    v.bn_stats(bst[:, t, :], src[:, t, :]).then_inc(dve_step, 1)
                    steps[0] += 1

            def statistics(norm, b):
                ts = range(b * BTILES, (b + 1) * BTILES)
                if norm in NORM_OF.values():
                    a = {n: a for a, n in NORM_OF.items()}[norm]
                    wait_emptied(dve, ("p", a, b))
                    row_statistics(Y, ts)
                else:
                    rnd = [r for r, n in NORM_BEHIND.items() if n == norm and r[1] == b][0]
                    dve.wait_ge(rfree, BTILES * (SECOND_NO["s", *rnd] + 1))
                    row_statistics(RB if norm == "b" else Y, ts[2:])
                dve.wait_ge(dve_step, steps[0])
                for t in ts:
                    last = v.bn_aggr(mv[:, t, :], bst[:, t, :])
                    if t < ts[-1]:
                        last.then_inc(dve_step, 1)
                        steps[0] += 1
                link(last)
                var = mv[:, bt(b), 1]
                if NORMS[norm] == 2:
                    link(v.tensor_scalar(shifted_var[:, 1, bt(b)], var, 1.0 + EPS, EPS * EPS, ALU.mult, ALU.add))
                v.tensor_scalar(shifted_var[:, 0, bt(b)], var, EPS, None, ALU.add).then_inc(stats, 1)

            def normalise(norm, b, residual=False):
                src = RB if norm == "b" else Y
                if norm in ("a", "c"):
                    dst, i = (H, 0) if residual else (NRM, 1)
                else:
                    dst, i = (NRM if norm in ("ln2", "n2") else H), 0
                dve.wait_ge(rstd, NORM_NO[norm, b] + 1)
                for t in range(b * BTILES, (b + 1) * BTILES):
                    v.tensor_scalar(dst[:, t, :], src[:, t, :], mv[:, t, 0:1], rs[:, i, t:t + 1],
                                    ALU.subtract, ALU.mult).then_inc(normed, 1)

            def patch_rows(b):
                if b == 0:
                    dve.wait_ge(loaded["pos"], 16)
                    dve.wait_ge(loaded["brows"], 16)
                    link(v.tensor_tensor(pos_sb, pos_sb, row("conv_b", TILE, TILES), ALU.add))
                wait_full(dve, ("c", b))
                out_of(("c", b), v.tensor_tensor(H[:, bt(b), :], gslots(("c", b), TILE, BTILES), pos_sb[:, bt(b), :], ALU.add))

            def unsplit_and_lower(k, b):
                i = SPLIT_X.index((k, b))
                turn = ("x", k, b)
                wait_full(dve, turn)
                for a in (1, 0):
                    if a == 0:
                        dve.wait_ge(xs_hi, 2 * i + 1)
                    dst, src = XT[:, a, bc(b)], gbanks(turn, HALF, BLOCK)[:, a, :]
                    if k in GAINS:
                        gain, shift = GAINS[k][b]
                        ins = v.tensor_scalar(dst, src, col(gain, a), col(shift, a), ALU.mult, ALU.add)
                    else:
                        ins = v.tensor_copy(dst, src)
                    ins.then_inc(xs_sum, 1)
                wait_emptied(dve, turn)
                v.tensor_tensor(XS[1][:, :, bc(b)], XT[:, :, bc(b)], XS[0][:, :, bc(b)].bitcast(F32),
                                ALU.subtract).then_inc(xs_lo, 1)

            def spread_keys(a, b):
                if a == 0:
                    dve.wait_ge(loaded["const"], 16)
                wait_emptied(dve, ("k", a, b))
                src = KT[:, :, bc(b)].rearrange("p a (i m) -> p a i m", m=SEQ)
                for h in range(POOL_FROM):
                    v.tensor_scalar(KB[:, :, b * IMAGES // 2:(b + 1) * IMAGES // 2, h, :], src,
                                    const_sb[0:HALF, HM_AT + h:HM_AT + h + 1], None, ALU.mult).then_inc(kb_dve, 1)

            def weights(a, b, t):
                n = pair_no(a, b, t)
                dve.wait_ge(scored, n + 1)
                s = R[0:ROWS, n % 2, 0:HEADS * SEQ].rearrange("p (h m) -> p h m", m=SEQ)
                link(v.tensor_reduce(mx[:, n % 2, :], s, AX.X, ALU.max))
                dve.wait_ge(turned, n - 1)
                v.tensor_tensor(P[:, n % 2, :, :], s, mx[:, n % 2, :].unsqueeze(2).broadcast_to([ROWS, HEADS, SEQ]),
                                ALU.subtract).then_inc(shifted, 1)

            def normalise_mixed(a, b, t):
                n = pair_no(a, b, t)
                dve.wait_ge(mixed, n + 1)
                o = R[0:ROWS, 3, 0:GROUPS * GW].rearrange("p (g w) -> p g w", w=GW)
                link(v.reciprocal(rden[:, n % 2, :, :], o[:, :, GV:GW]))
                if t == 0 and n > 0:
                    wait_full(dve, ("O", (0, 1, 3)[(n - 1) // PAIRS], (n - 1) % PAIRS // BPAIRS))
                v.tensor_tensor(O[:, t, :].rearrange("p (g s d) -> p g s d", g=GROUPS, s=GROUP),
                                o[:, :, 0:GV].rearrange("p g (s d) -> p g s d", s=GROUP),
                                rden[:, n % 2, :, :].unsqueeze(3).broadcast_to([ROWS, GROUPS, GROUP, HEAD]),
                                ALU.mult).then_inc(o_ready, 1)

            def add_projection(a, b):
                turn = ("p", a, b)
                wait_full(dve, turn)
                wait_resid(f"A{a}", b)
                out_of(turn, v.tensor_tensor(Y[:, bt(b), :], gslots(turn, TILE, BTILES), RB[:, bt(b), :], ALU.add))

            def hidden_lower(rnd, b, i):
                n = HIDDEN_NO["h", rnd, b, i]
                dve.wait_ge(hid_hi, n + 1)
                tmp = hid_tmp[:, n % 2, :]
                hi, lo = [p[:, 2 * i:2 * i + 2, :].rearrange("p u t -> p (u t)") for p in hid[HID_AT[rnd, b]]]
                if (rnd, b) in BRANCH:
                    j = BRANCH[rnd, b]
                    v.scalar_tensor_tensor(out=lo, in0=tmp, scalar=gum[:, j:j + 1], in1=hi.bitcast(F32), op0=ALU.mult,
                                           op1=ALU.subtract).then_inc(hid_lo, 1)
                else:
                    v.tensor_tensor(lo, tmp, hi.bitcast(F32), ALU.subtract).then_inc(hid_lo, 1)

            def weight_upper(r, i):
                dve.wait_ge(raw_loaded[i], 16 * (r + 1))
                wait_slot_free(dve, r, i)
                v.tensor_copy(w_parts[r % 2][i][0][:], raw[i][:]).then_inc(ws_hi, 1)

            def second_sum(rnd, b):
                no = SECOND_NO["s", rnd, b]
                width = WIDTH.get(rnd, DIM)
                norm = NORM_BEHIND.get((rnd, b))
                for i in range(BTILES):
                    t = b * BTILES + i
                    if i == 2 and norm:
                        dve.wait_ge(rfree, BTILES * no + 2)
                        row_statistics(RB if norm == "b" else Y, range(t - 2, t))
                    ps = R_slots[0:TILE, 2 * BANK * b + SLOT * i:2 * BANK * b + SLOT * i + width]
                    if i % 2 == 0:
                        dve.wait_ge(rfull, BTILES * no + min(i + 2, BTILES))
                    if rnd in ("M", "F"):
                        if i == 0:
                            wait_resid(rnd, b)
                        ins = v.tensor_tensor(Y[:, t, :], ps, RB[:, t, :], ALU.add)
                    elif rnd in WIDTH:
                        if i == 0:
                            dve.wait_ge(rfree, BTILES * no)
                        ins = v.tensor_tensor(Y[:, t, 0:width], ps, Y[:, t, 0:width], ALU.add)
                    else:
                        e = int(rnd[1])
                        if i == 0:
                            if e == 0:
                                wait_resid("E", b)
                            else:
                                dve.wait_ge(rfree, BTILES * (SECOND_NO["s", f"E{e - 1}", b] + 1))
                            if e == 1:
                                wait_emptied(dve, ("cb", b))
                        ins = v.scalar_tensor_tensor(out=RB[:, t, :], in0=ps, scalar=comb[:, t, e:e + 1],
                                                     in1=RB[:, t, :], op0=ALU.mult, op1=ALU.add)
                    ins.then_inc(rfree, 1)

            EE = EXPERTS * EXPERTS

            def logits(b):
                turn = ("gate", b)
                wait_full(dve, turn)
                out_of(turn, v.tensor_tensor(
                    L[:, bt(b), :], gbanks(turn, TILE, BTILES * EXPERTS)[:, 0, :].rearrange("p (t e) -> p t e", e=EXPERTS),
                    brows_sb[0:TILE, GATE_AT:GATE_AT + EXPERTS].unsqueeze(1).broadcast_to([TILE, BTILES, EXPERTS]), ALU.add))

            def rank():
                wait_emptied(dve, ("gate", 0))
                wait_emptied(dve, ("gate", 1))
                link(v.tensor_reduce(lm[:, 0, :], L[:], AX.X, ALU.max))
                v.tensor_tensor(LX[:], L[:], lm[:, 0, :].unsqueeze(2).broadcast_to([TILE, TILES, EXPERTS]),
                                ALU.subtract).then_inc(logit_max, 1)
                mine = L[:].unsqueeze(3).broadcast_to([TILE, TILES, EXPERTS, EXPERTS])
                other = L[:].unsqueeze(2).broadcast_to([TILE, TILES, EXPERTS, EXPERTS])
                for m, op, at in ((gtm, ALU.is_gt, GT_AT), (gem, ALU.is_ge, GE_AT)):
                    link(v.tensor_tensor(m[:].rearrange("p t (e f) -> p t e f", e=EXPERTS), other, mine, op))
                    link(v.tensor_tensor(m[:], m[:], const_sb[0:TILE, at:at + EE].unsqueeze(1)
                                         .broadcast_to([TILE, TILES, EE]), ALU.mult))
                link(v.tensor_tensor(gtm[:], gtm[:], gem[:], ALU.add))
                link(v.tensor_reduce(L[:], gtm[:].rearrange("p t (e f) -> p t e f", e=EXPERTS), AX.X, ALU.add))
                link(v.tensor_scalar(L[:], L[:], 1.5, None, ALU.is_lt))

            def combine_weights():
                dve.wait_ge(logit_exp, 1)
                link(v.tensor_tensor(LE[:], LE[:], L[:], ALU.mult))
                link(v.tensor_reduce(lm[:, 1, :], LE[:], AX.X, ALU.add))
                link(v.reciprocal(lm[:, 1, :], lm[:, 1, :]))
                v.tensor_tensor(comb[:], LE[:], lm[:, 1, :].unsqueeze(2).broadcast_to([TILE, TILES, EXPERTS]),
                                ALU.mult).then_inc(comb_ready, 1)
                dve.wait_ge(comb_ready, 1)

            def single_softmax(b):
                wait_full(dve, ("s2", b))
                pairs = slice(b * BPAIRS, (b + 1) * BPAIRS)
                p = P1[b]
                out_of(("s2", b), v.tensor_tensor(
                    p, gbanks(("s2", b), PAIR, BLOCK)[:, 0, :].rearrange("p (t m) -> p t m", m=PAIR),
                    amask.unsqueeze(1).broadcast_to([PAIR, BPAIRS, PAIR]), ALU.add))
                wait_emptied(dve, ("s2", b))
                link(v.tensor_reduce(st1[:, 0, pairs], p, AX.X, ALU.max))
                v.tensor_tensor(p, p, st1[:, 0, pairs].unsqueeze(2).broadcast_to([PAIR, BPAIRS, PAIR]),
                                ALU.subtract).then_inc(single, 1)
                dve.wait_ge(single_exp, b + 1)
                link(v.tensor_reduce(st1[:, 1, pairs], p, AX.X, ALU.add))
                link(v.reciprocal(st1[:, 2, pairs], st1[:, 1, pairs]))
                v.tensor_tensor(p, p, st1[:, 2, pairs].unsqueeze(2).broadcast_to([PAIR, BPAIRS, PAIR]),
                                ALU.mult).then_inc(single, 1)

            v.memset(QT[:, 0, :], 0.0).then_inc(warm_set, 1)
            v.memset(R[32:64, 0:2, :], 1.0).then_inc(pad_set, 1)
            v.memset(R[32:64, 3, :], 1.0).then_inc(pad_set, 1)
            for kind, *at in VECTOR_ORDER:
                if kind == "c":
                    patch_rows(*at)
                elif kind == "x":
                    if tuple(at) in SPLIT_X:
                        unsplit_and_lower(*at)
                    if tuple(at) == (5, 0):
                        v.memset(R[32:64, 3, :], 1.0).then_inc(pad_set, 1)
                elif kind == "k" and at[0] != 2:
                    spread_keys(*at)
                elif kind == "S" and at[0] > 0:
                    weights(*at)
                elif kind == "W":
                    normalise_mixed(*at)
                elif kind == "p":
                    add_projection(*at)
                elif kind == "st":
                    statistics(*at)
                elif kind == "n":
                    normalise(*at)
                elif kind == "nh":
                    normalise(*at, residual=True)
                elif kind == "h":
                    hidden_lower(*at)
                elif kind == "ws":
                    weight_upper(*at)
                elif kind == "s":
                    second_sum(*at)
                elif kind == "gate":
                    logits(*at)
                    if at[0] == 1:
                        rank()
                elif kind == "comb":
                    combine_weights()
                elif kind == "cb":
                    b = at[0]
                    dve.wait_ge(rfree, BTILES * (SECOND_NO["s", "E0", b] + 1))
                    wait_full(dve, ("cb", b))
                    out_of(("cb", b), v.tensor_tensor(RB[:, bt(b), :], gslots(("cb", b), TILE, BTILES), RB[:, bt(b), :], ALU.add))
                elif kind == "s2":
                    single_softmax(*at)

        @block.gpsimd
        def _(pool):
            g = nc.gpsimd
            steps = [0]

            def link(ins):
                ins.then_inc(pool_step, 1)
                steps[0] += 1
                pool.wait_ge(pool_step, steps[0])

            def residual(stage, b):
                def add(first, second):
                    return g.tensor_tensor(RB[:, bt(b), :], first[:, bt(b), :], second, ALU.add)

                def small(i):
                    return browss[0:TILE, i, :].unsqueeze(1).broadcast_to([TILE, BTILES, DIM])

                if stage == "A0":
                    wait_emptied(pool, ("c", b))
                    ins = add(H, row("A0_bp", TILE, BTILES))
                elif stage == "A1":
                    pool.wait_ge(normed, NORMED["a", b])
                    ins = add(H, row("A1_bp", TILE, BTILES))
                elif stage == "M":
                    wait_emptied(pool, ("p", 1, b))
                    ins = add(Y, row("mlp_b2", TILE, BTILES))
                elif stage == "E":
                    pool.wait_ge(rfree, BTILES * (SECOND_NO["s", "M", b] + 1))
                    ins = add(Y, H[:, bt(b), :])
                elif stage == "A2":
                    pool.wait_ge(normed, NORMED["b", b])
                    ins = add(H, row("A2_bv", TILE, BTILES))
                elif stage == "A3":
                    pool.wait_ge(normed, NORMED["c", b])
                    ins = add(H, row("A3_bp", TILE, BTILES) if b == 0 else small(0))
                else:
                    wait_emptied(pool, ("p", 3, b))
                    link(add(Y, H[:, bt(b), :]))
                    ins = add(RB, row("fc2_b", TILE, BTILES) if b == 0 else small(1))
                ins.then_inc(resid, 1)

            def spread_keys(a, b):
                wait_emptied(pool, ("k", a, b))
                src = KT[:, :, bc(b)].rearrange("p a (i m) -> p a i m", m=SEQ)
                for h in range(POOL_FROM, HHEADS):
                    g.tensor_scalar(KB[:, :, b * IMAGES // 2:(b + 1) * IMAGES // 2, h, :], src,
                                    const_sb[0:HALF, HM_AT + h:HM_AT + h + 1], None, ALU.mult).then_inc(kb_pool, 1)

            def inverse_deviation(norm, b):
                n = NORMS[norm]
                pool.wait_ge(stats, NORM_NO[norm, b] + 1)
                g.tensor_tensor(rs[:, 0:n, bt(b)], shifted_var[:, 0:n, bt(b)], mhalf[:, 0:n, :], ALU.pow).then_inc(rstd, 1)

            def weight_lower(r, i):
                pool.wait_ge(ws_hi, SPLIT_NO["ws", r, i] + 1)
                hi, lo = w_parts[r % 2][i]
                g.tensor_tensor(lo[:], raw[i][:], hi[:].bitcast(F32), ALU.subtract).then_inc(ws_lo, 1)

            def set_ones():
                ones = vmask[:, :, GV:GW].unsqueeze(1).broadcast_to([GK, IMAGES, GROUPS, GROUP])
                g.tensor_copy(V[:, :, :, GV:GW], ones).then_inc(ones_set, 1)

            def branch_sums():
                link(g.tensor_copy(gsum[:, 0:1], gum[:, 0:1]))
                link(g.tensor_tensor(gsum[:, 1:2], gsum[:, 0:1], gum[:, 1:2], ALU.add))
                link(g.tensor_tensor(gsum[:, 2:3], gsum[:, 1:2], gum[:, 2:3], ALU.add))
                c1, c2 = KEEP[2], KEEP[1]
                link(g.tensor_copy(gcol[0:c1, :], gsum[0:c1, 2:3]))
                link(g.tensor_copy(gcol[c1:HALF, :], gsum[c1:HALF, 1:2]))
                pool.wait_ge(loaded["proj3"], 16)
                w = proj_sb[3]
                for a, lo, hi, s in ((0, 0, c1, gcol[:, 0:1]), (0, c1, c2, gsum[0:HALF, 1:2]),
                                     (0, c2, DIM, gsum[0:HALF, 0:1]), (1, 0, DIM, gsum[0:HALF, 0:1])):
                    g.tensor_scalar(proj3s_sb[:, a, lo:hi], w[:, a, lo:hi], s, None, ALU.mult).then_inc(eff, 1)
                for i, name in enumerate(("A3_bp", "fc2_b")):
                    r = BROWS.index(name) * DIM
                    for lo, hi, k in ((0, c1, 2), (c1, c2, 1), (c2, DIM, 0)):
                        link(g.tensor_scalar(browss[:, i, lo:hi], brows_sb[:, r + lo:r + hi], gsum[:, k:k + 1], None,
                                             ALU.mult))

            link(g.memset(mhalf[:], -0.5))
            pool.wait_ge(loaded["const"], 16)
            pool.wait_ge(loaded["brows"], 16)
            for piece in ORDER:
                kind, *at = piece
                if kind == "p" and at[0] in NORM_OF:
                    inverse_deviation(NORM_OF[at[0]], at[1])
                elif kind == "s" and tuple(at) in NORM_BEHIND:
                    inverse_deviation(NORM_BEHIND[tuple(at)], at[1])
                elif kind == "k" and at[0] != 2:
                    spread_keys(*at)
                elif kind == "ws":
                    weight_lower(*at)
                elif piece == ("z2", 1):
                    wait_full(pool, piece)
                    set_ones()
                if piece in RESIDUAL_AT:
                    residual(*RESIDUAL_AT[piece])
                if piece == ("c", 1):
                    wait_emptied(pool, ("c", 1))
                    set_ones()
                if kind == "branches":
                    branch_sums()


HID_AT = {(r, b): b for r in ROUNDS for b in range(2)}
HID_AT["V1", 1], HID_AT["V2", 1] = 0, 1
BRANCH = {("F", 1): 0, ("V1", 1): 1, ("V2", 1): 2}


def _constants():
    c = np.zeros((128, NCONST), np.float32)
    c[:, ID_AT:ID_AT + 128] = np.eye(128)
    for p in range(HALF):
        c[p, HM_AT + p // HEAD] = 1
    for p in range(GK):
        for g in range(GROUPS):
            at = VM_AT + g * GW
            s = p // SEQ
            c[p, at + s * HEAD:at + (s + 1) * HEAD] = 1
            c[p, at + GV + s] = 1
    for p in range(PAIR):
        for m in range(PAIR):
            c[p, AM_AT + m] = 0 if p // SEQ == m // SEQ else -1e30
    for e in range(EXPERTS):
        for f in range(EXPERTS):
            c[:, GT_AT + e * EXPERTS + f] = f > e
            c[:, GE_AT + e * EXPERTS + f] = f < e
    return c


def _position_ids(n, side=32):
    boundaries = np.arange(1.0 / side, 1.0, 1.0 / side, dtype=np.float32)
    frac = np.arange(0.0, 1.0 - 1e-06, 1.0 / n, dtype=np.float32)
    at = np.searchsorted(boundaries, frac, side="right")
    return (at[:, None] * side + at).reshape(-1)


def kernel(**inputs):
    import concourse.bacc as _bacc
    from concourse.bass_utils import run_bass_kernel_spmd as _run

    a = {k: np.asarray(v) for k, v in inputs.items()}

    def channels(w):
        return w.reshape(2, HALF, -1).transpose(1, 0, 2)

    def hidden(w):
        return w.reshape(HK, 128, -1).transpose(1, 0, 2)

    x = a["x"].reshape(IMAGES, IN_CH, GRID, PATCH, GRID, PATCH).transpose(1, 3, 5, 0, 2, 4)
    x = x.reshape(PATCH_K, 128, 2, BTILES, TILE).transpose(1, 2, 3, 0, 4)
    conv = a["L0_tok_conv_w"].reshape(DIM, PATCH_K, 128).transpose(2, 1, 0)
    pos = a["L0_tok_pos_table"][_position_ids(GRID)]
    pos = np.concatenate([pos] * IMAGES).reshape(TILES, TILE, DIM).transpose(1, 0, 2)
    qb, ib = a["L0_attn_b_qkv"], a["L0_ffn_in_b"]
    cols = [qb[0:DIM], qb[DIM:2 * DIM], qb[2 * DIM:], a["L0_ffn_ln1_g"], a["L0_ffn_ln1_b"], ib[0:DIM], ib[DIM:2 * DIM],
            ib[2 * DIM:], a["L0_ffn_ln2_g"], a["L0_ffn_ln2_b"], a["L1_attn_bq"], a["L1_attn_bk"]]
    cols += [a["L1_ffn_" + n] for n in ("n1l_g", "n1l_b", "n1s_g", "n1s_b", "n2l_g", "n2l_b", "n2s_g", "n2s_b")]
    cols = np.stack(cols).reshape(len(COLS), 2, HALF).transpose(2, 0, 1)
    hcols = np.concatenate([a["L0_ffn_mlp_b1"][None], a["L0_ffn_exp_b1"], a["L1_ffn_b_fc1"][None]])
    hcols = hcols.reshape(len(HCOLS), HK, 128).transpose(2, 0, 1)
    brows = np.concatenate([a["L0_tok_conv_b"], a["L0_attn_b_proj"], a["L0_ffn_out_b"], a["L0_ffn_mlp_b2"],
                            a["L1_attn_bv"], a["L1_ffn_b_proj"], a["L1_ffn_b_fc2"], a["L0_ffn_gate_b"],
                            a["L1_ffn_gumbel_weights"]])
    ins = {
        "x": x, "conv_w": conv, "pos": pos, "qkv0": channels(a["L0_attn_w_qkv"]), "proj0": channels(a["L0_attn_w_proj"]),
        "inw": channels(a["L0_ffn_in_w"].T), "outw": channels(a["L0_ffn_out_w"].T),
        "mw1": channels(a["L0_ffn_mlp_w1"]), "mw2": hidden(a["L0_ffn_mlp_w2"]),
        "ew1": a["L0_ffn_exp_w1"].reshape(EXPERTS, 2, HALF, HIDDEN).transpose(2, 0, 1, 3),
        "ew2": a["L0_ffn_exp_w2"].reshape(EXPERTS, HK, 128, DIM).transpose(2, 0, 1, 3), "eb2": a["L0_ffn_exp_b2"],
        "gw": channels(a["L0_ffn_gate_w"].T),
        "qkv2": channels(np.concatenate([a["L1_attn_Wq"].T, a["L1_attn_Wk"].T, a["L1_attn_Wv"].T], axis=1)),
        "qkv3": channels(a["L1_ffn_w_qkv"]), "proj3": channels(a["L1_ffn_w_proj"]),
        "fw1": channels(a["L1_ffn_w_fc1"]), "fw2": hidden(a["L1_ffn_w_fc2"]),
        "cols": cols, "hcols": hcols, "brows": brows, "const": _constants(),
    }
    nc = _bacc.Bacc("TRN2", target_bir_lowering=False, num_devices=1)
    arrays, args = {}, []
    for name, v in ins.items():
        v = np.ascontiguousarray(v)
        arrays["in_" + name] = v
        args.append(nc.dram_tensor("in_" + name, v.shape, mybir.dt.from_np(v.dtype), kind="ExternalInput").ap())
    res = nc.dram_tensor("out_dram", (TOKENS, DIM), F32, kind="ExternalOutput").ap()
    tower(nc, out=res, **dict(zip(ins, args)))
    r = _run(nc, [arrays], core_ids=[0])
    return r.results[0]["out_dram"].reshape(IMAGES, SEQ, DIM)
```

```python
import numpy as np
import concourse.bass as bass
from concourse import mybir
from contextlib import ExitStack

F32 = mybir.dt.float32
F32R = mybir.dt.float32r
ALU = mybir.AluOpType
ACT = mybir.ActivationFunctionType
AX = mybir.AxisListType

IMAGES, IN_CH, SIDE_PX, PATCH = 16, 3, 96, 16
GRID = SIDE_PX // PATCH
SEQ = GRID * GRID
TOKENS = IMAGES * SEQ
DIM, HEADS, HIDDEN, EXPERTS = 192, 12, 768, 4
HEAD = DIM // HEADS
PATCH_K = IN_CH * PATCH * PATCH // 128
HALF = DIM // 2
TILE = 96
TILES = TOKENS // TILE
BLOCK = TOKENS // 2
BTILES = TILES // 2
HK = HIDDEN // 128
PAIRS = IMAGES // 2
BPAIRS = PAIRS // 2
PAIR = 2 * SEQ
SECOND = 64
ROWS = SECOND + SEQ
GROUP = 3
GROUPS = HEADS // GROUP
GK = GROUP * SEQ
GV = GROUP * HEAD
GW = GV + GROUP
HHEADS = HEADS // 2
POOL_FROM = 5
EPS = 1e-5
WARM = 4
BANK = 512
SLOT = 256
KEEP = (DIM, DIM // 2, DIM // 3)

COLS = ["A0_bq", "A0_bk", "A0_bv", "ln1_g", "ln1_b", "A1_bq", "A1_bk", "A1_bv", "ln2_g", "ln2_b",
        "A2_bq", "A2_bk", "n1l_g", "n1l_b", "n1s_g", "n1s_b", "n2l_g", "n2l_b", "n2s_g", "n2s_b"]
HCOLS = ["M", "E0", "E1", "E2", "E3", "F"]
BROWS = ["conv_b", "A0_bp", "A1_bp", "mlp_b2", "A2_bv", "A3_bp", "fc2_b"]
GATE_AT = len(BROWS) * DIM
GUM_AT = GATE_AT + EXPERTS
NROWS = GUM_AT + 3
ID_AT = 0
HM_AT = ID_AT + 128
VM_AT = HM_AT + HHEADS
AM_AT = VM_AT + GROUPS * GW
GT_AT = AM_AT + PAIR
GE_AT = GT_AT + EXPERTS * EXPERTS
NCONST = GE_AT + EXPERTS * EXPERTS

MHA = {0: 0, 1: 1, 3: 2}
ROUNDS = ["M", "E0", "E1", "E2", "E3", "F"]
X_OF = {0: 0, 1: 1, 2: 4, 3: 5}
NORM_OF = {0: "a", 2: "c", 3: "n2"}


NORM_BEHIND = {("M", 0): "ln2", ("M", 1): "ln2", ("E3", 0): "b", ("E3", 1): "b", ("F", 0): "d", ("V2", 1): "d"}


def _front(a, b):
    return [("x", X_OF[a], b), ("k", a, b), ("q", a, b), ("vt", a, b)]


def _attend(a, b, before, norm, split, then):
    s, e, t, w = [[(n, a, b, i) for i in range(BPAIRS)] for n in "SETW"]
    v = [("v", a, b, j) for j in range(2)]
    out = [] if not before else [("z2", before[1])] if before[0] == 2 else [("O", *before)]
    o = [s[0]] + out + [e[0], s[1], e[1]] + ([("p", *before)] if before else [])
    if then[-1][0] == "h" and then[0] == ("x", 2, 0):
        return o + [t[0], then[0], s[2], v[0], e[2], t[1], s[3], v[1], e[3], w[0], then[2], t[2], w[1]] + split + [
            t[3], w[2], w[3], then[3]]
    o += [t[0], s[2], v[0], e[2]] + norm + [t[1], s[3]]
    if then[-1][0] == "h":
        return o + [w[0], then[0], e[3], t[2], v[1], w[1]] + split + [t[3], ("table", "gelu"), w[2], then[2], w[3], then[3]]
    return o + [w[0], then[0], e[3], t[2], w[1], v[1]] + _residual_norm(norm) + [then[1], t[3], then[2], w[2]] + split + [then[3], w[3]]


def _residual_norm(norm):
    return [("nh",) + n[1:] for n in norm if n[1] in ("a", "c")]


def _hidden(rnd, b):
    return [("h", rnd, b, i) for i in range(HK // 2)]


def _order():
    o = [("qs", 0), ("c", 0), ("c", 1), ("x", 0, 0), ("x", 0, 1), ("k", 0, 0), ("q", 0, 0), ("vt", 0, 0)]
    o += _attend(0, 0, (), [], [("ws", 0, 0), ("qs", 1)], [("nop",)] + _front(0, 1)[1:])
    o += _attend(0, 1, (0, 0), [("n", "a", 0)], [("ws", 0, 1)], _front(1, 0))
    o += _attend(1, 0, (0, 1), [("n", "a", 1)], [("ws", 1, 0)], _front(1, 1))
    h = _hidden("M", 0)
    o += _attend(1, 1, (1, 0), [], [("ws", 1, 1)], [("x", 2, 0), ("nop",)] + h[0:2])
    o += [("O", 1, 1), h[2], ("p", 1, 1), ("x", 2, 1), ("s", "M", 0)]
    h = _hidden("M", 1)
    o += [("n", "ln2", 0), h[0], h[1], ("x", 3, 0), h[2], ("gate", 0), ("ws", 2, 0)]
    h = _hidden("E0", 0)
    o += [h[0], ("s", "M", 1), ("n", "ln2", 1), h[1], h[2], ("x", 3, 1), ("s", "E0", 0), ("gate", 1), ("ws", 2, 1)]
    h = _hidden("E0", 1)
    o += h[0:2] + [("comb",), h[2], ("ws", 3, 0)]
    for e in range(1, EXPERTS):
        if e > 1:
            o += [("s", f"E{e - 1}", 0)]
        o += _hidden(f"E{e}", 0) + [("s", f"E{e - 1}", 1)]
        if e + 2 < len(ROUNDS):
            o += [("ws", e + 2, 1)]
        h = _hidden(f"E{e}", 1)
        if e == 3:
            o += [("s", "E3", 0), ("n", "b", 0)] + h[0:2] + [("x", 4, 0), h[2], ("qs", 3)]
        elif e == 1:
            o += [("ct",), h[0], ("cb", 0), h[1], ("cb", 1), h[2], ("branches",)]
        else:
            o += h
        if e + 3 < len(ROUNDS):
            o += [("ws", e + 3, 0)]
    o += [("k", 2, 0), ("q", 2, 0), ("table", "exp"), ("s2", 0), ("e2", 0), ("s", "E3", 1), ("t2", 0), ("z2", 0),
          ("n", "b", 1), ("x", 4, 1), ("p", 2, 0), ("k", 2, 1), ("q", 2, 1), ("n", "c", 0), ("x", 5, 0), ("s2", 1), ("e2", 1)]
    o += _front(3, 0)[1:2] + [("nh", "c", 0)] + _front(3, 0)[2:] + [("t2", 1)]
    o += _attend(3, 0, (2, 1), [("n", "c", 1)], [], _front(3, 1))
    h = _hidden("F", 0)
    o += _attend(3, 1, (3, 0), [("n", "n2", 0)], [], [("x", 6, 0), ("nop",)] + h[0:2])
    o += [("O", 3, 1), h[2], ("p", 3, 1), ("n", "n2", 1), ("s", "F", 0), ("x", 6, 1), ("last tile", "F", 0), ("n", "d", 0)]
    o += _hidden("F", 1) + _hidden("V1", 1) + [("s", "F", 1)] + _hidden("V2", 1) + [("s", "V1", 1), ("s", "V2", 1)]
    o += [("n", "d", 1)]
    with_statistics = []
    for p in o:
        with_statistics.append(p)
        if p[0] == "p" and p[1] in NORM_OF:
            with_statistics.append(("st", NORM_OF[p[1]], p[2]))
        elif p[1:] in NORM_BEHIND and p[0] == "s":
            with_statistics.append(("st", NORM_BEHIND[p[1:]], p[2]))
    return with_statistics


ORDER = _order()
SPLIT_X = [p[1:] for p in ORDER if p[0] == "x" and p[1] != X_OF[2]]
BOTH_X = [x for x in SPLIT_X if x[0] in (1, 3, 5, 6)]
SPLIT_A = [p[1] for p in ORDER if p[0] == "qs"]


def _vector_order():
    o = list(ORDER)

    def move(piece, behind):
        o.remove(piece)
        o.insert(o.index(behind) + 1, piece)

    move(("h", "M", 0, 2), ("p", 1, 1))
    move(("h", "F", 0, 2), ("p", 3, 1))
    move(("s", "F", 0), ("h", "V1", 1, 2))
    move(("st", "d", 0), ("s", "F", 0))
    move(("n", "d", 0), ("h", "V2", 1, 2))
    move(("s", "E0", 0), ("comb",))
    move(("h", "M", 0, 0), ("W", 1, 1, 3))
    move(("h", "F", 0, 0), ("W", 3, 1, 3))
    move(("h", "E3", 1, 1), ("x", 4, 0))
    for a in MHA:
        for b in range(2):
            move(("S", a, b, 3), ("W", a, b, 0))
    move(("S", 1, 0, 3), ("x", 1, 1))
    move(("S", 3, 0, 3), ("x", 5, 1))
    return o


def _scalar_order():
    o = list(ORDER)
    h = ("h", "M", 0, 0)
    o.remove(h)
    o.insert(o.index(("T", 1, 1, 3)) + 1, h)
    o.insert(o.index(("T", 1, 1, 2)) + 1, ("table", "gelu"))
    return o


VECTOR_ORDER = _vector_order()
SCALAR_ORDER = _scalar_order()


IDLE = {
    ("gate", 0): 2, ("cb", 0): 2, ("cb", 1): 1, ("x", 1, 0): 3, ("x", 1, 1): 3, ("x", 5, 1): 3, ("k", 1, 0): 2,
    ("k", 1, 1): 2, ("k", 3, 1): 2, ("T", 1, 1, 3): 3, ("W", 1, 1, 3): 3, ("T", 3, 1, 3): 8, ("W", 3, 1, 2): 2,
    ("x", 2, 1): 3, ("x", 3, 0): 2, ("x", 3, 1): 2, ("s", "E0", 0): 8, ("h", "E1", 0, 0): 1, ("s2", 0): 4,
    ("z2", 0): 2, ("x", 4, 1): 2, ("k", 3, 0): 4, ("z2", 1): 1, ("s", "F", 0): 4, ("h", "F", 1, 0): 3,
    ("s", "V1", 1): 1, ("s", "V2", 1): 1, ("h", "V2", 1, 1): 2, ("h", "V1", 1, 0): 2, ("h", "V1", 1, 1): 2,
}


def _emptying(piece):
    kind = piece[0]
    if kind == "x":
        return 0 if piece[1:] in SPLIT_X else 1
    if kind in ("k", "q", "vt", "h"):
        return 2
    if kind == "O":
        return 2
    if kind == "v":
        return GROUP
    return 1 if kind in ("c", "p", "gate", "ct", "cb", "s2", "t2", "z2") else None


GAINS = {1: (("ln1_g", "ln1_b"),) * 2, 3: (("ln2_g", "ln2_b"),) * 2,
         5: (("n1l_g", "n1l_b"), ("n1s_g", "n1s_b")), 6: (("n2l_g", "n2l_b"), ("n2s_g", "n2s_b"))}
TURNS = [p for p in ORDER if _emptying(p) is not None]
TURN = {p: i for i, p in enumerate(TURNS)}
EMPTIED = {}
_sum = [0, 0]
for _i, _p in enumerate(TURNS):
    _sum[_i % 2] += _emptying(_p)
    EMPTIED[_p] = _sum[_i % 2]


def _numbered(kind):
    return {p: i for i, p in enumerate([p for p in ORDER if p[0] == kind])}


HIDDEN_NO, SECOND_NO, SPLIT_NO, VALUES_NO = _numbered("h"), _numbered("s"), _numbered("ws"), _numbered("v")
NORMS = {"a": 2, "ln2": 1, "b": 1, "c": 2, "n2": 1, "d": 1}
LAST_NORM = ("d", 1)
NORM_NO, NORMED_FIRST, NORMED = {}, {}, {}
_at = 0
for _p in [p for p in ORDER if p[0] in ("n", "nh")]:
    _at += BTILES
    NORMED[_p[1:]] = _at
    if _p[0] == "n":
        NORM_NO[_p[1:]] = len(NORM_NO)
        NORMED_FIRST[_p[1:]] = _at
WIDTH = {"V1": KEEP[1], "V2": KEEP[2]}
SECOND_BANKS = {s: 2 * s[2] for s in SECOND_NO}
SECOND_BANKS["s", "V1", 1] = 0
RESIDUAL_AT = {("c", 0): ("A0", 0), ("c", 1): ("A0", 1)}
for _b in range(2):
    RESIDUAL_AT[("nh", "a", _b)] = ("A1", _b)
    RESIDUAL_AT[("p", 1, _b)] = ("M", _b)
    RESIDUAL_AT[("n", "ln2", _b)] = ("E", _b)
    RESIDUAL_AT[("n", "b", _b)] = ("A2", _b)
    RESIDUAL_AT[("nh", "c", _b)] = ("A3", _b)
    RESIDUAL_AT[("n", "n2", _b)] = ("F", _b)
RESIDUAL_NO = {RESIDUAL_AT[p]: i for i, p in enumerate([p for p in ORDER if p in RESIDUAL_AT])}


def tower(nc, x, conv_w, pos, qkv0, proj0, inw, outw, mw1, mw2, ew1, ew2, eb2, gw, qkv2, qkv3, proj3,
          fw1, fw2, cols, hcols, brows, const, out):
    ctx = ExitStack()
    with ctx:
        def sb(name, shape, dt=F32):
            return ctx.enter_context(nc.sbuf_tensor(name, shape, dt))

        def sem(name):
            return ctx.enter_context(nc.semaphore(name))

        qkv_at = [sb("qkv_even", [HALF, 2, 3 * DIM]), sb("qkv_odd", [HALF, 2, 3 * DIM])]
        qkv_sb = {a: qkv_at[a % 2] for a in range(4)}
        proj_sb = {a: sb(f"proj{a}_sb", [HALF, 2, DIM]) for a in (0, 1, 3)}
        proj3s_sb = sb("proj3s_sb", [HALF, 2, DIM])
        raw = [sb("raw_w1", [HALF, 2, HIDDEN]), sb("raw_w2", [128, HK, DIM])]
        w_both = [[sb(f"w1_parts{s}", [HALF, 2, 2, HIDDEN], F32R), sb(f"w2_parts{s}", [128, HK, 2, DIM], F32R)]
                  for s in range(2)]
        w_parts = [[[w[:, :, part, :] for part in range(2)] for w in slot] for slot in w_both]
        eb2_sb = sb("eb2_sb", [EXPERTS, DIM])
        gw_sb = sb("gw_sb", [HALF, 2, EXPERTS])
        cols_sb = sb("cols_sb", [HALF, len(COLS), 2])
        hcols_sb = sb("hcols_sb", [128, len(HCOLS), HK])
        brows_sb = sb("brows_sb", [128, NROWS])
        const_sb = sb("const_sb", [128, NCONST])
        ident = const_sb[:, ID_AT:ID_AT + 128]
        vmask = const_sb[0:GK, VM_AT:VM_AT + GROUPS * GW].rearrange("p (g w) -> p g w", g=GROUPS)
        amask = const_sb[0:PAIR, AM_AT:AM_AT + PAIR]
        gum = brows_sb[:, GUM_AT:GUM_AT + 3]
        gsum = sb("gsum", [128, 3])
        gcol = sb("gcol", [HALF, 1])
        idle = sb("idle", [128, 1])
        browss = sb("browss", [128, 2, DIM])

        keys = sb("keys", [128, 2 * IMAGES * HHEADS * SEQ])
        xp_sb = keys[:, 0:PATCH_K * TOKENS].rearrange("p (b t k m) -> p b t k m", b=2, t=BTILES, k=PATCH_K)
        KB = keys[0:HALF, :].rearrange("p (a i h m) -> p a i h m", a=2, i=IMAGES, h=HHEADS)
        H = sb("H", [TILE, TILES, DIM])
        RB = sb("RB", [TILE, TILES, DIM])
        Y = sb("Y", [TILE, TILES, DIM])
        NRM = sb("NRM", [TILE, TILES, DIM])
        XT = sb("XT", [HALF, 2, TOKENS])
        XS = [sb(f"XT_{part}", [HALF, 2, TOKENS], F32R) for part in ("hi", "lo")]
        VT3 = sb("VT3", [HALF, 2, IMAGES // 2, GROUP * SEQ])
        QT = sb("QT", [HALF, 2, TOKENS])
        KT = sb("KT", [HALF, 2, TOKENS])
        OT = KT
        hid_tmp = sb("hid_tmp", [128, 2, 2 * BLOCK])
        hid = [[sb(f"hid{b}_{part}", [128, HK, BLOCK], F32R) for part in ("hi", "lo")] for b in range(2)]
        values = sb("values", [128, IMAGES * GROUPS * GW])
        V = values[0:GK, :].rearrange("p (i g w) -> p i g w", i=IMAGES, g=GROUPS)
        qkv_parts = {a: [hid[place][part][0:HALF, :, :].rearrange("p k t -> p (k t)")[:, 0:2 * 3 * DIM]
                         .rearrange("p (k n) -> p k n", k=2) for part in range(2)] for a, place in ((0, 1), (1, 0), (3, 0))}
        conv_parts = [w_parts[0][1][part] for part in range(2)]
        patch_parts = [hid[0][part][:, :, :].rearrange("p k t -> p (k t)")
                       .rearrange("p (t k m) -> p t k m", t=BTILES, k=PATCH_K) for part in range(2)]
        conv_sb = values[:, 0:PATCH_K * DIM].rearrange("p (k c) -> p k c", k=PATCH_K)
        pos_sb = values[0:TILE, PATCH_K * DIM:(PATCH_K + TILES) * DIM].rearrange("p (t c) -> p t c", t=TILES)
        XP = values[0:PAIR, 0:PAIRS * DIM].rearrange("p (t c) -> p t c", t=PAIRS)
        P = sb("P", [ROWS, 2, HEADS, SEQ])
        PT = sb("PT", [GK, 2, GROUPS, ROWS])
        O = sb("O", [ROWS, BPAIRS, DIM])
        mx = sb("mx", [ROWS, 2, HEADS])
        rden = sb("rden", [ROWS, 2, GROUPS, GROUP])
        P1 = [NRM[0:PAIR, b * BTILES:(b + 1) * BTILES, :].rearrange("p t c -> p (t c)")[:, 0:BPAIRS * PAIR]
              .rearrange("p (t m) -> p t m", t=BPAIRS) for b in range(2)]
        P1T = PT[0:PAIR, :, :, :].rearrange("p b g r -> p (b g r)")[:, 0:PAIRS * PAIR].rearrange("p (t m) -> p t m", t=PAIRS)
        st1 = sb("st1", [PAIR, 3, PAIRS])
        bst = sb("bst", [TILE, TILES, 6])
        mv = sb("mv", [TILE, TILES, 2])
        shifted_var = sb("shifted_var", [TILE, 2, TILES])
        rs = sb("rs", [TILE, 2, TILES])
        mhalf = sb("mhalf", [TILE, 2, BTILES])
        L = sb("L", [TILE, TILES, EXPERTS])
        LX = sb("LX", [TILE, TILES, EXPERTS])
        LE = sb("LE", [TILE, TILES, EXPERTS])
        lm = sb("lm", [TILE, 2, TILES])
        gtm = sb("gtm", [TILE, TILES, EXPERTS * EXPERTS])
        gem = sb("gem", [TILE, TILES, EXPERTS * EXPERTS])
        comb = sb("comb", [TILE, TILES, EXPERTS])
        combT = QT[0:EXPERTS, 0, :]

        G = [ctx.enter_context(nc.psum_tensor(f"G{i}", [128, 2, BANK], F32)) for i in range(2)]
        R = ctx.enter_context(nc.psum_tensor("R", [128, 4, BANK], F32))
        R_slots = R[:, :, :].rearrange("p b n -> p (b n)")
        h_dram = nc.dram_tensor("h_scratch", [TOKENS, DIM], F32).ap()

        def gslots(turn, parts, n):
            g = G[TURN[turn] % 2][0:parts, :, :].rearrange("p b n -> p (b n)")
            return g.rearrange("p (s c) -> p s c", c=SLOT)[:, 0:n, 0:DIM]

        def gbanks(turn, parts, n):
            return G[TURN[turn] % 2][0:parts, :, 0:n]

        def bt(b):
            return slice(b * BTILES, (b + 1) * BTILES)

        def bc(b):
            return slice(b * BLOCK, (b + 1) * BLOCK)

        def col(name, half):
            return cols_sb[:, COLS.index(name), half:half + 1]

        def row(name, parts, n):
            i = BROWS.index(name)
            return brows_sb[0:parts, i * DIM:(i + 1) * DIM].unsqueeze(1).broadcast_to([parts, n, DIM])

        LOADS = [f"x{t}" for t in range(BTILES + 1)] + ["conv_w0", "conv_w1", "pos", "brows", "const", "cols", "qkv0", "qkv1", "qkv2", "qkv3", "proj0",
                 "proj1", "proj3", "hcols", "gw", "eb2"]
        loaded = {n: sem("loaded_" + n) for n in LOADS}
        raw_loaded = [sem("raw_w1_loaded"), sem("raw_w2_loaded")]
        full = sem("turn_full")
        emptied = [sem("turn_emptied_0"), sem("turn_emptied_1")]
        pad_set = sem("pad_set")
        ones_set = sem("ones_set")
        conv_hi, conv_lo = sem("conv_hi"), sem("conv_lo")
        warm_set = sem("warm_set")
        kb_dve = sem("keys_spread_dve")
        kb_pool = sem("keys_spread_pool")
        scored = sem("scored")
        shifted = sem("shifted")
        probs = sem("probs")
        turned = sem("probs_transposed")
        pt_ready = sem("pt_ready")
        mixed = sem("mixed")
        o_ready = sem("o_ready")
        stats = sem("stats_ready")
        rstd = sem("rstd_ready")
        normed = sem("normed")
        resid = sem("residual_ready")
        xs_hi, xs_lo = sem("x_hi"), sem("x_lo")
        act_step = sem("act_step")
        qs_hi, qs_lo = sem("qkv_hi"), sem("qkv_lo")
        xs_sum = sem("x_unsplit")
        hid_hi, hid_lo = sem("hid_hi"), sem("hid_lo")
        tmp_ready = sem("hid_tmp_ready")
        ws_hi, ws_lo = sem("w_hi"), sem("w_lo")
        rfull = sem("r_full")
        rfree = sem("r_read")
        single = sem("single_steps")
        single_exp = sem("single_exp")
        h_saved = sem("h_saved")
        xp_loaded = [sem("xp_loaded_0"), sem("xp_loaded_1")]
        logit_diff = sem("logit_differences")
        logit_tanh = sem("logit_tanh")
        comb_ready = sem("comb_ready")
        eff = sem("scaled_weights")
        dve_step = sem("dve_step")
        pool_step = sem("pool_step")
        done = sem("out_saved")

        def wait_full(eng, turn):
            eng.wait_ge(full, TURN[turn] + 1)

        def wait_emptied(eng, turn):
            if turn[0] == "x" and turn[1:] in SPLIT_X:
                i = SPLIT_X.index(turn[1:])
                eng.wait_ge(xs_hi, 2 * (i + 1))
                if turn[1:] in BOTH_X:
                    eng.wait_ge(xs_sum, 2 * (BOTH_X.index(turn[1:]) + 1))
                else:
                    eng.wait_ge(xs_lo, i + 1)
                return
            eng.wait_ge(emptied[TURN[turn] % 2], EMPTIED[turn])

        def pair_no(a, b, t):
            return (2 * MHA[a] + b) * BPAIRS + t

        def wait_hid_free(eng, rnd, b):
            n = HIDDEN_NO["h", rnd, b, 0]
            before = [h for h in list(HIDDEN_NO)[:n] if HID_AT[h[1], h[2]] == HID_AT[rnd, b]]
            if before:
                eng.wait_ge(rfull, BTILES * (SECOND_NO["s", before[-1][1], before[-1][2]] + 1))

        def wait_slot_free(eng, r, i):
            if r >= 2 and i == 0:
                wait_full(eng, ("h", ROUNDS[r - 2], 1, HK // 2 - 1))
            elif r >= 2:
                eng.wait_ge(rfull, BTILES * (SECOND_NO["s", ROUNDS[r - 2], 1] + 1))

        block = ctx.enter_context(nc.Block())

        @block.sync
        def _(sp):
            def load(name, dst, src):
                sp.dma_start(dst, src).then_inc(loaded[name], 16)

            def load_raw(i, src):
                if i >= 2:
                    sp.wait_ge(ws_hi, i - 1)
                    sp.wait_ge(ws_lo, i - 1)
                sp.dma_start(raw[i % 2][:], src).then_inc(raw_loaded[i % 2], 16)

            for t in range(BTILES):
                load(f"x{t}", xp_sb[:, 0, t, :, :], x[:, 0, t, :, :])
            load(f"x{BTILES}", xp_sb[:, 1, :, :, :], x[:, 1, :, :, :])
            load("qkv0", qkv_sb[0][:], qkv0)
            load("proj0", proj_sb[0][:], proj0)
            load("qkv1", qkv_sb[1][:], inw)
            load("proj1", proj_sb[1][:], outw)
            load_raw(0, mw1)
            load_raw(1, mw2)
            load("hcols", hcols_sb[:], hcols)
            load("gw", gw_sb[:], gw)
            load("eb2", eb2_sb[:], eb2)
            load("proj3", proj_sb[3][:], proj3)
            load_raw(2, ew1[:, 0, :, :])
            load_raw(3, ew2[:, 0, :, :])
            wait_full(sp, ("vt", 0, 1))
            load("qkv2", qkv_sb[2][:], qkv2)
            load_raw(4, ew1[:, 1, :, :])
            load_raw(5, ew2[:, 1, :, :])
            wait_full(sp, ("vt", 1, 1))
            load("qkv3", qkv_sb[3][:], qkv3)
            for e in range(2, EXPERTS):
                load_raw(2 * e + 2, ew1[:, e, :, :])
                load_raw(2 * e + 3, ew2[:, e, :, :])
            load_raw(2 * EXPERTS + 2, fw1)
            load_raw(2 * EXPERTS + 3, fw2)
            for b in range(2):
                sp.wait_ge(normed, NORMED["b", b])
                sp.dma_start(h_dram.rearrange("(t p) c -> p t c", p=TILE)[:, bt(b), :], H[:, bt(b), :]).then_inc(h_saved, 16)
                sp.wait_ge(h_saved, 16 * (b + 1))
                pairs = slice(b * BPAIRS, (b + 1) * BPAIRS)
                sp.dma_start(XP[:, pairs, :], h_dram.rearrange("(t p) c -> p t c", p=PAIR)[:, pairs, :]).then_inc(xp_loaded[b], 16)
            for lo, hi in ((0, BTILES), (BTILES, BTILES + 2), (BTILES + 2, TILES)):
                sp.wait_ge(normed, NORMED["d", lo // BTILES] - (TILES - hi if lo >= BTILES else 0))
                sp.dma_start(out.rearrange("(t p) c -> p t c", p=TILE)[:, lo:hi, :], H[:, lo:hi, :]).then_inc(done, 16)
            sp.wait_ge(done, 3 * 16)

        @block.tensor
        def _(pe):
            mm, tr = nc.tensor.matmul, nc.tensor.transpose

            def idle(piece, bank):
                for i in range(IDLE.get(piece, 0)):
                    mm(bank[:, 0:128], ident, ident, start=True, stop=True)

            def claim(turn):
                if TURN[turn] >= 2:
                    wait_emptied(pe, TURNS[TURN[turn] - 2])
                idle(turn, G[TURN[turn] % 2][:, 0, :])

            def mm_split(o, w, m, start, stop):
                mm(o, w[0], m[0], start=start, stop=False)
                mm(o, w[0], m[1], start=False, stop=False)
                return mm(o, w[1], m[0], start=False, stop=stop)

            def patches(b):
                if b == 0:
                    pe.wait_ge(loaded["conv_w0"], 16)
                g = gslots(("c", b), TILE, BTILES)
                for t in range(BTILES):
                    if b == 0 or t == 0:
                        pe.wait_ge(loaded[f"x{b * BTILES + t}"], 16)
                    if b == 1:
                        pe.wait_ge(conv_hi, t + 2)
                        pe.wait_ge(conv_lo, t + 2)
                    for k in range(PATCH_K):
                        if b == 0 and t == 0 and k == PATCH_K // 2:
                            pe.wait_ge(loaded["conv_w1"], 16)
                        if b == 0:
                            last = mm(g[:, t, :], xp_sb[:, b, t, k, :], conv_sb[:, k, :],
                                      start=(k == 0), stop=(k == PATCH_K - 1))
                        else:
                            last = mm_split(g[:, t, :], [p[:, t, k, :] for p in patch_parts],
                                            [p[:, k, :] for p in conv_parts], k == 0, k == PATCH_K - 1)
                last.then_inc(full, 1)

            def tokens_to_channels(k, b):
                turn = ("x", k, b)
                src = {0: H, 1: NRM, 2: Y, 3: NRM, 4: H, 5: NRM, 6: NRM}[k]
                claim(turn)
                if k == 0:
                    pe.wait_ge(loaded["const"], 16)
                    wait_emptied(pe, ("c", b))
                elif k == 2:
                    wait_emptied(pe, ("p", 1, b))
                g = gbanks(turn, HALF, BLOCK)
                for t in range(BTILES):
                    if k not in (0, 2):
                        first = NORMED_FIRST[{1: "a", 3: "ln2", 4: "b", 5: "c", 6: "n2"}[k], b]
                        pe.wait_ge(normed, first - BTILES + t + 1)
                    for a in range(2):
                        last = tr(g[:, a, t * TILE:(t + 1) * TILE],
                                  src[:, b * BTILES + t, a * HALF:(a + 1) * HALF], ident[0:TILE, 0:TILE])
                last.then_inc(full, 1)

            def project(n, a, b):
                claim((n, a, b))
                if n == "k":
                    wait_emptied(pe, ("x", X_OF[a], b))
                    if a == 2:
                        pe.wait_ge(loaded[f"qkv{a}"], 16)
                    else:
                        pe.wait_ge(xs_lo, SPLIT_X.index((X_OF[a], b)) + 1)
                        pe.wait_ge(qs_hi, SPLIT_A.index(a) + 1)
                        pe.wait_ge(qs_lo, SPLIT_A.index(a) + 1)
                g = gbanks((n, a, b), HALF, BLOCK)
                at = {"q": 0, "k": DIM, "vt": 2 * DIM}[n]
                for i in range(2):
                    out_channels = slice(at + i * HALF, at + (i + 1) * HALF)
                    for k in range(2):
                        if a == 2:
                            last = mm(g[:, i, :], qkv_sb[a][:, k, out_channels], XT[:, k, bc(b)],
                                      start=(k == 0), stop=(k == 1))
                        else:
                            last = mm_split(g[:, i, :], [p[:, k, out_channels] for p in qkv_parts[a]],
                                            [p[:, k, bc(b)] for p in XS], k == 0, k == 1)
                last.then_inc(full, 1)

            def project_out(a, b):
                turn = ("p", a, b)
                w = qkv_sb[a][:, :, 2 * DIM:3 * DIM] if a == 2 else proj_sb[a]
                if a == 3 and b == 1:
                    w = proj3s_sb
                    pe.wait_ge(eff, 4)
                if a != 2:
                    pe.wait_ge(loaded[f"proj{a}"], 16)
                claim(turn)
                wait_emptied(pe, ("z2", b) if a == 2 else ("O", a, b))
                g = gslots(turn, TILE, BTILES)
                for t in range(BTILES):
                    at = b * BLOCK + t * TILE
                    for k in range(2):
                        last = mm(g[:, t, :], OT[:, k, at:at + TILE], w[:, k, 0:DIM], start=(k == 0), stop=(k == 1))
                last.then_inc(full, 1)

            def values_of(a, b, j):
                turn = ("v", a, b, j)
                claim(turn)
                wait_emptied(pe, ("vt", a, b))
                g = gslots(turn, GK, 4)
                for i in range(4):
                    for k in range(2):
                        last = tr(g[:, i, k * HALF:(k + 1) * HALF], VT3[:, k, 4 * j + i, :], ident[0:HALF, 0:HALF])
                last.then_inc(full, 1)

            def scores(a, b, t):
                n = pair_no(a, b, t)
                if t == 0:
                    wait_emptied(pe, ("q", a, b))
                    pe.wait_ge(kb_dve, POOL_FROM * (2 * MHA[a] + b + 1))
                    pe.wait_ge(kb_pool, (HHEADS - POOL_FROM) * (2 * MHA[a] + b + 1))
                if n == 0:
                    pe.wait_ge(pad_set, 2)
                if n >= 2:
                    pe.wait_ge(shifted, n - 1)
                for s in range(2):
                    i = 2 * (b * BPAIRS + t) + s
                    for k in range(2):
                        last = mm(R[SECOND * s:SECOND * s + SEQ, n % 2, k * HHEADS * SEQ:(k + 1) * HHEADS * SEQ],
                                  QT[:, k, i * SEQ:(i + 1) * SEQ],
                                  KB[:, k, i, :, :].rearrange("p h m -> p (h m)"), start=True, stop=True)
                last.then_inc(scored, 1)

            def transpose_probs(a, b, t):
                n = pair_no(a, b, t)
                if ("T", a, b, t) in IDLE:
                    pe.wait_ge(shifted, n)
                    idle(("T", a, b, t), R[:, (n + 1) % 2, :])
                if n >= 1:
                    pe.wait_ge(pt_ready, n)
                if a == 0:
                    pe.wait_ge(shifted, n + 1)
                else:
                    pe.wait_ge(probs, n + 1 - PAIRS)
                for g in range(GROUPS):
                    last = tr(R[0:GK, 2, g * ROWS:(g + 1) * ROWS],
                              P[:, n % 2, g * GROUP:(g + 1) * GROUP, :].rearrange("p h m -> p (h m)"),
                              ident[0:ROWS, 0:ROWS])
                last.then_inc(turned, 1)

            def mix(a, b, t):
                n = pair_no(a, b, t)
                idle(("W", a, b, t), R[:, 0, :])
                pe.wait_ge(pt_ready, n + 1)
                if t % 2 == 0:
                    wait_emptied(pe, ("v", a, b, t // 2))
                if t == 0:
                    pe.wait_ge(ones_set, 2 if a == 3 else 1)
                    pe.wait_ge(pad_set, 3 if a == 3 else 2)
                if n >= 1:
                    pe.wait_ge(o_ready, n)
                for s in range(2):
                    for g in range(GROUPS):
                        last = mm(R[SECOND * s:SECOND * s + SEQ, 3, g * GW:(g + 1) * GW],
                                  PT[:, n % 2, g, SECOND * s:SECOND * s + SEQ],
                                  V[:, 2 * (b * BPAIRS + t) + s, g, :], start=True, stop=True)
                last.then_inc(mixed, 1)

            def transpose_out(a, b):
                turn = ("O", a, b)
                claim(turn)
                pe.wait_ge(o_ready, pair_no(a, b, BPAIRS))
                g = gbanks(turn, HALF, BPAIRS * 2 * SECOND)
                for t in range(BPAIRS):
                    for k in range(2):
                        last = tr(g[:, k, 2 * SECOND * t:2 * SECOND * t + ROWS], O[:, t, k * HALF:(k + 1) * HALF], ident[0:ROWS, 0:ROWS])
                last.then_inc(full, 1)

            def hidden(rnd, b, i):
                r = ROUNDS.index("F" if rnd in WIDTH else rnd)
                turn = ("h", rnd, b, i)
                claim(turn)
                if i == 0:
                    pe.wait_ge(ws_hi, 2 * r + 1)
                    pe.wait_ge(ws_lo, 2 * r + 1)
                    n = SPLIT_X.index(({"M": 2, "F": 6, "V1": 6, "V2": 6}.get(rnd, 3), b)) + 1
                    pe.wait_ge(xs_hi, 2 * n)
                    pe.wait_ge(xs_lo, n)
                g = gbanks(turn, 128, BLOCK)
                w = w_parts[r % 2][0]
                keep = WIDTH.get(rnd, HALF)
                for u in range(2):
                    at = (2 * i + u) * 128
                    for k in range(1 if rnd in WIDTH else 2):
                        last = mm_split(g[:, u, :], [p[0:keep, k, at:at + 128] for p in w],
                                        [p[0:keep, k, bc(b)] for p in XS], k == 0, k == 1 or rnd in WIDTH)
                last.then_inc(full, 1)

            def second(rnd, b, last_tile=False):
                r = ROUNDS.index("F" if rnd in WIDTH else rnd)
                no = SECOND_NO["s", rnd, b]
                first_bank = SECOND_BANKS["s", rnd, b]
                before = [s for s in list(SECOND_NO)[:no] if SECOND_BANKS[s] == first_bank]
                if before:
                    pe.wait_ge(rfree, BTILES * (SECOND_NO[before[-1]] + 1))
                if not last_tile:
                    idle(("s", rnd, b), R[:, first_bank, :])
                pe.wait_ge(ws_hi, 2 * r + 2)
                pe.wait_ge(ws_lo, 2 * r + 2)
                h = HIDDEN_NO["h", rnd, b, HK // 2 - 1] + 1
                pe.wait_ge(hid_hi, h)
                pe.wait_ge(hid_lo, h)
                width = WIDTH.get(rnd, DIM)
                src = hid[HID_AT[rnd, b]]
                apart = ("last tile", rnd, b) in ORDER
                for t in range(BTILES):
                    if apart and (t == BTILES - 1) != last_tile:
                        continue
                    at = BANK * first_bank + SLOT * t
                    for k in range(HK):
                        if rnd in WIDTH:
                            both = R_slots[0:TILE, at:at + 2 * width].rearrange("p (u c) -> p u c", u=2)
                            hi, lo = [p[:, k, t * TILE:(t + 1) * TILE] for p in src]
                            mm(both, hi, w_both[r % 2][1][:, k, :, 0:width], start=(k == 0), stop=False)
                            last = mm(R_slots[0:TILE, at:at + width], lo, w_parts[r % 2][1][0][:, k, 0:width],
                                      start=False, stop=(k == HK - 1))
                            continue
                        last = mm_split(R_slots[0:TILE, at:at + width], [p[:, k, t * TILE:(t + 1) * TILE] for p in src],
                                        [p[:, k, 0:width] for p in w_parts[r % 2][1]], k == 0, k == HK - 1)
                    last.then_inc(rfull, 1)

            def gate(b):
                pe.wait_ge(loaded["gw"], 16)
                wait_emptied(pe, ("x", 3, b))
                claim(("gate", b))
                for t in range(BTILES):
                    at = b * BLOCK + t * TILE
                    for k in range(2):
                        last = mm(gbanks(("gate", b), TILE, BTILES * EXPERTS)[:, 0, t * EXPERTS:(t + 1) * EXPERTS],
                                  XT[:, k, at:at + TILE], gw_sb[:, k, :], start=(k == 0), stop=(k == 1))
                last.then_inc(full, 1)

            def transpose_comb():
                pe.wait_ge(comb_ready, 1)
                claim(("ct",))
                g = gbanks(("ct",), EXPERTS, BLOCK)
                for t in range(TILES):
                    at = (t % BTILES) * TILE
                    last = tr(g[:, t // BTILES, at:at + TILE], comb[:, t, :], ident[0:TILE, 0:TILE])
                last.then_inc(full, 1)

            def expert_biases(b):
                if b == 0:
                    pe.wait_ge(loaded["eb2"], 16)
                    wait_emptied(pe, ("ct",))
                claim(("cb", b))
                for t in range(BTILES):
                    at = b * BLOCK + t * TILE
                    last = mm(gslots(("cb", b), TILE, BTILES)[:, t, :], combT[:, at:at + TILE], eb2_sb[:],
                              start=True, stop=True)
                last.then_inc(full, 1)

            def single_scores(b):
                claim(("s2", b))
                wait_emptied(pe, ("k", 2, b))
                wait_emptied(pe, ("q", 2, b))
                g = gbanks(("s2", b), PAIR, BLOCK)
                for t in range(BPAIRS):
                    at = b * BLOCK + t * PAIR
                    for k in range(2):
                        last = mm(g[:, 0, t * PAIR:(t + 1) * PAIR], QT[:, k, at:at + PAIR], KT[:, k, at:at + PAIR],
                                  start=(k == 0), stop=(k == 1))
                last.then_inc(full, 1)

            def single_transpose(b):
                pe.wait_ge(single, 2 * b + 2)
                claim(("t2", b))
                g = gbanks(("t2", b), PAIR, BLOCK)
                for t in range(BPAIRS):
                    last = tr(g[:, 0, t * PAIR:(t + 1) * PAIR], P1[b][:, t, :], ident[0:PAIR, 0:PAIR])
                last.then_inc(full, 1)

            def single_mix(b):
                claim(("z2", b))
                wait_emptied(pe, ("t2", b))
                pe.wait_ge(xp_loaded[b], 16)
                g = gbanks(("z2", b), HALF, BLOCK)
                for t in range(BPAIRS):
                    for k in range(2):
                        last = mm(g[:, k, t * PAIR:(t + 1) * PAIR], XP[:, b * BPAIRS + t, k * HALF:(k + 1) * HALF],
                                  P1T[:, b * BPAIRS + t, :], start=True, stop=True)
                last.then_inc(full, 1)

            pe.wait_ge(warm_set, 1)
            for i in range(WARM):
                mm(R[0:HALF, 2, 0:BLOCK], QT[:, 0, 0:HALF], QT[:, 0, 0:BLOCK], start=True, stop=True)
            for kind, *at in ORDER:
                if kind == "c":
                    patches(*at)
                elif kind == "x":
                    tokens_to_channels(*at)
                elif kind in ("k", "q", "vt"):
                    project(kind, *at)
                elif kind == "v":
                    values_of(*at)
                elif kind == "S":
                    scores(*at)
                elif kind == "T":
                    transpose_probs(*at)
                elif kind == "W":
                    mix(*at)
                elif kind == "O":
                    transpose_out(*at)
                elif kind == "p":
                    project_out(*at)
                elif kind == "h":
                    hidden(*at)
                elif kind == "s":
                    second(*at)
                elif kind == "last tile":
                    second(*at, last_tile=True)
                elif kind == "gate":
                    gate(*at)
                elif kind == "ct":
                    transpose_comb()
                elif kind == "cb":
                    expert_biases(*at)
                elif kind == "s2":
                    single_scores(*at)
                elif kind == "t2":
                    single_transpose(*at)
                elif kind == "z2":
                    single_mix(*at)

        @block.scalar
        def _(act):
            A = nc.scalar.activation
            act_steps = [0]

            def out_of(turn, ins):
                ins.then_inc(emptied[TURN[turn] % 2], 1)

            def channels(k, b):
                turn = ("x", k, b)
                if (k, b) not in SPLIT_X:
                    return
                wait_full(act, turn)
                g = gbanks(turn, HALF, BLOCK)
                whole, upper = XT[:, :, bc(b)], XS[0][:, :, bc(b)]
                if k in GAINS and (k, b) not in BOTH_X:
                    for a in range(2):
                        gain, shift = GAINS[k][b]
                        A(whole[:, a, :], g[:, a, :], ACT.Identity, bias=col(shift, a), scale=col(gain, a)).then_inc(act_step, 1)
                        act_steps[0] += 1
                    act.wait_ge(act_step, act_steps[0])
                    A(upper, whole, ACT.Copy).then_inc(xs_hi, 2)
                    return
                for a in range(2):
                    if (k, b) in BOTH_X:
                        gain, shift = GAINS[k][b]
                        if a == 1:
                            act.wait_ge(xs_sum, 2 * BOTH_X.index((k, b)) + 1)
                        A(upper[:, a, :], g[:, a, :], ACT.Identity, bias=col(shift, a), scale=col(gain, a)).then_inc(xs_hi, 1)
                    else:
                        A(upper[:, a, :], g[:, a, :], ACT.Copy).then_inc(xs_hi, 1)

            def value_channels(a, b):
                turn = ("vt", a, b)
                n = VALUES_NO["v", a, b, 0]
                if n:
                    wait_full(act, list(VALUES_NO)[n - 1])
                wait_full(act, turn)
                for k in range(2):
                    out_of(turn, A(VT3[:, k, :, :].rearrange("p i (r m) -> p i r m", r=GROUP),
                                   gbanks(turn, HALF, BLOCK)[:, k, :].rearrange("p (i m) -> p i m", m=SEQ)
                                   .unsqueeze(2).broadcast_to([HALF, IMAGES // 2, GROUP, SEQ]), ACT.Copy))

            def keys_or_queries(n, a, b):
                turn = (n, a, b)
                wait_full(act, turn)
                g = gbanks(turn, HALF, BLOCK)
                for i in range(2):
                    dst = (KT if n == "k" else QT)[:, i, bc(b)]
                    if a == 3:
                        out_of(turn, A(dst, g[:, i, :], ACT.Copy))
                    else:
                        out_of(turn, A(dst, g[:, i, :], ACT.Identity, bias=col(f"A{a}_b{n}", i)))

            def weights(a, b, t):
                n = pair_no(a, b, t)
                p = P[:, n % 2, :, :].rearrange("p h m -> p (h m)")
                scale = HEAD ** -0.5
                if a == 0:
                    act.wait_ge(scored, n + 1)
                    if n >= 2:
                        act.wait_ge(turned, n - 1)
                    A(p, R[0:ROWS, n % 2, 0:HEADS * SEQ], ACT.Square, bias=1.0, scale=scale).then_inc(shifted, 1)
                else:
                    act.wait_ge(shifted, n + 1)
                    A(p, p, ACT.Exp, scale=scale).then_inc(probs, 1)

            def copy_transposed(a, b, t):
                n = pair_no(a, b, t)
                act.wait_ge(turned, n + 1)
                if n >= 2:
                    act.wait_ge(mixed, n - 1)
                dst, src = PT[:, n % 2, :, :].rearrange("p g r -> p (g r)"), R[0:GK, 2, 0:GROUPS * ROWS]
                (A(dst, src, ACT.Identity, bias=1.0) if a == 0 else A(dst, src, ACT.Copy)).then_inc(pt_ready, 1)

            def values_of(a, b, j):
                turn = ("v", a, b, j)
                wait_full(act, turn)
                src = gslots(turn, GK, 4).rearrange("p i (g c) -> p i g c", g=GROUPS)
                at = b * IMAGES // 2 + 4 * j
                for h in range(GROUP):
                    ch = slice(h * HEAD, (h + 1) * HEAD)
                    out_of(turn, A(V[:, at:at + 4, :, ch], src[:, :, :, ch], ACT.Identity, bias=0.0,
                                   scale=vmask[:, 0, h * HEAD:h * HEAD + 1]))

            def attention_out(a, b):
                turn = ("O", a, b)
                wait_full(act, turn)
                for k in range(2):
                    src = gbanks(turn, HALF, BPAIRS * 2 * SECOND)[:, k, :].rearrange("p (i r) -> p i r", r=SECOND)[:, :, 0:SEQ]
                    dst = OT[:, k, bc(b)].rearrange("p (i m) -> p i m", m=SEQ)
                    out_of(turn, A(dst, src, ACT.Copy) if a == 3 else
                           A(dst, src, ACT.Identity, bias=col(f"A{a}_bv", k)))

            def gelu(rnd, b, i):
                turn = ("h", rnd, b, i)
                n = HIDDEN_NO[turn]
                tmp = hid_tmp[:, n % 2, :].rearrange("p (u t) -> p u t", u=2)
                if n == 0:
                    act.wait_ge(loaded["hcols"], 16)
                if n >= 2:
                    act.wait_ge(hid_lo, n - 1)
                wait_full(act, turn)
                bias = HCOLS.index("F" if rnd in WIDTH else rnd)
                for u in range(2):
                    out_of(turn, A(tmp[:, u, :], gbanks(turn, 128, BLOCK)[:, u, :], ACT.Gelu,
                                   bias=hcols_sb[:, bias, 2 * i + u:2 * i + u + 1]))
                if rnd in WIDTH:
                    return
                wait_emptied(act, turn)
                if i == 0:
                    wait_hid_free(act, rnd, b)
                dst = hid[HID_AT[rnd, b]][0][:, 2 * i:2 * i + 2, :]
                if (rnd, b) in BRANCH:
                    j = BRANCH[rnd, b]
                    A(dst, tmp, ACT.Identity, bias=0.0, scale=gum[:, j:j + 1]).then_inc(hid_hi, 1)
                else:
                    A(dst, tmp, ACT.Copy).then_inc(hid_hi, 1)

            for i in range(2):
                ks = slice(i * PATCH_K // 2, (i + 1) * PATCH_K // 2)
                act.dma_start(conv_sb[:, ks, :], conv_w[:, ks, :]).then_inc(loaded[f"conv_w{i}"], 16)
            act.dma_start(pos_sb, pos).then_inc(loaded["pos"], 16)
            act.dma_start(const_sb[:], const).then_inc(loaded["const"], 16)
            act.dma_start(brows_sb[:], brows.partition_broadcast(128)).then_inc(loaded["brows"], 16)
            act.dma_start(cols_sb[:], cols).then_inc(loaded["cols"], 16)
            act.wait_ge(loaded["conv_w0"], 16)
            act.wait_ge(loaded["conv_w1"], 16)
            A(conv_parts[0], conv_sb, ACT.Copy).then_inc(conv_hi, 1)
            act.wait_ge(loaded[f"x{BTILES}"], 16)
            for t in range(BTILES):
                A(patch_parts[0][:, t, :, :], xp_sb[:, 1, t, :, :], ACT.Copy).then_inc(conv_hi, 1)
            act.wait_ge(loaded["cols"], 16)
            act.wait_ge(loaded["const"], 16)
            A(idle[:], const_sb[:, 0:1], ACT.Exp)
            act.wait_ge(loaded["brows"], 16)
            for kind, *at in SCALAR_ORDER:
                if kind == "x":
                    channels(*at)
                elif kind in ("k", "q"):
                    keys_or_queries(kind, *at)
                elif kind == "vt":
                    value_channels(*at)
                elif kind == "v":
                    values_of(*at)
                elif kind == "E":
                    weights(*at)
                elif kind == "table":
                    A(idle[:], const_sb[:, 0:1], {"exp": ACT.Exp, "gelu": ACT.Gelu}[at[0]])
                elif kind == "T":
                    copy_transposed(*at)
                elif kind == "O":
                    attention_out(*at)
                elif kind == "h":
                    gelu(*at)
                elif kind == "comb":
                    act.wait_ge(logit_diff, 1)
                    A(LE[:], LX[:], ACT.Tanh).then_inc(logit_tanh, 1)
                elif kind == "ct":
                    wait_full(act, ("ct",))
                    out_of(("ct",), A(combT.rearrange("p (b t) -> p b t", b=2), gbanks(("ct",), EXPERTS, BLOCK), ACT.Copy))
                elif kind == "e2":
                    b = at[0]
                    p = P1[b]
                    act.wait_ge(single, 2 * b + 1)
                    A(p, p, ACT.Exp, scale=DIM ** -0.5).then_inc(single_exp, 1)
                elif kind == "t2":
                    turn, b = ("t2", at[0]), at[0]
                    wait_full(act, turn)
                    out_of(turn, A(P1T[:, b * BPAIRS:(b + 1) * BPAIRS, :].rearrange("p t m -> p (t m)"),
                                   gbanks(turn, PAIR, BLOCK)[:, 0, :], ACT.Copy))
                elif kind == "z2":
                    turn = ("z2", at[0])
                    wait_full(act, turn)
                    out_of(turn, A(OT[:, :, bc(at[0])], gbanks(turn, HALF, BLOCK), ACT.Copy))

        @block.vector
        def _(dve):
            v = nc.vector
            steps = [0]

            def link(ins):
                ins.then_inc(dve_step, 1)
                steps[0] += 1
                dve.wait_ge(dve_step, steps[0])

            def out_of(turn, ins):
                ins.then_inc(emptied[TURN[turn] % 2], 1)

            def wait_resid(stage, b):
                dve.wait_ge(resid, RESIDUAL_NO[stage, b] + 1)

            def row_statistics(src, ts):
                for t in ts:
                    v.bn_stats(bst[:, t, :], src[:, t, :]).then_inc(dve_step, 1)
                    steps[0] += 1

            def deviations(norm, ts):
                for t in ts:
                    v.bn_aggr(mv[:, t, :], bst[:, t, :]).then_inc(dve_step, 1)
                    steps[0] += 1
                dve.wait_ge(dve_step, steps[0])
                at = slice(ts[0], ts[-1] + 1)
                var = mv[:, at, 1]
                if NORMS[norm] == 2:
                    link(v.tensor_scalar(shifted_var[:, 1, at], var, 1.0 + EPS, EPS * EPS, ALU.mult, ALU.add))
                v.tensor_scalar(shifted_var[:, 0, at], var, EPS, None, ALU.add).then_inc(stats, 1)

            def statistics(norm, b):
                ts = range(b * BTILES, (b + 1) * BTILES)
                if norm in NORM_OF.values():
                    a = {n: a for a, n in NORM_OF.items()}[norm]
                    wait_emptied(dve, ("p", a, b))
                    row_statistics(Y, ts)
                else:
                    rnd = [r for r, n in NORM_BEHIND.items() if n == norm and r[1] == b][0]
                    dve.wait_ge(rfree, BTILES * (SECOND_NO["s", *rnd] + 1))
                    row_statistics(RB if norm == "b" else Y, ts[2:])
                dve.wait_ge(dve_step, steps[0])
                deviations(norm, ts[2:] if (norm, b) == LAST_NORM else ts)

            def normalise_tiles(dst, src, i, ts):
                for t in ts:
                    v.tensor_scalar(dst[:, t, :], src[:, t, :], mv[:, t, 0:1], rs[:, i, t:t + 1],
                                    ALU.subtract, ALU.mult).then_inc(normed, 1)

            def normalise(norm, b, residual=False):
                src = RB if norm == "b" else Y
                if norm in ("a", "c"):
                    dst, i = (H, 0) if residual else (NRM, 1)
                else:
                    dst, i = (NRM if norm in ("ln2", "n2") else H), 0
                ts = range(b * BTILES, (b + 1) * BTILES)
                if (norm, b) == LAST_NORM:
                    dve.wait_ge(rstd, NORM_NO[norm, b] + 2)
                    ts = ts[2:]
                else:
                    dve.wait_ge(rstd, NORM_NO[norm, b] + 1)
                normalise_tiles(dst, src, i, ts)

            def patch_rows(b):
                if b == 0:
                    dve.wait_ge(loaded["pos"], 16)
                    dve.wait_ge(loaded["brows"], 16)
                    link(v.tensor_tensor(pos_sb, pos_sb, row("conv_b", TILE, TILES), ALU.add))
                wait_full(dve, ("c", b))
                out_of(("c", b), v.tensor_tensor(H[:, bt(b), :], gslots(("c", b), TILE, BTILES), pos_sb[:, bt(b), :], ALU.add))

            def lower_part(k, b):
                i = SPLIT_X.index((k, b))
                turn = ("x", k, b)
                whole, upper, lower = XT[:, :, bc(b)], XS[0][:, :, bc(b)], XS[1][:, :, bc(b)]
                g = gbanks(turn, HALF, BLOCK)
                if k not in GAINS:
                    for a in range(2):
                        dve.wait_ge(xs_hi, 2 * i + a + 1)
                        last = v.tensor_tensor(lower[:, a, :], g[:, a, :], upper[:, a, :].bitcast(F32), ALU.subtract)
                    last.then_inc(xs_lo, 1)
                    return
                if (k, b) in BOTH_X:
                    wait_full(dve, turn)
                    gain, shift = GAINS[k][b]
                    for a in (1, 0):
                        if a == 0:
                            dve.wait_ge(xs_hi, 2 * i + 1)
                        v.tensor_scalar(whole[:, a, :], g[:, a, :], col(gain, a), col(shift, a), ALU.mult,
                                        ALU.add).then_inc(xs_sum, 1)
                    wait_emptied(dve, turn)
                dve.wait_ge(xs_hi, 2 * i + 2)
                v.tensor_tensor(lower, whole, upper.bitcast(F32), ALU.subtract).then_inc(xs_lo, 1)

            def qkv_upper(a):
                dve.wait_ge(loaded[f"qkv{a}"], 16)
                if a == 1:
                    wait_full(dve, ("c", 1))
                elif a == 3:
                    dve.wait_ge(rfull, BTILES * (SECOND_NO["s", "E3", 0] + 1))
                v.tensor_copy(qkv_parts[a][0], qkv_sb[a][:]).then_inc(qs_hi, 1)

            def spread_keys(a, b):
                if a == 0:
                    dve.wait_ge(loaded["const"], 16)
                wait_emptied(dve, ("k", a, b))
                src = KT[:, :, bc(b)].rearrange("p a (i m) -> p a i m", m=SEQ)
                for h in range(POOL_FROM):
                    v.tensor_scalar(KB[:, :, b * IMAGES // 2:(b + 1) * IMAGES // 2, h, :], src,
                                    const_sb[0:HALF, HM_AT + h:HM_AT + h + 1], None, ALU.mult).then_inc(kb_dve, 1)

            def weights(a, b, t):
                n = pair_no(a, b, t)
                dve.wait_ge(scored, n + 1)
                s = R[0:ROWS, n % 2, 0:HEADS * SEQ].rearrange("p (h m) -> p h m", m=SEQ)
                link(v.tensor_reduce(mx[:, n % 2, :], s, AX.X, ALU.max))
                dve.wait_ge(turned, n - 1)
                v.tensor_tensor(P[:, n % 2, :, :], s, mx[:, n % 2, :].unsqueeze(2).broadcast_to([ROWS, HEADS, SEQ]),
                                ALU.subtract).then_inc(shifted, 1)

            def normalise_mixed(a, b, t):
                n = pair_no(a, b, t)
                dve.wait_ge(mixed, n + 1)
                o = R[0:ROWS, 3, 0:GROUPS * GW].rearrange("p (g w) -> p g w", w=GW)
                link(v.reciprocal(rden[:, n % 2, :, :], o[:, :, GV:GW]))
                if t == 0 and n > 0:
                    wait_full(dve, ("O", (0, 1, 3)[(n - 1) // PAIRS], (n - 1) % PAIRS // BPAIRS))
                v.tensor_tensor(O[:, t, :].rearrange("p (g s d) -> p g s d", g=GROUPS, s=GROUP),
                                o[:, :, 0:GV].rearrange("p g (s d) -> p g s d", s=GROUP),
                                rden[:, n % 2, :, :].unsqueeze(3).broadcast_to([ROWS, GROUPS, GROUP, HEAD]),
                                ALU.mult).then_inc(o_ready, 1)

            def add_projection(a, b):
                turn = ("p", a, b)
                wait_full(dve, turn)
                wait_resid(f"A{a}", b)
                out_of(turn, v.tensor_tensor(Y[:, bt(b), :], gslots(turn, TILE, BTILES), RB[:, bt(b), :], ALU.add))

            def hidden_lower(rnd, b, i):
                n = HIDDEN_NO["h", rnd, b, i]
                tmp = hid_tmp[:, n % 2, :]
                if rnd in WIDTH:
                    wait_emptied(dve, ("h", rnd, b, i))
                    j = BRANCH[rnd, b]
                    v.tensor_scalar(hid[HID_AT[rnd, b]][0][:, 2 * i:2 * i + 2, :].rearrange("p u t -> p (u t)"), tmp,
                                    gum[:, j:j + 1], None, ALU.mult).then_inc(hid_hi, 1)
                dve.wait_ge(hid_hi, n + 1)
                hi, lo = [p[:, 2 * i:2 * i + 2, :].rearrange("p u t -> p (u t)") for p in hid[HID_AT[rnd, b]]]
                if (rnd, b) in BRANCH:
                    j = BRANCH[rnd, b]
                    v.scalar_tensor_tensor(out=lo, in0=tmp, scalar=gum[:, j:j + 1], in1=hi.bitcast(F32), op0=ALU.mult,
                                           op1=ALU.subtract).then_inc(hid_lo, 1)
                else:
                    v.tensor_tensor(lo, tmp, hi.bitcast(F32), ALU.subtract).then_inc(hid_lo, 1)

            def weight_upper(r, i):
                dve.wait_ge(raw_loaded[i], 16 * (r + 1))
                wait_slot_free(dve, r, i)
                v.tensor_copy(w_parts[r % 2][i][0], raw[i][:]).then_inc(ws_hi, 1)

            def second_sum(rnd, b):
                no = SECOND_NO["s", rnd, b]
                width = WIDTH.get(rnd, DIM)
                norm = NORM_BEHIND.get((rnd, b))
                for i in range(BTILES):
                    t = b * BTILES + i
                    if i == 2 and norm:
                        dve.wait_ge(rfree, BTILES * no + 2)
                        row_statistics(RB if norm == "b" else Y, range(t - 2, t))
                        if (norm, b) == LAST_NORM:
                            dve.wait_ge(dve_step, steps[0])
                            deviations(norm, range(t - 2, t))
                            dve.wait_ge(rstd, NORM_NO[norm, b] + 1)
                            normalise_tiles(H, Y, 0, range(t - 2, t))
                    at = BANK * SECOND_BANKS["s", rnd, b] + SLOT * i
                    ps = R_slots[0:TILE, at:at + width]
                    if i % 2 == 0:
                        dve.wait_ge(rfull, BTILES * no + min(i + 2, BTILES))
                    if rnd in ("M", "F"):
                        if i == 0:
                            wait_resid(rnd, b)
                        ins = v.tensor_tensor(Y[:, t, :], ps, RB[:, t, :], ALU.add)
                    elif rnd in WIDTH:
                        if i == 0:
                            dve.wait_ge(rfree, BTILES * no)
                        link(v.tensor_tensor(Y[:, t, 0:width], ps, Y[:, t, 0:width], ALU.add))
                        second_half = R_slots[0:TILE, at + width:at + 2 * width]
                        ins = v.tensor_tensor(Y[:, t, 0:width], second_half, Y[:, t, 0:width], ALU.add)
                    else:
                        e = int(rnd[1])
                        if i == 0:
                            if e == 0:
                                wait_resid("E", b)
                            else:
                                dve.wait_ge(rfree, BTILES * (SECOND_NO["s", f"E{e - 1}", b] + 1))
                            if e == 1:
                                wait_emptied(dve, ("cb", b))
                        ins = v.scalar_tensor_tensor(out=RB[:, t, :], in0=ps, scalar=comb[:, t, e:e + 1],
                                                     in1=RB[:, t, :], op0=ALU.mult, op1=ALU.add)
                    ins.then_inc(rfree, 1)

            EE = EXPERTS * EXPERTS

            def logits(b):
                turn = ("gate", b)
                wait_full(dve, turn)
                out_of(turn, v.tensor_tensor(
                    L[:, bt(b), :], gbanks(turn, TILE, BTILES * EXPERTS)[:, 0, :].rearrange("p (t e) -> p t e", e=EXPERTS),
                    brows_sb[0:TILE, GATE_AT:GATE_AT + EXPERTS].unsqueeze(1).broadcast_to([TILE, BTILES, EXPERTS]), ALU.add))

            def rank():
                wait_emptied(dve, ("gate", 0))
                wait_emptied(dve, ("gate", 1))
                link(v.tensor_reduce(lm[:, 0, :], L[:], AX.X, ALU.max))
                link(v.tensor_tensor(LX[:], L[:], lm[:, 0, :].unsqueeze(2).broadcast_to([TILE, TILES, EXPERTS]),
                                     ALU.subtract))
                mine = L[:].unsqueeze(3).broadcast_to([TILE, TILES, EXPERTS, EXPERTS])
                other = L[:].unsqueeze(2).broadcast_to([TILE, TILES, EXPERTS, EXPERTS])
                for m, op, at in ((gtm, ALU.is_gt, GT_AT), (gem, ALU.is_ge, GE_AT)):
                    link(v.tensor_tensor(m[:].rearrange("p t (e f) -> p t e f", e=EXPERTS), other, mine, op))
                    link(v.tensor_tensor(m[:], m[:], const_sb[0:TILE, at:at + EE].unsqueeze(1)
                                         .broadcast_to([TILE, TILES, EE]), ALU.mult))
                link(v.tensor_tensor(gtm[:], gtm[:], gem[:], ALU.add))
                link(v.tensor_reduce(L[:], gtm[:].rearrange("p t (e f) -> p t e f", e=EXPERTS), AX.X, ALU.add))
                link(v.tensor_scalar(L[:], L[:], 1.5, 0.5, ALU.is_lt, ALU.mult))
                link(v.tensor_tensor(LE[:], LX[:], L[:], ALU.mult))
                link(v.tensor_reduce(lm[:, 1, :], LE[:], AX.X, ALU.add))
                v.tensor_tensor(LX[:], LX[:], lm[:, 1, :].unsqueeze(2).broadcast_to([TILE, TILES, EXPERTS]),
                                ALU.subtract).then_inc(logit_diff, 1)

            def combine_weights():
                dve.wait_ge(logit_tanh, 1)
                v.scalar_tensor_tensor(out=comb[:], in0=LE[:], scalar=1.0, in1=L[:], op0=ALU.add,
                                       op1=ALU.mult).then_inc(comb_ready, 1)
                dve.wait_ge(comb_ready, 1)

            def single_softmax(b):
                wait_full(dve, ("s2", b))
                pairs = slice(b * BPAIRS, (b + 1) * BPAIRS)
                p = P1[b]
                out_of(("s2", b), v.tensor_tensor(
                    p, gbanks(("s2", b), PAIR, BLOCK)[:, 0, :].rearrange("p (t m) -> p t m", m=PAIR),
                    amask.unsqueeze(1).broadcast_to([PAIR, BPAIRS, PAIR]), ALU.add))
                wait_emptied(dve, ("s2", b))
                link(v.tensor_reduce(st1[:, 0, pairs], p, AX.X, ALU.max))
                v.tensor_tensor(p, p, st1[:, 0, pairs].unsqueeze(2).broadcast_to([PAIR, BPAIRS, PAIR]),
                                ALU.subtract).then_inc(single, 1)
                dve.wait_ge(single_exp, b + 1)
                link(v.tensor_reduce(st1[:, 1, pairs], p, AX.X, ALU.add))
                link(v.reciprocal(st1[:, 2, pairs], st1[:, 1, pairs]))
                v.tensor_tensor(p, p, st1[:, 2, pairs].unsqueeze(2).broadcast_to([PAIR, BPAIRS, PAIR]),
                                ALU.mult).then_inc(single, 1)

            v.memset(QT[:, 0, :], 0.0).then_inc(warm_set, 1)
            v.memset(R[32:64, 0:2, :], 1.0).then_inc(pad_set, 1)
            v.memset(R[32:64, 3, :], 1.0).then_inc(pad_set, 1)
            dve.wait_ge(conv_hi, 1)
            v.tensor_tensor(conv_parts[1], conv_sb, conv_parts[0].bitcast(F32), ALU.subtract).then_inc(conv_lo, 1)
            for t in range(BTILES):
                dve.wait_ge(conv_hi, t + 2)
                v.tensor_tensor(patch_parts[1][:, t, :, :], xp_sb[:, 1, t, :, :], patch_parts[0][:, t, :, :].bitcast(F32),
                                ALU.subtract).then_inc(conv_lo, 1)
            for kind, *at in VECTOR_ORDER:
                if kind == "c":
                    patch_rows(*at)
                elif kind == "x":
                    if tuple(at) in SPLIT_X:
                        lower_part(*at)
                    if at[0] == 4:
                        turn = ("x", *at)
                        wait_full(dve, turn)
                        out_of(turn, v.tensor_copy(XT[:, :, bc(at[1])], gbanks(turn, HALF, BLOCK)))
                    if tuple(at) == (5, 0):
                        v.memset(R[32:64, 3, :], 1.0).then_inc(pad_set, 1)
                elif kind == "k" and at[0] != 2:
                    spread_keys(*at)
                elif kind == "S" and at[0] > 0:
                    weights(*at)
                elif kind == "W":
                    normalise_mixed(*at)
                elif kind == "p":
                    add_projection(*at)
                elif kind == "st":
                    statistics(*at)
                elif kind == "n":
                    normalise(*at)
                elif kind == "nh":
                    normalise(*at, residual=True)
                elif kind == "h":
                    hidden_lower(*at)
                elif kind == "ws":
                    weight_upper(*at)
                elif kind == "qs":
                    qkv_upper(*at)
                elif kind == "s":
                    second_sum(*at)
                elif kind == "gate":
                    logits(*at)
                    if at[0] == 1:
                        rank()
                elif kind == "comb":
                    combine_weights()
                elif kind == "cb":
                    b = at[0]
                    dve.wait_ge(rfree, BTILES * (SECOND_NO["s", "E0", b] + 1))
                    wait_full(dve, ("cb", b))
                    out_of(("cb", b), v.tensor_tensor(RB[:, bt(b), :], gslots(("cb", b), TILE, BTILES), RB[:, bt(b), :], ALU.add))
                elif kind == "s2":
                    single_softmax(*at)

        @block.gpsimd
        def _(pool):
            g = nc.gpsimd
            steps = [0]

            def link(ins):
                ins.then_inc(pool_step, 1)
                steps[0] += 1
                pool.wait_ge(pool_step, steps[0])

            def residual(stage, b):
                def add(first, second):
                    return g.tensor_tensor(RB[:, bt(b), :], first[:, bt(b), :], second, ALU.add)

                def small(i):
                    return browss[0:TILE, i, :].unsqueeze(1).broadcast_to([TILE, BTILES, DIM])

                if stage == "A0":
                    wait_emptied(pool, ("c", b))
                    ins = add(H, row("A0_bp", TILE, BTILES))
                elif stage == "A1":
                    pool.wait_ge(normed, NORMED["a", b])
                    ins = add(H, row("A1_bp", TILE, BTILES))
                elif stage == "M":
                    wait_emptied(pool, ("p", 1, b))
                    ins = add(Y, row("mlp_b2", TILE, BTILES))
                elif stage == "E":
                    pool.wait_ge(rfree, BTILES * (SECOND_NO["s", "M", b] + 1))
                    ins = add(Y, H[:, bt(b), :])
                elif stage == "A2":
                    pool.wait_ge(normed, NORMED["b", b])
                    ins = add(H, row("A2_bv", TILE, BTILES))
                elif stage == "A3":
                    pool.wait_ge(normed, NORMED["c", b])
                    ins = add(H, row("A3_bp", TILE, BTILES) if b == 0 else small(0))
                else:
                    wait_emptied(pool, ("p", 3, b))
                    link(add(Y, H[:, bt(b), :]))
                    ins = add(RB, row("fc2_b", TILE, BTILES) if b == 0 else small(1))
                ins.then_inc(resid, 1)

            def spread_keys(a, b):
                wait_emptied(pool, ("k", a, b))
                src = KT[:, :, bc(b)].rearrange("p a (i m) -> p a i m", m=SEQ)
                for h in range(POOL_FROM, HHEADS):
                    g.tensor_scalar(KB[:, :, b * IMAGES // 2:(b + 1) * IMAGES // 2, h, :], src,
                                    const_sb[0:HALF, HM_AT + h:HM_AT + h + 1], None, ALU.mult).then_inc(kb_pool, 1)

            def inverse_deviation(norm, b):
                n = NORMS[norm]
                parts = [(0, BTILES)] if (norm, b) != LAST_NORM else [(0, 2), (2, BTILES)]
                for i, (lo, hi) in enumerate(parts):
                    at = slice(b * BTILES + lo, b * BTILES + hi)
                    pool.wait_ge(stats, NORM_NO[norm, b] + 1 + i)
                    g.tensor_tensor(rs[:, 0:n, at], shifted_var[:, 0:n, at], mhalf[:, 0:n, lo:hi], ALU.pow).then_inc(rstd, 1)

            def weight_lower(r, i):
                pool.wait_ge(ws_hi, SPLIT_NO["ws", r, i] + 1)
                hi, lo = w_parts[r % 2][i]
                g.tensor_tensor(lo, raw[i][:], hi.bitcast(F32), ALU.subtract).then_inc(ws_lo, 1)

            def set_ones():
                ones = vmask[:, :, GV:GW].unsqueeze(1).broadcast_to([GK, IMAGES, GROUPS, GROUP])
                g.tensor_copy(V[:, :, :, GV:GW], ones).then_inc(ones_set, 1)

            def branch_sums():
                link(g.tensor_copy(gsum[:, 0:1], gum[:, 0:1]))
                link(g.tensor_tensor(gsum[:, 1:2], gsum[:, 0:1], gum[:, 1:2], ALU.add))
                link(g.tensor_tensor(gsum[:, 2:3], gsum[:, 1:2], gum[:, 2:3], ALU.add))
                c1, c2 = KEEP[2], KEEP[1]
                link(g.tensor_copy(gcol[0:c1, :], gsum[0:c1, 2:3]))
                link(g.tensor_copy(gcol[c1:HALF, :], gsum[c1:HALF, 1:2]))
                pool.wait_ge(loaded["proj3"], 16)
                w = proj_sb[3]
                for a, lo, hi, s in ((0, 0, c1, gcol[:, 0:1]), (0, c1, c2, gsum[0:HALF, 1:2]),
                                     (0, c2, DIM, gsum[0:HALF, 0:1]), (1, 0, DIM, gsum[0:HALF, 0:1])):
                    g.tensor_scalar(proj3s_sb[:, a, lo:hi], w[:, a, lo:hi], s, None, ALU.mult).then_inc(eff, 1)
                for i, name in enumerate(("A3_bp", "fc2_b")):
                    r = BROWS.index(name) * DIM
                    for lo, hi, k in ((0, c1, 2), (c1, c2, 1), (c2, DIM, 0)):
                        link(g.tensor_scalar(browss[:, i, lo:hi], brows_sb[:, r + lo:r + hi], gsum[:, k:k + 1], None,
                                             ALU.mult))

            link(g.memset(mhalf[:], -0.5))
            pool.wait_ge(loaded["const"], 16)
            pool.wait_ge(loaded["brows"], 16)
            for piece in ORDER:
                kind, *at = piece
                if kind == "p" and at[0] in NORM_OF:
                    inverse_deviation(NORM_OF[at[0]], at[1])
                elif kind == "s" and tuple(at) in NORM_BEHIND:
                    inverse_deviation(NORM_BEHIND[tuple(at)], at[1])
                elif kind == "k" and at[0] != 2:
                    spread_keys(*at)
                elif kind == "ws":
                    weight_lower(*at)
                elif kind == "qs":
                    i = SPLIT_A.index(at[0])
                    pool.wait_ge(qs_hi, i + 1)
                    hi, lo = qkv_parts[at[0]]
                    g.tensor_tensor(lo, qkv_sb[at[0]][:], hi.bitcast(F32), ALU.subtract).then_inc(qs_lo, 1)
                elif piece == ("z2", 1):
                    wait_full(pool, piece)
                    set_ones()
                if piece in RESIDUAL_AT:
                    residual(*RESIDUAL_AT[piece])
                if piece == ("c", 1):
                    wait_emptied(pool, ("c", 1))
                    set_ones()
                if kind == "branches":
                    branch_sums()


HID_AT = {(r, b): b for r in ROUNDS for b in range(2)}
HID_AT["V1", 1], HID_AT["V2", 1] = 0, 1
BRANCH = {("F", 1): 0, ("V1", 1): 1, ("V2", 1): 2}


def _constants():
    c = np.zeros((128, NCONST), np.float32)
    c[:, ID_AT:ID_AT + 128] = np.eye(128)
    for p in range(HALF):
        c[p, HM_AT + p // HEAD] = 1
    for p in range(GK):
        for g in range(GROUPS):
            at = VM_AT + g * GW
            s = p // SEQ
            c[p, at + s * HEAD:at + (s + 1) * HEAD] = 1
            c[p, at + GV + s] = 1
    for p in range(PAIR):
        for m in range(PAIR):
            c[p, AM_AT + m] = 0 if p // SEQ == m // SEQ else -1e30
    for e in range(EXPERTS):
        for f in range(EXPERTS):
            c[:, GT_AT + e * EXPERTS + f] = f > e
            c[:, GE_AT + e * EXPERTS + f] = f < e
    return c


def _position_ids(n, side=32):
    boundaries = np.arange(1.0 / side, 1.0, 1.0 / side, dtype=np.float32)
    frac = np.arange(0.0, 1.0 - 1e-06, 1.0 / n, dtype=np.float32)
    at = np.searchsorted(boundaries, frac, side="right")
    return (at[:, None] * side + at).reshape(-1)


def kernel(**inputs):
    import concourse.bacc as _bacc
    from concourse.bass_utils import run_bass_kernel_spmd as _run

    a = {k: np.asarray(v) for k, v in inputs.items()}

    def channels(w):
        return w.reshape(2, HALF, -1).transpose(1, 0, 2)

    def hidden(w):
        return w.reshape(HK, 128, -1).transpose(1, 0, 2)

    x = a["x"].reshape(IMAGES, IN_CH, GRID, PATCH, GRID, PATCH).transpose(1, 3, 5, 0, 2, 4)
    x = x.reshape(PATCH_K, 128, 2, BTILES, TILE).transpose(1, 2, 3, 0, 4)
    conv = a["L0_tok_conv_w"].reshape(DIM, PATCH_K, 128).transpose(2, 1, 0)
    pos = a["L0_tok_pos_table"][_position_ids(GRID)]
    pos = np.concatenate([pos] * IMAGES).reshape(TILES, TILE, DIM).transpose(1, 0, 2)
    qb, ib = a["L0_attn_b_qkv"], a["L0_ffn_in_b"]
    cols = [qb[0:DIM], qb[DIM:2 * DIM], qb[2 * DIM:], a["L0_ffn_ln1_g"], a["L0_ffn_ln1_b"], ib[0:DIM], ib[DIM:2 * DIM],
            ib[2 * DIM:], a["L0_ffn_ln2_g"], a["L0_ffn_ln2_b"], a["L1_attn_bq"], a["L1_attn_bk"]]
    cols += [a["L1_ffn_" + n] for n in ("n1l_g", "n1l_b", "n1s_g", "n1s_b", "n2l_g", "n2l_b", "n2s_g", "n2s_b")]
    cols = np.stack(cols).reshape(len(COLS), 2, HALF).transpose(2, 0, 1)
    hcols = np.concatenate([a["L0_ffn_mlp_b1"][None], a["L0_ffn_exp_b1"], a["L1_ffn_b_fc1"][None]])
    hcols = hcols.reshape(len(HCOLS), HK, 128).transpose(2, 0, 1)
    brows = np.concatenate([a["L0_tok_conv_b"], a["L0_attn_b_proj"], a["L0_ffn_out_b"], a["L0_ffn_mlp_b2"],
                            a["L1_attn_bv"], a["L1_ffn_b_proj"], a["L1_ffn_b_fc2"], a["L0_ffn_gate_b"],
                            a["L1_ffn_gumbel_weights"]])
    ins = {
        "x": x, "conv_w": conv, "pos": pos, "qkv0": channels(a["L0_attn_w_qkv"]), "proj0": channels(a["L0_attn_w_proj"]),
        "inw": channels(a["L0_ffn_in_w"].T), "outw": channels(a["L0_ffn_out_w"].T),
        "mw1": channels(a["L0_ffn_mlp_w1"]), "mw2": hidden(a["L0_ffn_mlp_w2"]),
        "ew1": a["L0_ffn_exp_w1"].reshape(EXPERTS, 2, HALF, HIDDEN).transpose(2, 0, 1, 3),
        "ew2": a["L0_ffn_exp_w2"].reshape(EXPERTS, HK, 128, DIM).transpose(2, 0, 1, 3), "eb2": a["L0_ffn_exp_b2"],
        "gw": channels(a["L0_ffn_gate_w"].T),
        "qkv2": channels(np.concatenate([a["L1_attn_Wq"].T, a["L1_attn_Wk"].T, a["L1_attn_Wv"].T], axis=1)),
        "qkv3": channels(a["L1_ffn_w_qkv"]), "proj3": channels(a["L1_ffn_w_proj"]),
        "fw1": channels(a["L1_ffn_w_fc1"]), "fw2": hidden(a["L1_ffn_w_fc2"]),
        "cols": cols, "hcols": hcols, "brows": brows, "const": _constants(),
    }
    nc = _bacc.Bacc("TRN2", target_bir_lowering=False, num_devices=1)
    arrays, args = {}, []
    for name, v in ins.items():
        v = np.ascontiguousarray(v)
        arrays["in_" + name] = v
        args.append(nc.dram_tensor("in_" + name, v.shape, mybir.dt.from_np(v.dtype), kind="ExternalInput").ap())
    res = nc.dram_tensor("out_dram", (TOKENS, DIM), F32, kind="ExternalOutput").ap()
    tower(nc, out=res, **dict(zip(ins, args)))
    r = _run(nc, [arrays], core_ids=[0])
    return r.results[0]["out_dram"].reshape(IMAGES, SEQ, DIM)
```
